# Optimizing a Trainium2 kernel written in Bass

```python
import numpy as np
import jax
import jax.numpy as jnp

def _softmax(x, axis=-1):
    return jax.nn.softmax(x, axis=axis)
def _gelu(x):
    return jax.nn.gelu(x, approximate=True)
def _silu(x):
    return jax.nn.silu(x)
def _sigmoid(x):
    return jax.nn.sigmoid(x)
def _layernorm(x, axis=-1, eps=1e-5):
    m = jnp.mean(x, axis=axis, keepdims=True)
    v = jnp.var(x, axis=axis, keepdims=True)
    return (x - m) / jnp.sqrt(v + eps)
def _scatter_add(tgt, idx, src, axis=0):
    return tgt.at[idx].add(src)
def _segment_sum(src, seg, n):
    return jax.ops.segment_sum(src, seg, n)

kernel_name = 'mk_conv_preact_d4_conv_nchw512_e47ea6'

def setup_inputs(seed: int = 0):
    np.random.seed(seed)
    _w = jnp.asarray
    def _rec_inputs():
        import jax
        import jax.numpy as jnp
        _gk = jax.random.key(seed)
        x = 7.22e-05 + 1 * jax.random.normal(jax.random.fold_in(_gk, 1), (4, 512, 64, 64), jnp.float32)
        return x
    x = _rec_inputs()
    def _L0_conv_setup():
        import jax, jax.numpy as jnp
        import numpy as np
        B, DIM, H, W = (4, 512, 64, 64)
        NH = 8
        HD = DIM // NH
        CS = 16
        BASE_LR = 1.0
        EPS_IN = 1e-06
        EPS_OUT = 1e-05

        def _ln(x, g, b, eps):
            mu = x.mean(-1, keepdims=True)
            var = ((x - mu) ** 2).mean(-1, keepdims=True)
            return (x - mu) / jnp.sqrt(var + eps) * g + b

        def _ln_l2_bwd(Z, tgt, g, b):
            D = Z.shape[-1]
            mu = Z.mean(-1, keepdims=True)
            var = ((Z - mu) ** 2).mean(-1, keepdims=True)
            std = jnp.sqrt(var + EPS_IN)
            xh = (Z - mu) / std
            gxh = (g * xh + b - tgt) * g
            return (D * gxh - gxh.sum(-1, keepdims=True) - xh * (gxh * xh).sum(-1, keepdims=True)) / (D * std)

        def _rope(x, L):
            inv = 1.0 / 10000.0 ** (jnp.arange(0, HD, 2, dtype=jnp.float32) / HD)
            fr = jnp.arange(L, dtype=jnp.float32)[:, None] * inv[None, :]
            emb = jnp.concatenate([fr, fr], axis=-1)
            cos, sin = (jnp.cos(emb), jnp.sin(emb))
            x1, x2 = jnp.split(x, 2, axis=-1)
            return x * cos + jnp.concatenate([-x2, x1], axis=-1) * sin

        def _ttt_linear(xn, q_w, k_w, v_w, o_w, W1, b1, ttt_ln_w, ttt_ln_b, lr_w, lr_b, tok_idx_delta, post_w, post_b):
            Bsz, L, _ = xn.shape
            NC = L // CS
            heads = lambda t: t.reshape(Bsz, L, NH, HD).transpose(0, 2, 1, 3)
            XQ = _rope(heads(xn @ q_w.T), L)
            XK = _rope(heads(xn @ k_w.T), L)
            XV = heads(xn @ v_w.T)
            Xc = xn.reshape(Bsz, NC, CS, DIM)
            ttt_lr = jax.nn.sigmoid(jnp.einsum('bnkc,hdc->bhnkd', Xc, lr_w) + lr_b.reshape(1, NH, 1, 1, 1))
            ttt_lr_eta = BASE_LR / HD * ttt_lr.transpose(0, 1, 2, 4, 3)
            token_idx = jnp.maximum(1.0 / jnp.arange(1, CS + 1, dtype=jnp.float32) + tok_idx_delta, 0.0)
            eta = token_idx.reshape(1, 1, 1, CS, 1) * ttt_lr_eta
            g = ttt_ln_w[None, :, None, :]
            bb = ttt_ln_b[None, :, None, :]

            def step(carry, inp):
                W1c, b1c = carry
                xq, xk, xv, et = inp
                Z1 = xk @ W1c + b1c
                grad = _ln_l2_bwd(Z1, xv - xk, g, bb)
                Attn1 = jnp.tril(xq @ xk.swapaxes(-1, -2))
                b1_bar = b1c - jnp.tril(et) @ grad
                Z1_bar = xq @ W1c - et * Attn1 @ grad + b1_bar
                last_eta = et[..., -1, :, None]
                W1n = W1c - (last_eta * xk).swapaxes(-1, -2) @ grad
                b1n = b1c - (last_eta * grad).sum(-2, keepdims=True)
                return ((W1n, b1n), xq + _ln(Z1_bar, g, bb, EPS_IN))
            W1_0 = jnp.broadcast_to(W1[None], (Bsz, NH, HD, HD)) + 0.0
            b1_0 = jnp.broadcast_to(b1[None], (Bsz, NH, 1, HD)) + 0.0
            chunk = lambda t: t.reshape(Bsz, NH, NC, CS, HD).transpose(2, 0, 1, 3, 4)
            _, out = jax.lax.scan(step, (W1_0, b1_0), (chunk(XQ), chunk(XK), chunk(XV), eta.transpose(2, 0, 1, 3, 4)))
            out = out.transpose(1, 2, 0, 3, 4).reshape(Bsz, NH, L, HD).transpose(0, 2, 1, 3).reshape(Bsz, L, DIM)
            return _ln(out, post_w, post_b, EPS_IN) @ o_w.T
        key = jax.random.key(seed)
        ks = jax.random.split(key, 8)
        r = lambda k, s: 0.02 * jax.random.normal(k, s, dtype=jnp.float32)
        return {'x': jax.random.normal(ks[0], (B, DIM, H, W), dtype=jnp.float32), 'ln_w': jnp.ones((DIM,), jnp.float32), 'ln_b': jnp.zeros((DIM,), jnp.float32), 'q_w': r(ks[1], (DIM, DIM)), 'k_w': r(ks[2], (DIM, DIM)), 'v_w': r(ks[3], (DIM, DIM)), 'o_w': r(ks[4], (DIM, DIM)), 'W1': r(ks[5], (NH, HD, HD)), 'b1': jnp.zeros((NH, 1, HD), jnp.float32), 'ttt_ln_w': jnp.ones((NH, HD), jnp.float32), 'ttt_ln_b': jnp.zeros((NH, HD), jnp.float32), 'lr_w': r(ks[6], (NH, 1, DIM)), 'lr_b': jnp.zeros((NH, 1, 1), jnp.float32), 'tok_idx_delta': jnp.zeros((CS,), jnp.float32), 'post_w': jnp.ones((DIM,), jnp.float32), 'post_b': jnp.zeros((DIM,), jnp.float32)}
    _L0_conv_all = _L0_conv_setup()
    _L0_conv_in = {k: v for k, v in _L0_conv_all.items() if k in ('ln_w', 'ln_b', 'q_w', 'k_w', 'v_w', 'o_w', 'W1', 'b1', 'ttt_ln_w', 'ttt_ln_b', 'lr_w', 'lr_b', 'tok_idx_delta', 'post_w', 'post_b', )}
    del _L0_conv_all

    def _L1_conv_setup():
        import jax, jax.numpy as jnp
        import numpy as np
        GROUPS = 4
        CHANNELS = 512
        SCALE = 0.02
        key = jax.random.key(seed)
        k_x, k_w1, k_w2, k_b1, k_b2 = jax.random.split(key, 5)
        d = CHANNELS // GROUPS
        x = jax.random.normal(k_x, (8, CHANNELS, 128, 128), dtype=jnp.float32)
        w1 = SCALE * jax.random.normal(k_w1, (2, GROUPS, d, d), dtype=jnp.float32)
        w2 = SCALE * jax.random.normal(k_w2, (2, GROUPS, d, d), dtype=jnp.float32)
        b1 = SCALE * jax.random.normal(k_b1, (2, GROUPS, d), dtype=jnp.float32)
        b2 = SCALE * jax.random.normal(k_b2, (2, GROUPS, d), dtype=jnp.float32)
        return {'x': x, 'w1': w1, 'w2': w2, 'b1': b1, 'b2': b2}
    _L1_conv_all = _L1_conv_setup()
    _L1_conv_in = {k: v for k, v in _L1_conv_all.items() if k in ('w1', 'w2', 'b1', 'b2', )}
    del _L1_conv_all

    def _L2_conv_setup():
        import jax, jax.numpy as jnp
        import numpy as np
        from jax import lax
        DN = ('NCHW', 'OIHW', 'NCHW')
        key = jax.random.key(seed)
        ks = jax.random.split(key, 5)
        B, C, H, W = (32, 512, 56, 56)
        R = 16
        return {'x': jax.random.normal(ks[0], (B, C, H, W), jnp.float32), 'w1': jax.random.normal(ks[1], (1, 3, 3, 3), jnp.float32) * 0.2, 'w2': jax.random.normal(ks[2], (1, 1, 3, 3), jnp.float32) * 0.2, 'fc1_w': jax.random.normal(ks[3], (C // R, C), jnp.float32) * 0.05, 'fc2_w': jax.random.normal(ks[4], (C, C // R), jnp.float32) * 0.05}
    _L2_conv_all = _L2_conv_setup()
    _L2_conv_in = {k: v for k, v in _L2_conv_all.items() if k in ('w1', 'w2', 'fc1_w', 'fc2_w', )}
    del _L2_conv_all

    def _L3_conv_setup():
        import jax, jax.numpy as jnp
        import numpy as np
        GROUPS = 4
        CHANNELS = 512
        SCALE = 0.02
        key = jax.random.key(seed)
        k_x, k_w1, k_w2, k_b1, k_b2 = jax.random.split(key, 5)
        d = CHANNELS // GROUPS
        x = jax.random.normal(k_x, (8, CHANNELS, 128, 128), dtype=jnp.float32)
        w1 = SCALE * jax.random.normal(k_w1, (2, GROUPS, d, d), dtype=jnp.float32)
        w2 = SCALE * jax.random.normal(k_w2, (2, GROUPS, d, d), dtype=jnp.float32)
        b1 = SCALE * jax.random.normal(k_b1, (2, GROUPS, d), dtype=jnp.float32)
        b2 = SCALE * jax.random.normal(k_b2, (2, GROUPS, d), dtype=jnp.float32)
        return {'x': x, 'w1': w1, 'w2': w2, 'b1': b1, 'b2': b2}
    _L3_conv_all = _L3_conv_setup()
    _L3_conv_in = {k: v for k, v in _L3_conv_all.items() if k in ('w1', 'w2', 'b1', 'b2', )}
    del _L3_conv_all

    return {
        "x": x,
        "L0_conv_ln_w": _L0_conv_in["ln_w"],
        "L0_conv_ln_b": _L0_conv_in["ln_b"],
        "L0_conv_q_w": _L0_conv_in["q_w"],
        "L0_conv_k_w": _L0_conv_in["k_w"],
        "L0_conv_v_w": _L0_conv_in["v_w"],
        "L0_conv_o_w": _L0_conv_in["o_w"],
        "L0_conv_W1": _L0_conv_in["W1"],
        "L0_conv_b1": _L0_conv_in["b1"],
        "L0_conv_ttt_ln_w": _L0_conv_in["ttt_ln_w"],
        "L0_conv_ttt_ln_b": _L0_conv_in["ttt_ln_b"],
        "L0_conv_lr_w": _L0_conv_in["lr_w"],
        "L0_conv_lr_b": _L0_conv_in["lr_b"],
        "L0_conv_tok_idx_delta": _L0_conv_in["tok_idx_delta"],
        "L0_conv_post_w": _L0_conv_in["post_w"],
        "L0_conv_post_b": _L0_conv_in["post_b"],
        "L1_conv_w1": _L1_conv_in["w1"],
        "L1_conv_w2": _L1_conv_in["w2"],
        "L1_conv_b1": _L1_conv_in["b1"],
        "L1_conv_b2": _L1_conv_in["b2"],
        "L2_conv_w1": _L2_conv_in["w1"],
        "L2_conv_w2": _L2_conv_in["w2"],
        "L2_conv_fc1_w": _L2_conv_in["fc1_w"],
        "L2_conv_fc2_w": _L2_conv_in["fc2_w"],
        "L3_conv_w1": _L3_conv_in["w1"],
        "L3_conv_w2": _L3_conv_in["w2"],
        "L3_conv_b1": _L3_conv_in["b1"],
        "L3_conv_b2": _L3_conv_in["b2"],
    }

def reference(x, L0_conv_ln_w, L0_conv_ln_b, L0_conv_q_w, L0_conv_k_w, L0_conv_v_w, L0_conv_o_w, L0_conv_W1, L0_conv_b1, L0_conv_ttt_ln_w, L0_conv_ttt_ln_b, L0_conv_lr_w, L0_conv_lr_b, L0_conv_tok_idx_delta, L0_conv_post_w, L0_conv_post_b, L1_conv_w1, L1_conv_w2, L1_conv_b1, L1_conv_b2, L2_conv_w1, L2_conv_w2, L2_conv_fc1_w, L2_conv_fc2_w, L3_conv_w1, L3_conv_w2, L3_conv_b1, L3_conv_b2):
    import jax
    import jax.numpy as jnp
    def _L0_conv_ref(x, ln_w, ln_b, q_w, k_w, v_w, o_w, W1, b1, ttt_ln_w, ttt_ln_b, lr_w, lr_b, tok_idx_delta, post_w, post_b):
        import jax, jax.numpy as jnp
        import numpy as np
        B, DIM, H, W = (4, 512, 64, 64)
        NH = 8
        HD = DIM // NH
        CS = 16
        BASE_LR = 1.0
        EPS_IN = 1e-06
        EPS_OUT = 1e-05

        def _ln(x, g, b, eps):
            mu = x.mean(-1, keepdims=True)
            var = ((x - mu) ** 2).mean(-1, keepdims=True)
            return (x - mu) / jnp.sqrt(var + eps) * g + b

        def _ln_l2_bwd(Z, tgt, g, b):
            D = Z.shape[-1]
            mu = Z.mean(-1, keepdims=True)
            var = ((Z - mu) ** 2).mean(-1, keepdims=True)
            std = jnp.sqrt(var + EPS_IN)
            xh = (Z - mu) / std
            gxh = (g * xh + b - tgt) * g
            return (D * gxh - gxh.sum(-1, keepdims=True) - xh * (gxh * xh).sum(-1, keepdims=True)) / (D * std)

        def _rope(x, L):
            inv = 1.0 / 10000.0 ** (jnp.arange(0, HD, 2, dtype=jnp.float32) / HD)
            fr = jnp.arange(L, dtype=jnp.float32)[:, None] * inv[None, :]
            emb = jnp.concatenate([fr, fr], axis=-1)
            cos, sin = (jnp.cos(emb), jnp.sin(emb))
            x1, x2 = jnp.split(x, 2, axis=-1)
            return x * cos + jnp.concatenate([-x2, x1], axis=-1) * sin

        def _ttt_linear(xn, q_w, k_w, v_w, o_w, W1, b1, ttt_ln_w, ttt_ln_b, lr_w, lr_b, tok_idx_delta, post_w, post_b):
            Bsz, L, _ = xn.shape
            NC = L // CS
            heads = lambda t: t.reshape(Bsz, L, NH, HD).transpose(0, 2, 1, 3)
            XQ = _rope(heads(xn @ q_w.T), L)
            XK = _rope(heads(xn @ k_w.T), L)
            XV = heads(xn @ v_w.T)
            Xc = xn.reshape(Bsz, NC, CS, DIM)
            ttt_lr = jax.nn.sigmoid(jnp.einsum('bnkc,hdc->bhnkd', Xc, lr_w) + lr_b.reshape(1, NH, 1, 1, 1))
            ttt_lr_eta = BASE_LR / HD * ttt_lr.transpose(0, 1, 2, 4, 3)
            token_idx = jnp.maximum(1.0 / jnp.arange(1, CS + 1, dtype=jnp.float32) + tok_idx_delta, 0.0)
            eta = token_idx.reshape(1, 1, 1, CS, 1) * ttt_lr_eta
            g = ttt_ln_w[None, :, None, :]
            bb = ttt_ln_b[None, :, None, :]

            def step(carry, inp):
                W1c, b1c = carry
                xq, xk, xv, et = inp
                Z1 = xk @ W1c + b1c
                grad = _ln_l2_bwd(Z1, xv - xk, g, bb)
                Attn1 = jnp.tril(xq @ xk.swapaxes(-1, -2))
                b1_bar = b1c - jnp.tril(et) @ grad
                Z1_bar = xq @ W1c - et * Attn1 @ grad + b1_bar
                last_eta = et[..., -1, :, None]
                W1n = W1c - (last_eta * xk).swapaxes(-1, -2) @ grad
                b1n = b1c - (last_eta * grad).sum(-2, keepdims=True)
                return ((W1n, b1n), xq + _ln(Z1_bar, g, bb, EPS_IN))
            W1_0 = jnp.broadcast_to(W1[None], (Bsz, NH, HD, HD)) + 0.0
            b1_0 = jnp.broadcast_to(b1[None], (Bsz, NH, 1, HD)) + 0.0
            chunk = lambda t: t.reshape(Bsz, NH, NC, CS, HD).transpose(2, 0, 1, 3, 4)
            _, out = jax.lax.scan(step, (W1_0, b1_0), (chunk(XQ), chunk(XK), chunk(XV), eta.transpose(2, 0, 1, 3, 4)))
            out = out.transpose(1, 2, 0, 3, 4).reshape(Bsz, NH, L, HD).transpose(0, 2, 1, 3).reshape(Bsz, L, DIM)
            return _ln(out, post_w, post_b, EPS_IN) @ o_w.T
        Bsz, d = x.shape[:2]
        n_tok = x.shape[2] * x.shape[3]
        xf = x.reshape(Bsz, d, n_tok).transpose(0, 2, 1)
        xn = _ln(xf, ln_w, ln_b, EPS_OUT)
        y = _ttt_linear(xn, q_w, k_w, v_w, o_w, W1, b1, ttt_ln_w, ttt_ln_b, lr_w, lr_b, tok_idx_delta, post_w, post_b)
        return y.transpose(0, 2, 1).reshape(x.shape)

    def _L1_conv_ref(x, w1, w2, b1, b2):
        import jax, jax.numpy as jnp
        import numpy as np
        GROUPS = 4
        CHANNELS = 512
        SCALE = 0.02
        B, C, H, W = x.shape
        g = w1.shape[1]
        d = C // g
        spec = jnp.fft.rfft2(x, axes=(2, 3), norm='ortho')
        origin = spec
        out = spec.reshape(B, g, d, H, spec.shape[-1])
        xr, xi = (out.real, out.imag)

        def cmul(ar, ai, w, b):
            or_ = jnp.einsum('bkihw,kio->bkohw', ar, w[0]) - jnp.einsum('bkihw,kio->bkohw', ai, w[1]) + b[0][None, :, :, None, None]
            oi_ = jnp.einsum('bkihw,kio->bkohw', ai, w[0]) + jnp.einsum('bkihw,kio->bkohw', ar, w[1]) + b[1][None, :, :, None, None]
            return (or_, oi_)
        o1r, o1i = cmul(xr, xi, w1, b1)
        o1r, o1i = (jax.nn.relu(o1r), jax.nn.relu(o1i))
        o2r, o2i = cmul(o1r, o1i, w2, b2)
        out_c = (o2r + 1j * o2i).reshape(B, C, H, spec.shape[-1])
        out_c = out_c * origin
        return jnp.fft.irfft2(out_c, s=(H, W), axes=(2, 3), norm='ortho')

    def _L2_conv_ref(x, w1, w2, fc1_w, fc2_w):
        import jax, jax.numpy as jnp
        import numpy as np
        from jax import lax
        DN = ('NCHW', 'OIHW', 'NCHW')
        b, c, h, w = x.shape
        y1 = jnp.broadcast_to(x.mean(axis=(2, 3), keepdims=True), (b, c, 4, 4))
        y2 = x.reshape(b, c, 2, h // 2, 2, w // 2).mean(axis=(3, 5))
        y2 = jnp.repeat(jnp.repeat(y2, 2, axis=2), 2, axis=3)
        y4 = x.reshape(b, c, 4, h // 4, 4, w // 4).mean(axis=(3, 5))
        t = jnp.stack([y1, y2, y4], axis=2).reshape(b * c, 3, 4, 4)
        z = lax.conv_general_dilated(t, w1, (1, 1), 'VALID', dimension_numbers=DN)
        z = lax.conv_general_dilated(z, w2, (3, 3), [(1, 1), (1, 1)], dimension_numbers=DN)
        s = z.reshape(b, c)
        s = jax.nn.relu(s @ fc1_w.T) @ fc2_w.T
        s = jax.nn.sigmoid(s).reshape(b, c, 1, 1)
        return x * s

    def _L3_conv_ref(x, w1, w2, b1, b2):
        import jax, jax.numpy as jnp
        import numpy as np
        GROUPS = 4
        CHANNELS = 512
        SCALE = 0.02
        B, C, H, W = x.shape
        g = w1.shape[1]
        d = C // g
        spec = jnp.fft.rfft2(x, axes=(2, 3), norm='ortho')
        origin = spec
        out = spec.reshape(B, g, d, H, spec.shape[-1])
        xr, xi = (out.real, out.imag)

        def cmul(ar, ai, w, b):
            or_ = jnp.einsum('bkihw,kio->bkohw', ar, w[0]) - jnp.einsum('bkihw,kio->bkohw', ai, w[1]) + b[0][None, :, :, None, None]
            oi_ = jnp.einsum('bkihw,kio->bkohw', ai, w[0]) + jnp.einsum('bkihw,kio->bkohw', ar, w[1]) + b[1][None, :, :, None, None]
            return (or_, oi_)
        o1r, o1i = cmul(xr, xi, w1, b1)
        o1r, o1i = (jax.nn.relu(o1r), jax.nn.relu(o1i))
        o2r, o2i = cmul(o1r, o1i, w2, b2)
        out_c = (o2r + 1j * o2i).reshape(B, C, H, spec.shape[-1])
        out_c = out_c * origin
        return jnp.fft.irfft2(out_c, s=(H, W), axes=(2, 3), norm='ortho')

    def _gn(v, G=32, eps=1e-5):
        B_, C_, H_, W_ = v.shape
        g = v.reshape(B_, G, C_ // G, H_, W_)
        m = jnp.mean(g, axis=(2, 3, 4), keepdims=True)
        s = jnp.var(g, axis=(2, 3, 4), keepdims=True)
        return ((g - m) / jnp.sqrt(s + eps)).reshape(v.shape)

    def _ln_c(v, eps=1e-6):
        m = jnp.mean(v, axis=1, keepdims=True)
        s = jnp.var(v, axis=1, keepdims=True)
        return (v - m) / jnp.sqrt(s + eps)

    def _ln_t(v, eps=1e-5):
        m = jnp.mean(v, axis=-1, keepdims=True)
        s = jnp.var(v, axis=-1, keepdims=True)
        return (v - m) / jnp.sqrt(s + eps)

    def _to_tokens(v):
        B_, C_, H_, W_ = v.shape
        return v.reshape(B_, C_, H_ * W_).transpose(0, 2, 1)
    def _from_tokens(t, like):
        B_, C_, H_, W_ = like.shape
        return t.transpose(0, 2, 1).reshape(B_, C_, H_, W_)

    x = x + _L0_conv_ref(_gn(x), L0_conv_ln_w, L0_conv_ln_b, L0_conv_q_w, L0_conv_k_w, L0_conv_v_w, L0_conv_o_w, L0_conv_W1, L0_conv_b1, L0_conv_ttt_ln_w, L0_conv_ttt_ln_b, L0_conv_lr_w, L0_conv_lr_b, L0_conv_tok_idx_delta, L0_conv_post_w, L0_conv_post_b)
    x = x + _L1_conv_ref(_gn(x), L1_conv_w1, L1_conv_w2, L1_conv_b1, L1_conv_b2)
    x = x + _L2_conv_ref(_gn(x), L2_conv_w1, L2_conv_w2, L2_conv_fc1_w, L2_conv_fc2_w)
    x = x + _L3_conv_ref(_gn(x), L3_conv_w1, L3_conv_w2, L3_conv_b1, L3_conv_b2)
    return x


_drawn_inputs = setup_inputs


def setup_inputs(seed=0):
    import zlib

    import numpy as np

    out = dict(_drawn_inputs(seed))
    spreads = {'L0_conv_ln_w': (1.0, 0.2),
     'L0_conv_ln_b': (0.0, 0.1),
     'L0_conv_b1': (0.0, 0.1),
     'L0_conv_ttt_ln_w': (1.0, 0.2),
     'L0_conv_ttt_ln_b': (0.0, 0.1),
     'L0_conv_lr_b': (0.0, 0.8),
     'L0_conv_tok_idx_delta': (0.0, 0.1),
     'L0_conv_post_w': (1.0, 0.2),
     'L0_conv_post_b': (0.0, 0.1)}
    factors = {'L1_conv_b1': 8.0,
     'L2_conv_w1': 8.0,
     'L2_conv_w2': 8.0,
     'L2_conv_fc1_w': 8.0,
     'L2_conv_fc2_w': 8.0,
     'L3_conv_b1': 8.0,
     'L3_conv_b2': 3.554}
    for name, (base, spread) in spreads.items():
        noise = np.random.default_rng([zlib.crc32(name.encode()), seed]).standard_normal(out[name].shape)
        drawn = base * np.exp(spread * noise) if base else spread * noise
        out[name] = jnp.asarray(drawn.astype(out[name].dtype))
    for name, factor in factors.items():
        out[name] = (out[name] * factor).astype(out[name].dtype)
    return out
```

```python
from contextlib import ExitStack, contextmanager

import numpy as np

import concourse.bass as bass
from concourse import mybir

F32 = mybir.dt.float32
ALU = mybir.AluOpType
ACT = mybir.ActivationFunctionType
AX = mybir.AxisListType

P = 128
B, C, H, W = 4, 512, 64, 64
TOK = H * W
CT = C // P
UNITS = B * CT
NH, HD, CS = 8, 64, 16
RW = 2 * HD + 4


def dft_matrices():
    k = np.arange(64)
    ang = 2 * np.pi * np.outer(k, k) / 64
    cos, sin = np.cos(ang) / 8, np.sin(ang) / 8
    rows = np.zeros((64, 32, 2))
    rows[:, :, 0], rows[:, :, 1] = cos[:, :32], -sin[:, :32]
    rows[:, 0, 1] = cos[:, 32]
    back = np.zeros((32, 2, 64))
    back[:, 0], back[:, 1] = 2 * cos[:32], -2 * sin[:32]
    back[0, 0], back[0, 1] = cos[0], cos[32]
    F1 = np.zeros((2, 64, 32, 2, 2))
    G1 = np.zeros((2, 32, 2, 2, 64))
    for r in range(2):
        F1[r, :, :, r, :] = rows
        G1[r, :, :, r, :] = back
    F2 = np.zeros((64, 2, 2, 64))
    F2[:, 0, 0], F2[:, 1, 0], F2[:, 0, 1], F2[:, 1, 1] = cos, sin, -sin, cos
    F2a, F2b = np.zeros_like(F2), np.zeros_like(F2)
    F2a[:, 0], F2b[:, 1] = F2[:, 0], F2[:, 0]
    G2 = np.zeros((2, 64, 64, 2))
    G2[0, :, :, 0], G2[1, :, :, 0], G2[0, :, :, 1], G2[1, :, :, 1] = cos, -sin, sin, cos
    G2a, G2b = np.zeros_like(G2), np.zeros_like(G2)
    G2a[..., 0], G2b[..., 1] = G2[..., 0], G2[..., 0]
    mats = [F1, F2, F2a, F2b, G2, G2a, G2b, G1, np.eye(128)]
    return np.stack([m.reshape(128, 128) for m in mats]).astype(np.float32)




@contextmanager
def semaphore(nc, name):
    sem = nc.alloc_semaphore(name=name)
    yield sem
    nc.gpsimd.sem_clear(sem)
    nc.release_semaphore(sem)
class Signal:

    def __init__(self, ctx, nc, name, per=1, credit=0):
        self.sem = ctx.enter_context(semaphore(nc, name))
        self.per, self.credit = per, credit

    def at(self, step, n):
        return step * self.per + (n + self.credit)

    def give(self, eng):
        eng.sem_inc(self.sem, self.credit)


def spectral_batches():
    packed, slots = [(0, 3)], [(0, 4)]
    while slots[-1][0] + slots[-1][1] < W // 2 + 1:
        s = slots[-1][0] + slots[-1][1]
        n = min(4, W // 2 + 1 - s)
        packed.append((s - 1, n))
        slots.append((s, n))
    return packed, slots


def fourier_layer(nc, name, x_in, x_out, weights, biases, dft, coef, chan_stats, block_sums, units_outer=B):
    x_view = x_in.rearrange("b (k c) h w -> (b k) c (h w)", c=P)
    o_view = x_out.rearrange("b (k c) h w -> (b k) c (h w)", c=P)
    packed, slots = spectral_batches()
    NB1 = TOK // 512
    NB2 = len(slots)
    NT = 2 * (NB1 + NB2)
    chunks = [(0, 7), (7, 14), (14, 21), (21, 27), (27, 33)]
    NCH = len(chunks)
    CW = 7 * H

    with ExitStack() as ctx:
        def sb(n, shape):
            return ctx.enter_context(nc.sbuf_tensor(f"{name}_{n}", shape, F32))

        def ps(n, shape):
            return ctx.enter_context(nc.psum_tensor(f"{name}_{n}", shape, F32))

        def sig(n, per=1, credit=0):
            return Signal(ctx, nc, f"{name}_{n}", per, credit)

        xb = [sb(f"x{k}", [P, TOK]) for k in range(2)]
        wt = [sb(f"weights{k}", [P, 4, P]) for k in range(2)]
        wneg = [sb(f"weights_neg{k}", [P, 2, P]) for k in range(2)]
        bias = [sb(f"bias{k}", [P, 4]) for k in range(2)]
        half = sb("half", [P, TOK])
        spec = sb("spec", [P, W // 2 + 1, 2, H])
        turned = [sb(f"turned{k}", [P, 512]) for k in range(2)]
        hidden = [sb(f"hidden{k}", [P, 2, CW]) for k in range(2)]
        prod = [sb(f"prod{k}", [P, 4, CW]) for k in range(2)]
        mats = sb("mats", [P, 9, P])
        ident = sb("ident", [P, P])
        stats6 = sb("stats6", [P, UNITS, NB1 * 6])
        rowsum = sb("rowsum", [P, H * 4])
        psT = [ps(f"psT{k}", [P, 512]) for k in range(2)]
        psD = [ps(f"psD{k}", [P, 512]) for k in range(2)]
        psA = [ps(f"psA{k}", [P, 512]) for k in range(2)]
        psB = [ps(f"psB{k}", [P, 512]) for k in range(2)]

        const_in = sig("const_in")
        x_loaded = [sig(f"x_loaded{k}") for k in range(2)]
        w_loaded = [sig(f"w_loaded{k}") for k in range(2)]
        x_stored = [sig(f"x_stored{k}") for k in range(2)]
        neg_made = sig("neg_made", 1)
        turned_ps = sig("turned_ps", NT)
        turned_sb = sig("turned_sb", NT, credit=2)
        dft_ps = sig("dft_ps", NT, credit=2)
        dft_sb = sig("dft_sb", NT, credit=2 * NT)
        dc_added = sig("dc_added", 1)
        mix1_ps = sig("mix1_ps", 2 * NCH)
        hidden_sb = sig("hidden_sb", 2 * NCH)
        mix2_ps = sig("mix2_ps", 2 * NCH)
        terms_sb = sig("terms_sb", NCH)
        prod_sb = sig("prod_sb", NCH, credit=2)
        rest_added = sig("rest_added", 1)
        rows_summed = sig("rows_summed", 1)
        stat_done = sig("stat_done", NB1 + 1, credit=2 * NB1 + 2)

        F1, F2, F2a, F2b, G2, G2a, G2b, G1 = (mats[:, n, :] for n in range(8))
        block = ctx.enter_context(nc.Block())

        def loop(eng, body):
            with eng.Fori(0, units_outer) as b:
                with eng.Fori(0, 2) as pair:
                    for k in range(2):
                        body(b * 4 + pair * 2 + k, b * 2 + pair, k, pair * 2 + k)

        @block.sync
        def _(sp):
            sp.dma_start(mats[:, 0:8, :], dft.rearrange("n p m -> p n m")[:, 0:8, :]).then_inc(const_in.sem, 16)
            sp.dma_start(ident[:], dft[8]).then_inc(const_in.sem, 16)

            def unit(u, it, k, ct):
                sp.wait_ge(x_stored[k].sem, it * 16)
                if chan_stats is not None:
                    sp.wait_ge(stat_done.sem, stat_done.at(u, -stat_done.per))
                sp.wait_ge(dft_sb.sem, dft_sb.at(u, -NT))
                sp.dma_start(xb[k][:], x_view[bass.ds(u, 1)].rearrange("o c n -> (o c) n")).then_inc(x_loaded[k].sem, 16)
                sp.dma_start(wt[k][:], weights[bass.ds(ct, 1)].rearrange("q i r o -> (q i) r o")).then_inc(w_loaded[k].sem, 16)
                sp.dma_start(bias[k][:], biases[bass.ds(ct, 1)].rearrange("q c r -> (q c) r")).then_inc(w_loaded[k].sem, 16)

            dft_sb.give(sp)
            if chan_stats is not None:
                stat_done.give(sp)
            loop(sp, unit)

        @block.gpsimd
        def _(pool):
            def unit(u, it, k, ct):
                for c, (s0, s1) in enumerate(chunks):
                    n = (s1 - s0) * H
                    q = (k * NCH + c) % 2
                    pool.wait_ge(terms_sb.sem, terms_sb.at(u, c + 1))
                    re = spec[:, s0:s1, 0, :]
                    im = spec[:, s0:s1, 1, :]
                    pv = prod[q][:, :, 0:n].rearrange("p t (s h) -> p t s h", h=H)
                    nc.gpsimd.tensor_tensor(re, pv[:, 0], pv[:, 1], ALU.subtract)
                    nc.gpsimd.tensor_tensor(im, pv[:, 2], pv[:, 3], ALU.add).then_inc(prod_sb.sem, 1)
            loop(pool, unit)

        @block.scalar
        def _(act):
            def evacuate(u, t, width=512):
                act.wait_ge(turned_ps.sem, turned_ps.at(u, t + 1))
                act.wait_ge(dft_ps.sem, dft_ps.at(u, t - 1))
                nc.scalar.copy(turned[t % 2][:, 0:width], psT[t % 2][:, 0:width]).then_inc(turned_sb.sem, 1)

            def unit(u, it, k, ct):
                act.wait_ge(w_loaded[k].sem, it * 32 + 32)
                nc.scalar.mul(wneg[k][:], wt[k][:, 1:4:2, :], -1.0).then_inc(neg_made.sem, 1)
                for t in range(NB1):
                    evacuate(u, t)
                for n in range(NB2):
                    evacuate(u, NB1 + n, packed[n][1] * P)
                for c, (s0, s1) in enumerate(chunks):
                    n = (s1 - s0) * H
                    q = (k * NCH + c) % 2
                    if c >= 2:
                        act.wait_ge(mix2_ps.sem, mix2_ps.at(u, 2 * (c - 1)))
                    for r in range(2):
                        act.wait_ge(mix1_ps.sem, mix1_ps.at(u, 2 * c + r + 1))
                        nc.scalar.activation(hidden[q][:, r, 0:n], psA[r][:, 0:n], ACT.Relu,
                                             bias=bias[k][:, r:r + 1]).then_inc(hidden_sb.sem, 1)
                for n in range(NB2):
                    evacuate(u, NB1 + NB2 + n, slots[n][1] * P)
                for t in range(NB1):
                    evacuate(u, NB1 + 2 * NB2 + t)
                act.wait_ge(dft_sb.sem, dft_sb.at(u, NT))
                act.dma_start(o_view[bass.ds(u, 1)].rearrange("o c n -> (o c) n"), xb[k][:]).then_inc(x_stored[k].sem, 16)
            dft_ps.give(act)
            loop(act, unit)
            for k in range(2):
                act.wait_ge(x_stored[k].sem, 16 * 2 * units_outer)

        @block.vector
        def _(dve):
            def unit(u, it, k, ct):
                cf = coef[:, bass.ds(u, 1), :].rearrange("p o e -> p (o e)")
                for t in range(NB1):
                    dve.wait_ge(dft_ps.sem, dft_ps.at(u, t + 1))
                    dst = half[:, :].rearrange("p (w j e) -> p w j e", w=32, e=4)[:, :, 4 * t:4 * t + 4, :]
                    nc.vector.tensor_scalar(dst, psD[t % 2][:, :].rearrange("p (j w e) -> p w j e", j=4, e=4),
                                            cf[:, 0:1], None, ALU.mult).then_inc(dft_sb.sem, 1)
                for n, (s, m) in enumerate(slots):
                    t = NB1 + n
                    dve.wait_ge(dft_ps.sem, dft_ps.at(u, t + 1))
                    nc.vector.tensor_copy(spec[:, s:s + m].rearrange("p s r h -> p (s r h)"),
                                          psD[t % 2][:, 0:m * P]).then_inc(dft_sb.sem, 1)
                    if n == 0:
                        dve.wait_ge(dft_sb.sem, dft_sb.at(u, t + 1))
                        nc.vector.tensor_tensor(spec[:, 0, 0, 0:1], spec[:, 0, 0, 0:1], cf[:, 1:2],
                                                ALU.add).then_inc(dc_added.sem, 1)
                for c, (s0, s1) in enumerate(chunks):
                    n = (s1 - s0) * H
                    q = (k * NCH + c) % 2
                    dve.wait_ge(prod_sb.sem, prod_sb.at(u, c - 1))
                    re = spec[:, s0:s1, 0, :]
                    im = spec[:, s0:s1, 1, :]
                    if c == 0:
                        dve.wait_ge(dc_added.sem, u + 1)
                        dve.wait_ge(dft_sb.sem, dft_sb.at(u, NB1 + NB2))
                    for r, (b0, b1_) in enumerate(((re, im), (im, re))):
                        dve.wait_ge(mix2_ps.sem, mix2_ps.at(u, 2 * c + r + 1))
                        src = psB[r][:, 0:n].rearrange("p (s h) -> p s h", h=H)
                        for term, with_ in ((0, re), (3, im)) if r == 0 else ((1, im), (2, re)):
                            last = nc.vector.scalar_tensor_tensor(
                                prod[q][:, term, 0:n].rearrange("p (s h) -> p s h", h=H), src,
                                bias[k][:, 2 + r:3 + r], with_, ALU.add, ALU.mult)
                    last.then_inc(terms_sb.sem, 1)
                    if c == 0:
                        dve.wait_ge(prod_sb.sem, prod_sb.at(u, c + 1))
                        nc.vector.tensor_tensor(spec[:, 0, 0, 0:1], spec[:, 0, 0, 0:1], cf[:, 3:4],
                                                ALU.add).then_inc(rest_added.sem, 1)
                for n, (p0, m) in enumerate(packed):
                    t = NB1 + NB2 + n
                    dve.wait_ge(dft_ps.sem, dft_ps.at(u, t + 1))
                    dst = half[:, :].rearrange("p (h w e) -> p h w e", h=H, e=2)[:, :, p0:p0 + m, :]
                    nc.vector.tensor_copy(dst, psD[t % 2][:, 0:m * P].rearrange("p (w h e) -> p h w e", h=H, e=2)
                                          ).then_inc(dft_sb.sem, 1)
                for n in range(NB1):
                    t = NB1 + 2 * NB2 + n
                    dve.wait_ge(dft_ps.sem, dft_ps.at(u, t + 1))
                    part = xb[k][:, 512 * n:512 * n + 512]
                    nc.vector.scalar_tensor_tensor(part, part, cf[:, 2:3], psD[t % 2][:, :],
                                                   ALU.mult, ALU.add).then_inc(dft_sb.sem, 1)
                if chan_stats is not None:
                    for n in range(NB1):
                        dve.wait_ge(dft_sb.sem, dft_sb.at(u, NB1 + 2 * NB2 + n + 1))
                        nc.vector.bn_stats(stats6[:, bass.ds(u, 1), 6 * n:6 * n + 6].rearrange("p o e -> p (o e)"), xb[k][:, 512 * n:512 * n + 512]).then_inc(stat_done.sem, 1)
                    nc.vector.tensor_reduce(rowsum[:, :], xb[k][:, :].rearrange("p (a w) -> p a w", w=16),
                                            AX.X, ALU.add).then_inc(rows_summed.sem, 1)
                    dve.wait_ge(rows_summed.sem, u + 1)
                    nc.vector.tensor_reduce(block_sums[:, bass.ds(u, 1), :].rearrange("p o (a b) -> p (o a) b", b=4),
                                            rowsum[:, :].rearrange("p (a h b) -> p a b h", a=4, b=4),
                                            AX.X, ALU.add).then_inc(stat_done.sem, 1)
            dve.wait_ge(const_in.sem, 32)
            prod_sb.give(dve)
            loop(dve, unit)
            if chan_stats is not None:
                dve.wait_ge(stat_done.sem, units_outer * 4 * stat_done.per + stat_done.credit)
                for u in range(units_outer * 4):
                    nc.vector.bn_aggr(chan_stats[:, u, :], stats6[:, u, :])

        @block.tensor
        def _(pe):
            def transposes(u, t, blocks):
                pe.wait_ge(turned_sb.sem, turned_sb.at(u, t - 1))
                for j, src in enumerate(blocks):
                    last = pe.transpose(psT[t % 2][:, j * P:(j + 1) * P], src, ident[:])
                last.then_inc(turned_ps.sem, 1)

            def transforms(u, t, products):
                pe.wait_ge(turned_sb.sem, turned_sb.at(u, t + 1))
                pe.wait_ge(dft_sb.sem, dft_sb.at(u, t - 1))
                for col, width, terms in products:
                    for n, (j, mat) in enumerate(terms):
                        last = pe.matmul(psD[t % 2][:, col:col + width], turned[t % 2][:, j * P:(j + 1) * P], mat,
                                         start=n == 0, stop=n == len(terms) - 1)
                last.then_inc(dft_ps.sem, 1)

            def stage(u, t0, turns, trans):
                turns[0]()
                for n in range(len(turns)):
                    if n + 1 < len(turns):
                        turns[n + 1]()
                    trans[n]()

            def unit(u, it, k, ct):
                pe.wait_ge(x_loaded[k].sem, it * 16 + 16)
                stage(u, 0,
                      [lambda n=n: transposes(u, n, [xb[k][:, (4 * n + j) * P:(4 * n + j + 1) * P] for j in range(4)])
                       for n in range(NB1)],
                      [lambda n=n: transforms(u, n, [(j * P, P, [(j, F1)]) for j in range(4)]) for n in range(NB1)])
                pe.wait_ge(dft_sb.sem, dft_sb.at(u, NB1))
                t0 = NB1
                stage(u, t0,
                      [lambda n=n, p0=p0, m=m: transposes(u, t0 + n, [half[:, (p0 + j) * P:(p0 + j + 1) * P] for j in range(m)])
                       for n, (p0, m) in enumerate(packed)],
                      [lambda n=n, m=m: transforms(u, t0 + n, ([(0, P, [(0, F2a)]), (P, P, [(0, F2b)])] +
                                                          [(j * P + P, P, [(j, F2)]) for j in range(1, m)]) if n == 0 else
                                              [(j * P, P, [(j, F2)]) for j in range(m)])
                       for n, (p0, m) in enumerate(packed)])
                pe.wait_ge(w_loaded[k].sem, it * 32 + 32)
                pe.wait_ge(neg_made.sem, u + 1)

                def mix1(c):
                    s0, s1 = chunks[c]
                    n = (s1 - s0) * H
                    re = spec[:, s0:s1, 0, :]
                    im = spec[:, s0:s1, 1, :]
                    if c == 0:
                        pe.wait_ge(dc_added.sem, u + 1)
                    pe.wait_ge(dft_sb.sem, dft_sb.at(u, NB1 + min(NB2, -(-s1 // 4))))
                    for r, (wa, wb) in enumerate(((wt[k][:, 0], wneg[k][:, 0]), (wt[k][:, 1], wt[k][:, 0]))):
                        if c:
                            pe.wait_ge(hidden_sb.sem, hidden_sb.at(u, 2 * c - 1 + r))
                        pe.matmul(psA[r][:, 0:n], wa, re, start=True, stop=False)
                        pe.matmul(psA[r][:, 0:n], wb, im, start=False, stop=True).then_inc(mix1_ps.sem, 1)

                def mix2(c):
                    s0, s1 = chunks[c]
                    n = (s1 - s0) * H
                    q = (k * NCH + c) % 2
                    pe.wait_ge(hidden_sb.sem, hidden_sb.at(u, 2 * c + 2))
                    if c:
                        pe.wait_ge(terms_sb.sem, terms_sb.at(u, c))
                    for r, (wa, wb) in enumerate(((wt[k][:, 2], wneg[k][:, 1]), (wt[k][:, 3], wt[k][:, 2]))):
                        pe.matmul(psB[r][:, 0:n], wa, hidden[q][:, 0, 0:n], start=True, stop=False)
                        pe.matmul(psB[r][:, 0:n], wb, hidden[q][:, 1, 0:n], start=False, stop=True).then_inc(mix2_ps.sem, 1)

                mix1(0)
                for c in range(NCH):
                    if c + 1 < NCH:
                        mix1(c + 1)
                    mix2(c)

                t1 = NB1 + NB2

                def turn_back(n):
                    s, m = slots[n]
                    chunk = next(c for c, (a, b) in enumerate(chunks) if s + m <= b)
                    if n == 0:
                        pe.wait_ge(rest_added.sem, u + 1)
                    pe.wait_ge(prod_sb.sem, prod_sb.at(u, chunk + 1))
                    transposes(u, t1 + n, [spec[:, s + j].rearrange("p r h -> p (r h)") for j in range(m)])

                stage(u, t1,
                      [lambda n=n: turn_back(n) for n in range(NB2)],
                      [lambda n=n: transforms(u, t1 + n, ([(0, P, [(0, G2a), (1, G2b)])] +
                                                          [(j * P - P, P, [(j, G2)]) for j in range(2, 4)]) if n == 0 else
                                              [(j * P, P, [(j, G2)]) for j in range(slots[n][1])])
                       for n in range(NB2)])
                pe.wait_ge(dft_sb.sem, dft_sb.at(u, NB1 + 2 * NB2))
                t2 = NB1 + 2 * NB2
                stage(u, t2,
                      [lambda n=n: transposes(u, t2 + n, [half[:, (4 * n + j) * P:(4 * n + j + 1) * P] for j in range(4)])
                       for n in range(NB1)],
                      [lambda n=n: transforms(u, t2 + n, [(j * P, P, [(j, G1)]) for j in range(4)]) for n in range(NB1)])

            pe.wait_ge(const_in.sem, 32)
            turned_sb.give(pe)
            loop(pe, unit)


class Steps:

    def __init__(self, ctx, nc, name, eng=None):
        self.sem = ctx.enter_context(semaphore(nc, name))
        self.count = 0

    def then(self, eng, ins):
        self.count += 1
        ins.then_inc(self.sem, 1)
        eng.wait_ge(self.sem, self.count)


def channel_statistics(nc, name, x_in, chan_stats):
    x_view = x_in.rearrange("b (k c) h w -> (b k) c (h w)", c=P)
    parts = TOK // 512
    with ExitStack() as ctx:
        xb = [ctx.enter_context(nc.sbuf_tensor(f"{name}_x{k}", [P, TOK], F32)) for k in range(2)]
        stats6 = ctx.enter_context(nc.sbuf_tensor(f"{name}_s", [P, UNITS, parts * 6], F32))
        loaded = [Signal(ctx, nc, f"{name}_loaded{k}") for k in range(2)]
        read = [Signal(ctx, nc, f"{name}_read{k}", credit=1) for k in range(2)]
        block = ctx.enter_context(nc.Block())

        @block.sync
        def _(sp):
            for k in range(2):
                read[k].give(sp)
            with sp.Fori(0, UNITS // 2) as it:
                for k in range(2):
                    sp.wait_ge(read[k].sem, read[k].at(it, 0))
                    sp.dma_start(xb[k][:], x_view[bass.ds(it * 2 + k, 1)].rearrange("o c n -> (o c) n")).then_inc(loaded[k].sem, 16)

        @block.vector
        def _(dve):
            with dve.Fori(0, UNITS // 2) as it:
                for k in range(2):
                    dve.wait_ge(loaded[k].sem, it * 16 + 16)
                    for n in range(parts):
                        last = nc.vector.bn_stats(stats6[:, bass.ds(it * 2 + k, 1), 6 * n:6 * n + 6].rearrange("p o e -> p (o e)"),
                                                  xb[k][:, 512 * n:512 * n + 512])
                    last.then_inc(read[k].sem, 1)
            for k in range(2):
                dve.wait_ge(read[k].sem, UNITS // 2 + 1)
            for u in range(UNITS):
                nc.vector.bn_aggr(chan_stats[:, u, :], stats6[:, u, :])


def group_norm(nc, name, chan_stats, group_mean, eps, gmean, grstd):
    with ExitStack() as ctx:
        moments = ctx.enter_context(nc.sbuf_tensor(f"{name}_moments", [P, 2, UNITS], F32))
        var = ctx.enter_context(nc.sbuf_tensor(f"{name}_var", [P, UNITS], F32))
        ps = ctx.enter_context(nc.psum_tensor(f"{name}_ps", [P, 2, UNITS], F32))
        made = ctx.enter_context(semaphore(nc, f"{name}_moments_made"))
        averaged = ctx.enter_context(semaphore(nc, f"{name}_averaged"))
        var_made = ctx.enter_context(semaphore(nc, f"{name}_var_made"))
        std_made = ctx.enter_context(semaphore(nc, f"{name}_std_made"))
        steps = Steps(ctx, nc, f"{name}_steps")
        block = ctx.enter_context(nc.Block())
        mean, cvar = chan_stats[:, :, 0], chan_stats[:, :, 1]

        @block.vector
        def _(dve):
            steps.then(dve, nc.vector.tensor_tensor(moments[:, 1, :], mean, mean, ALU.mult))
            steps.then(dve, nc.vector.tensor_tensor(moments[:, 1, :], moments[:, 1, :], cvar, ALU.add))
            nc.vector.tensor_copy(moments[:, 0, :], mean).then_inc(made, 1)
            dve.wait_ge(averaged, 1)
            steps.then(dve, nc.vector.tensor_copy(gmean[:], ps[:, 0, :]))
            steps.then(dve, nc.vector.tensor_tensor(var[:], gmean[:], gmean[:], ALU.mult))
            steps.then(dve, nc.vector.tensor_tensor(var[:], ps[:, 1, :], var[:], ALU.subtract))
            nc.vector.tensor_scalar(var[:], var[:], 0.0, eps, ALU.max, ALU.add).then_inc(var_made, 1)
            dve.wait_ge(std_made, 1)
            steps.then(dve, nc.vector.reciprocal(grstd[:], var[:]))

        @block.scalar
        def _(act):
            act.wait_ge(var_made, 1)
            nc.scalar.activation(var[:], var[:], ACT.Sqrt).then_inc(std_made, 1)

        @block.tensor
        def _(pe):
            pe.wait_ge(made, 1)
            pe.matmul(ps[:].rearrange("p a b -> p (a b)"), group_mean[:], moments[:].rearrange("p a b -> p (a b)"),
                      start=True, stop=True).then_inc(averaged, 1)


def prepare_projections(nc, T, d):
    with ExitStack() as ctx:
        vecs = ctx.enter_context(nc.sbuf_tensor("prep_vecs", [P, 4, CT], F32))
        lnb = ctx.enter_context(nc.sbuf_tensor("prep_lnb", [P, CT, P], F32))
        mean_mat = ctx.enter_context(nc.sbuf_tensor("prep_mean", [P, P], F32))
        lr_b = ctx.enter_context(nc.sbuf_tensor("prep_lr_b", [P, NH], F32))
        ps = [ctx.enter_context(nc.psum_tensor(f"prep_ps{n}", [P, 512], F32)) for n in range(5)]
        landed = ctx.enter_context(semaphore(nc, "prep_landed"))
        ready = ctx.enter_context(semaphore(nc, "prep_lnb_ready"))
        biases = ctx.enter_context(semaphore(nc, "prep_biases"))
        scaled = ctx.enter_context(semaphore(nc, "prep_scaled"))
        means = ctx.enter_context(semaphore(nc, "prep_means"))
        steps = Steps(ctx, nc, "prep_steps")
        block = ctx.enter_context(nc.Block())
        loads = 10

        @block.sync
        def _(sp):
            def load(dst, src):
                sp.dma_start(dst, src).then_inc(landed, 16)
            for n in range(3):
                load(T.w[:, n], d["wT"][n])
            load(T.wo[:], d["wT"][3])
            load(T.lrw[:, :, 0:NH], d["lr_wT"])
            load(vecs[:], d["vecs"])
            load(T.gain[:], d["ttt_rows"][0].partition_broadcast(P))
            load(T.shift[:], d["ttt_rows"][1].partition_broadcast(P))
            load(lr_b[:], d["lr_b_row"].partition_broadcast(P))
            load(T.ident[:], d["dft"][8])

        @block.vector
        def _(dve):
            v = nc.vector
            dve.wait_ge(landed, 16 * loads)
            steps.then(dve, v.memset(lnb[:], 1.0))
            steps.then(dve, v.memset(mean_mat[:], 1.0 / C))
            steps.then(dve, v.memset(T.mean_col[:], 1.0 / C))
            steps.then(dve, v.memset(T.lrw[:, :, NH:NH + 1], 1.0 / C))
            for ct in range(CT):
                last = v.tensor_scalar(lnb[:, ct], lnb[:, ct], vecs[:, 1, ct:ct + 1], None, ALU.mult)
            last.then_inc(ready, 1)
            dve.wait_ge(biases, 1)
            for n in range(2):
                steps.then(dve, v.tensor_copy(T.wbias[:, n], ps[n][:]))
            steps.then(dve, v.tensor_tensor(T.wbias[:, 2], T.shift[:], ps[2][:], ALU.subtract))
            steps.then(dve, v.tensor_tensor(T.wbias[:, 2], T.wbias[:, 2], T.gain[:], ALU.mult))
            steps.then(dve, v.tensor_tensor(T.lrb[:], ps[3][:, 0:NH], lr_b[:], ALU.add))
            steps.then(dve, v.tensor_copy(T.wo_bias[:], ps[4][:, 0:CT]))
            for ct in range(CT):
                for n in range(3):
                    steps.then(dve, v.tensor_scalar(T.w[:, n, ct], T.w[:, n, ct], vecs[:, 0, ct:ct + 1], None, ALU.mult))
                steps.then(dve, v.scalar_tensor_tensor(T.w[:, 2, ct], T.w[:, 2, ct], -1.0, T.gain[:], ALU.mult, ALU.mult))
                steps.then(dve, v.tensor_scalar(T.wo[:, ct], T.wo[:, ct], vecs[:, 2, ct:ct + 1], None, ALU.mult))
                steps.then(dve, v.tensor_scalar(T.lrw[:, ct, 0:NH], T.lrw[:, ct, 0:NH], vecs[:, 0, ct:ct + 1], None, ALU.mult))
            dve.sem_inc(scaled, 1)
            dve.wait_ge(means, 1)
            for ct in range(CT):
                for n in range(3):
                    steps.then(dve, v.tensor_tensor(T.w[:, n, ct], T.w[:, n, ct], ps[n][:], ALU.subtract))
                steps.then(dve, v.tensor_tensor(T.lrw[:, ct, 0:NH], T.lrw[:, ct, 0:NH], ps[3][:, 0:NH], ALU.subtract))

        @block.tensor
        def _(pe):
            pe.wait_ge(landed, 16 * loads)
            pe.wait_ge(ready, 1)
            for ct in range(CT):
                for n in range(3):
                    pe.matmul(ps[n][:], lnb[:, ct], T.w[:, n, ct], start=ct == 0, stop=ct == CT - 1)
                pe.matmul(ps[3][:, 0:NH], lnb[:, ct], T.lrw[:, ct, 0:NH], start=ct == 0, stop=ct == CT - 1)
            for ot in range(CT):
                for ct in range(CT):
                    last = pe.matmul(ps[4][:, ot:ot + 1], T.wo[:, ct, ot * P:(ot + 1) * P], vecs[:, 3, ct:ct + 1],
                                     start=ct == 0, stop=ct == CT - 1)
            last.then_inc(biases, 1)
            pe.wait_ge(scaled, 1)
            for ct in range(CT):
                for n in range(3):
                    pe.matmul(ps[n][:], mean_mat[:], T.w[:, n, ct], start=ct == 0, stop=ct == CT - 1)
                last = pe.matmul(ps[3][:, 0:NH], mean_mat[:], T.lrw[:, ct, 0:NH], start=ct == 0, stop=ct == CT - 1)
            last.then_inc(means, 1)


def project(nc, T, x_in, rope, gn, rec, q_out, images=B, groups=TOK // 512):
    x_view = x_in.rearrange("b (k c) h w -> b c k (h w)", c=P)
    SUB = 4
    with ExitStack() as ctx:
        def sb(n, shape):
            return ctx.enter_context(nc.sbuf_tensor(f"proj_{n}", shape, F32))

        def sig(n, per=1, credit=0):
            return Signal(ctx, nc, f"proj_{n}", per, credit)

        h = [sb(f"h{k}", [P, CT, 512]) for k in range(2)]
        table = [sb(f"rope{k}", [P, SUB, 96]) for k in range(2)]
        gn_now = [sb(f"gn_now{k}", [P, CT, 2]) for k in range(2)]
        sq = sb("sq", [P, CT, 512])
        st = sb("st", [P, SUB, NH + 2])
        small = sb("small", [P, 4, SUB])
        lr = sb("lr", [P, SUB, NH])
        rate = sb("rate", [P, SUB, NH])
        rstd = sb("rstd", [P, SUB])
        lin = [sb(f"lin{k}", [P, 3, 512]) for k in range(2)]
        by_cos = [sb(f"by_cos{k}", [P, 2, 512]) for k in range(2)]
        by_sin = [sb(f"by_sin{k}", [P, 2, 512]) for k in range(2)]
        gk = [sb(f"gk{k}", [P, 512]) for k in range(2)]
        rec_sb = sb("rec", [P, SUB, NH, RW])
        q_sb = sb("q", [P, SUB, 512])
        zero = sb("zero", [2 * CS, NH * RW])
        ps = [[ctx.enter_context(nc.psum_tensor(f"proj_ps{k}{n}", [P, 512], F32)) for n in range(3)] for k in range(2)]
        ps_st = ctx.enter_context(nc.psum_tensor("proj_ps_st", [P, SUB, NH + 2], F32))

        x_loaded = [sig(f"x_loaded{k}") for k in range(2)]
        gn_ready = sig("gn_ready")
        normed = sig("normed", CT)
        squared = sig("squared", 1)
        st_ps = sig("st_ps", 1)
        st_sb = sig("st_sb", 1)
        small_steps = sig("small_steps", 4)
        var_sb = sig("var_sb", 1)
        std_sb = sig("std_sb", 1)
        rstd_sb = sig("rstd_sb", 1)
        lr_sb = sig("lr_sb", 1)
        rate_sb = sig("rate_sb", 1)
        prod_ps = sig("prod_ps", 3 * SUB)
        lin_sb = sig("lin_sb", 3 * SUB, credit=6)
        cos_sb = sig("cos_sb", 2 * SUB, credit=4)
        sin_sb = sig("sin_sb", 2 * SUB)
        rot_sb = sig("rot_sb", 2 * SUB, credit=4)
        gk_sb = sig("gk_sb", SUB)
        u_sb = sig("u_sb", SUB, credit=SUB)
        rec_out = [sig(f"rec_out{j}") for j in range(SUB)]
        q_gone = [sig(f"q_out{j}") for j in range(SUB)]
        init = sig("init")
        pad_out = sig("pad_out")
        block = ctx.enter_context(nc.Block())
        steps_total = images * groups

        def loop(eng, body):
            with eng.Fori(0, images) as b:
                with eng.Fori(0, groups // 2) as g2:
                    for k in range(2):
                        body(b * groups + g2 * 2 + k, b * (groups // 2) + g2, k, b, g2 * 2 + k)

        @block.sync
        def _(sp):
            def body(s, it, k, b, g):
                sp.wait_ge(u_sb.sem, u_sb.at(s, -SUB))
                sp.dma_start(h[k][:], x_view[bass.ds(b, 1), :, :, bass.ds(g * 512, 512)].rearrange("o c k n -> (o c) k n")).then_inc(x_loaded[k].sem, 16)
                sp.dma_start(table[k][:], rope[bass.ds(g * 512, 512), :].rearrange("(j p) e -> p j e", p=P)).then_inc(x_loaded[k].sem, 16)
            cos_sb.give(sp)
            loop(sp, body)

        @block.scalar
        def _(act):
            def body(s, it, k, b, g):
                nc.scalar.copy(gn_now[k][:], gn[:, bass.ds(b * CT, CT), :]).then_inc(gn_ready.sem, 1)
                act.wait_ge(gn_ready.sem, s + 1)
                act.wait_ge(x_loaded[k].sem, it * 32 + 32)
                for ct in range(CT):
                    nc.scalar.activation(h[k][:, ct], h[k][:, ct], ACT.Identity, bias=gn_now[k][:, ct, 1:2],
                                         scale=gn_now[k][:, ct, 0:1]).then_inc(normed.sem, 1)
                act.wait_ge(var_sb.sem, s + 1)
                nc.scalar.activation(small[:, 2, :], small[:, 1, :], ACT.Sqrt).then_inc(std_sb.sem, 1)
                act.wait_ge(lr_sb.sem, s + 1)
                act.wait_ge(gk_sb.sem, gk_sb.at(s, 0))
                nc.scalar.activation(rate[:], lr[:], ACT.Sigmoid).then_inc(rate_sb.sem, 1)
                for j in range(SUB):
                    act.wait_ge(u_sb.sem, u_sb.at(s, j + 1))
                    act.dma_start(rec[bass.ds(b, 1), bass.ds(g * 512 + j * P, P), :, :].rearrange("o n h e -> (o n) h e"),
                                  rec_sb[:, j]).then_inc(rec_out[j].sem, 16)
                    act.dma_start(q_out[bass.ds(b, 1), bass.ds(g * 512 + j * P, P), :].rearrange("o n e -> (o n) e"),
                                  q_sb[:, j]).then_inc(q_gone[j].sem, 16)
            loop(act, body)
            act.wait_ge(init.sem, 1)
            for b in range(B):
                act.dma_start(rec[b, TOK:TOK + 2 * CS].rearrange("n h e -> n (h e)"), zero[:]).then_inc(pad_out.sem, 16)
            act.wait_ge(pad_out.sem, 16 * B)
            for j in range(SUB):
                act.wait_ge(rec_out[j].sem, 16 * steps_total)
                act.wait_ge(q_gone[j].sem, 16 * steps_total)

        @block.gpsimd
        def _(pool):
            g_ = nc.gpsimd

            def body(s, it, k, b, g):
                pool.wait_ge(normed.sem, normed.at(s, CT))
                pool.wait_ge(st_ps.sem, s)
                g_.tensor_tensor(sq[:].rearrange("p a b -> p (a b)"), h[k][:].rearrange("p a b -> p (a b)"),
                                 h[k][:].rearrange("p a b -> p (a b)"), ALU.mult).then_inc(squared.sem, 1)
                pool.wait_ge(rate_sb.sem, s + 1)
                for j in range(SUB):
                    q = j % 2
                    cos = table[k][:, j:j + 1, 0:32].broadcast_to([P, NH * 2, 32])
                    for n in range(2):
                        pool.wait_ge(lin_sb.sem, lin_sb.at(s, 3 * j + n + 1))
                        pool.wait_ge(rot_sb.sem, rot_sb.at(s, 2 * (j - 2) + n + 1))
                        g_.tensor_tensor(by_cos[q][:, n].rearrange("p (a e) -> p a e", e=32),
                                         lin[q][:, n].rearrange("p (a e) -> p a e", e=32), cos, ALU.mult).then_inc(cos_sb.sem, 1)
                    pool.wait_ge(rot_sb.sem, rot_sb.at(s, 2 * j + 2))
                    pool.wait_ge(u_sb.sem, u_sb.at(s, j - 1))
                    g_.tensor_tensor(gk[q][:].rearrange("p (h e) -> p h e", h=NH), rec_sb[:, j, :, 0:HD],
                                     T.gain[:].rearrange("p (h e) -> p h e", h=NH), ALU.mult)
                    g_.tensor_copy(rec_sb[:, j, :, 2 * HD], rate[:, j, :]).then_inc(gk_sb.sem, 1)
            u_sb.give(pool)
            pool.wait_ge(init.sem, 1)
            loop(pool, body)

        @block.vector
        def _(dve):
            v = nc.vector

            def body(s, it, k, b, g):
                n_small = [0]

                def small_step(ins):
                    n_small[0] += 1
                    ins.then_inc(small_steps.sem, 1)
                    dve.wait_ge(small_steps.sem, small_steps.at(s, n_small[0]))

                dve.wait_ge(st_ps.sem, s + 1)
                v.tensor_copy(st[:], ps_st[:]).then_inc(st_sb.sem, 1)
                dve.wait_ge(st_sb.sem, s + 1)
                small_step(v.tensor_tensor(small[:, 0, :], st[:, :, NH], st[:, :, NH], ALU.mult))
                small_step(v.tensor_tensor(small[:, 1, :], st[:, :, NH + 1], small[:, 0, :], ALU.subtract))
                v.tensor_scalar(small[:, 1, :], small[:, 1, :], 0.0, 1e-5, ALU.max, ALU.add).then_inc(var_sb.sem, 1)
                dve.wait_ge(std_sb.sem, s + 1)
                v.reciprocal(rstd[:], small[:, 2, :]).then_inc(rstd_sb.sem, 1)
                dve.wait_ge(rstd_sb.sem, s + 1)
                small_step(v.tensor_tensor(lr[:], st[:, :, 0:NH], rstd[:].unsqueeze(2).broadcast_to([P, SUB, NH]), ALU.mult))
                small_step(v.tensor_tensor(lr[:], lr[:], T.lrb[:].unsqueeze(1).broadcast_to([P, SUB, NH]), ALU.add))
                dve.sem_inc(lr_sb.sem, 1)
                assert n_small[0] == small_steps.per

                def target(j):
                    dve.wait_ge(gk_sb.sem, gk_sb.at(s, j + 1))
                    v.tensor_tensor(rec_sb[:, j, :, HD:2 * HD], gk[j % 2][:].rearrange("p (h e) -> p h e", h=NH),
                                    lin[j % 2][:, 2].rearrange("p (h e) -> p h e", h=NH), ALU.add).then_inc(u_sb.sem, 1)

                for j in range(SUB):
                    q = j % 2
                    for n in range(3):
                        dve.wait_ge(prod_ps.sem, prod_ps.at(s, 3 * j + n + 1))
                        if n < 2:
                            dve.wait_ge(cos_sb.sem, cos_sb.at(s, 2 * (j - 2) + n + 1))
                        v.scalar_tensor_tensor(lin[q][:, n], ps[q][n][:], rstd[:, j:j + 1], T.wbias[:, n],
                                               ALU.mult, ALU.add).then_inc(lin_sb.sem, 1)
                    if j:
                        target(j - 1)
                    for n in range(2):
                        dve.wait_ge(lin_sb.sem, lin_sb.at(s, 3 * j + n + 1))
                        x2 = lin[q][:, n].rearrange("p (h t e) -> p h t e", t=2, e=32)
                        o2 = by_sin[q][:, n].rearrange("p (h t e) -> p h t e", t=2, e=32)
                        for t in range(2):
                            sin = table[k][:, j:j + 1, 32 + 32 * t:64 + 32 * t].broadcast_to([P, NH, 32])
                            last = v.tensor_tensor(o2[:, :, t], x2[:, :, 1 - t], sin, ALU.mult)
                        last.then_inc(sin_sb.sem, 1)
                    dve.wait_ge(rec_out[j].sem, s * 16)
                    dve.wait_ge(q_gone[j].sem, s * 16)
                    for n, dst in enumerate((q_sb[:, j].rearrange("p (h e) -> p h e", h=NH), rec_sb[:, j, :, 0:HD])):
                        dve.wait_ge(sin_sb.sem, sin_sb.at(s, 2 * j + n + 1))
                        dve.wait_ge(cos_sb.sem, cos_sb.at(s, 2 * j + n + 1))
                        v.tensor_tensor(dst, by_cos[q][:, n].rearrange("p (h e) -> p h e", h=NH),
                                        by_sin[q][:, n].rearrange("p (h e) -> p h e", h=NH), ALU.add).then_inc(rot_sb.sem, 1)
                target(SUB - 1)

            v.memset(zero[:], 0.0)
            v.memset(rec_sb[:], 0.0).then_inc(init.sem, 1)
            dve.wait_ge(init.sem, 1)
            rot_sb.give(dve)
            lin_sb.give(dve)
            loop(dve, body)

        @block.tensor
        def _(pe):
            def body(s, it, k, b, g):
                pe.wait_ge(st_sb.sem, s)
                for j in range(SUB):
                    for ct in range(CT):
                        if j == 0:
                            pe.wait_ge(normed.sem, normed.at(s, ct + 1))
                        pe.matmul(ps_st[:, j, 0:NH + 1], h[k][:, ct, j * P:(j + 1) * P], T.lrw[:, ct],
                                  start=ct == 0, stop=ct == CT - 1)
                products(s, k, 0, (0, 1))
                pe.wait_ge(squared.sem, s + 1)
                for j in range(SUB):
                    for ct in range(CT):
                        last = pe.matmul(ps_st[:, j, NH + 1:NH + 2], sq[:, ct, j * P:(j + 1) * P], T.mean_col[:],
                                         start=ct == 0, stop=ct == CT - 1)
                last.then_inc(st_ps.sem, 1)
                products(s, k, 0, (2,))
                for j in range(1, SUB):
                    products(s, k, j, (0, 1, 2))

            def products(s, k, j, which):
                for n in which:
                    pe.wait_ge(lin_sb.sem, lin_sb.at(s, 3 * (j - 2) + n + 1))
                    for ct in range(CT):
                        last = pe.matmul(ps[j % 2][n][:], h[k][:, ct, j * P:(j + 1) * P], T.w[:, n, ct],
                                         start=ct == 0, stop=ct == CT - 1)
                    last.then_inc(prod_ps.sem, 1)

            loop(pe, body)


def scan_chunks(nc, T, d, rec, grad_out, w_snap, b_snap, superchunks=TOK // P):
    GR = 2
    PB = B // GR
    HP = NH // 2
    F = PB * HD
    UNROLL = 4
    with ExitStack() as ctx:
        def sb(n, shape):
            return ctx.enter_context(nc.sbuf_tensor(f"scan_{n}", shape, F32))

        def sig(n, per=1, credit=0):
            return [Signal(ctx, nc, f"scan_{n}{g}", per, credit) for g in range(GR)]

        def many(n, shape, count):
            return [[sb(f"{n}{g}{q}", shape) for q in range(count)] for g in range(GR)]

        def each(n, shape):
            return [sb(f"{n}{g}", shape) for g in range(GR)]

        record = many("record", [P, PB, RW], UNROLL)
        k_pad = many("k_pad", [P, PB, 2, HD], 2)
        k_t = many("k_t", [P, PB, P], 2)
        stored = many("stored", [P, PB, HD], 2)
        w_sb = each("state_w", [P, HP, F])
        b_sb = each("state_b", [NH, F])
        zg = each("zg", [P, PB, HD])
        xh = each("xh", [P, PB, HD])
        both = each("both", [P, 2, PB, HD])
        sums = each("sums", [P, 2, PB])
        cx = each("cx", [P, PB, HD])
        core = each("core", [P, PB, HD])
        step_g = each("step_g", [P, PB, HD])
        ssq = each("ssq", [P, PB])
        std = each("std", [P, PB])
        rstd = each("rstd", [P, PB])
        rate = each("rate", [P, PB])
        rate_w = each("rate_w", [P, PB])
        square = sb("square", [P, GR, PB, HD])
        gain8 = sb("gain8", [P, HD])
        place = sb("place", [P, 2])
        eps = sb("eps", [P, 1])
        tok_in = sb("tok_in", [P, 2])
        last = sb("last", [P, 1])
        ind = sb("ind", [NH, P])
        ind_t = sb("ind_t", [P, NH])
        w0 = sb("w0", [P, HP, B, HD])
        w0_in = sb("w0_in", [P, HP, HD])
        b0 = sb("b0", [NH, B, HD])
        b0_in = sb("b0_in", [NH, HD])
        m0 = sb("m0", [P, HP])
        mb0 = sb("mb0", [NH, 1])
        ps_w = ctx.enter_context(nc.psum_tensor("scan_ps_w", [P, HP, 512], F32))
        ps_b = ps_w[:, 0, 256:512]
        ps_z = ctx.enter_context(nc.psum_tensor("scan_ps_z", [P, GR, 512], F32))
        ps_t = ctx.enter_context(nc.psum_tensor("scan_ps_t", [P, GR, 4, P], F32))

        landed = ctx.enter_context(semaphore(nc, "scan_landed"))
        init = ctx.enter_context(semaphore(nc, "scan_init"))
        start_ps = ctx.enter_context(semaphore(nc, "scan_start_ps"))
        steps = Steps(ctx, nc, "scan_steps")
        rec_in = [[Signal(ctx, nc, f"scan_rec_in{g}{q}") for q in range(UNROLL)] for g in range(GR)]
        grad_gone = [[Signal(ctx, nc, f"scan_grad_gone{g}{q}") for q in range(2)] for g in range(GR)]
        snap_gone = sig("snap_gone")
        pad_sb = sig("pad_sb", credit=1)
        kt_ps = sig("kt_ps")
        kt_sb = sig("kt_sb")
        z_ps = sig("z_ps")
        ssq_sb = sig("ssq_sb")
        std_sb = sig("std_sb")
        rstd_sb = sig("rstd_sb")
        rate_sb = sig("rate_sb", 2, credit=2)
        t_sb = sig("t_sb", credit=1)
        chain = sig("chain", 7)
        core_sb = sig("core_sb")
        stored_sb = sig("stored_sb")
        step_sb = sig("step_sb")
        state_ps = sig("state_ps")
        state_sb = sig("state_sb", 2)
        block = ctx.enter_context(nc.Block())
        loads = 8


        def loop(eng, body, outer=None):
            with eng.Fori(0, superchunks) as sc:
                if outer:
                    outer(sc)
                with eng.Fori(0, P // CS // UNROLL) as part:
                    for k in range(UNROLL):
                        body(sc * 8 + part * UNROLL + k, sc * 2 + part, k, sc, part)

        def load(sp, g, r, s):
            for b in range(PB):
                sp.dma_start(record[g][r][:, b, :], rec[PB * g + b, bass.ds(s * CS, CS)].rearrange("t h e -> h t e")
                             ).then_inc(rec_in[g][r].sem, 16)

        @block.sync
        def _(sp):
            for dst, src in ((gain8, d["gain_rows"]), (place, d["place"]), (ind, d["ind"]), (ind_t, d["ind_t"]),
                             (w0_in, d["w0"]), (b0_in, d["b0"])):
                sp.dma_start(dst[:], src).then_inc(landed, 16)
            for n in range(2):
                sp.dma_start(tok_in[:, n:n + 1], d["tok_rows"][n, CS - 1:CS].partition_broadcast(P)).then_inc(landed, 16)
            for g in range(GR):
                pad_sb[g].give(sp)
                rate_sb[g].give(sp)
                t_sb[g].give(sp)
            for s in range(2):
                for g in range(GR):
                    load(sp, g, s, s)

            def snapshot(sc):
                for g in range(GR):
                    sp.wait_ge(state_sb[g].sem, state_sb[g].at(sc * 8, 2))
                    for b in range(PB):
                        sp.dma_start(w_snap[bass.ds(sc, 1), PB * g + b].rearrange("o p a e -> (o p) a e"),
                                     w_sb[g][:].rearrange("p a (b e) -> p a b e", b=PB)[:, :, b, :]).then_inc(snap_gone[g].sem, 16)
                        sp.dma_start(b_snap[bass.ds(sc, 1), PB * g + b].rearrange("o h e -> (o h) e"),
                                     b_sb[g][:, b * HD:(b + 1) * HD]).then_inc(snap_gone[g].sem, 16)

            def body(s, it, k, sc, part):
                for g in range(GR):
                    sp.wait_ge(rate_sb[g].sem, rate_sb[g].at(s, -2))
                    sp.wait_ge(t_sb[g].sem, t_sb[g].at(s, -1))
                    sp.wait_ge(pad_sb[g].sem, pad_sb[g].at(s, -1))
                    load(sp, g, (k + 2) % UNROLL, s + 2)
                for g in range(GR):
                    sp.wait_ge(stored_sb[g].sem, s + 1)
                    for b in range(PB):
                        sp.dma_start(grad_out[PB * g + b, bass.ds(s * CS, CS)].rearrange("t h e -> h t e"),
                                     stored[g][k % 2][:, b, :]).then_inc(grad_gone[g][k % 2].sem, 16)

            loop(sp, body, snapshot)
            steps_of = 8 * superchunks // UNROLL
            for g in range(GR):
                sp.wait_ge(snap_gone[g].sem, 64 * superchunks)
                for r in range(UNROLL):
                    sp.wait_ge(rec_in[g][r].sem, 32 * (steps_of + (r < 2)))
                for q in range(2):
                    sp.wait_ge(grad_gone[g][q].sem, 32 * steps_of * UNROLL // 2)

        @block.gpsimd
        def _(pool):
            v = nc.gpsimd

            def pad(g, k, s, it):
                pool.wait_ge(rec_in[g][k].sem, it * 32 + 32)
                v.tensor_tensor(k_pad[g][k % 2][:], record[g][k][:, :, 0:HD].unsqueeze(2).broadcast_to([P, PB, 2, HD]),
                                place[:].unsqueeze(1).unsqueeze(3).broadcast_to([P, PB, 2, HD]), ALU.mult).then_inc(pad_sb[g].sem, 1)

            pool.wait_ge(landed, 16 * loads)
            pool.wait_ge(init, 1)
            for g in range(GR):
                pad(g, 0, 0, 0)

            def body(s, it, k, sc, part):
                for g in range(GR):
                    pool.wait_ge(rstd_sb[g].sem, s + 1)
                    v.tensor_tensor(rate[g][:], rstd[g][:], record[g][k][:, :, 2 * HD], ALU.mult).then_inc(rate_sb[g].sem, 1)
                    pool.wait_ge(step_sb[g].sem, s)
                    pool.wait_ge(rate_sb[g].sem, rate_sb[g].at(s, 1))
                    v.tensor_tensor(rate_w[g][:], rate[g][:], last[:].broadcast_to([P, PB]), ALU.mult).then_inc(rate_sb[g].sem, 1)
                    pool.wait_ge(state_ps[g].sem, s + g)
                    pad(g, (k + 1) % UNROLL, s + 1, it + (k + 1) // UNROLL)
                    pool.wait_ge(core_sb[g].sem, s + 1)
                    pool.wait_ge(grad_gone[g][k % 2].sem, it * 32 * (UNROLL // 2) + 32 * (k // 2))
                    v.tensor_tensor(stored[g][k % 2][:], core[g][:], rate[g][:].unsqueeze(2).broadcast_to([P, PB, HD]),
                                    ALU.mult).then_inc(stored_sb[g].sem, 1)

            loop(pool, body)

        @block.scalar
        def _(act):
            a = nc.scalar

            def state_out(g):
                a.copy(w_sb[g][:], ps_w[:, :, g * F:(g + 1) * F]).then_inc(state_sb[g].sem, 1)
                a.copy(b_sb[g][:], ps_b[0:NH, g * F:(g + 1) * F]).then_inc(state_sb[g].sem, 1)

            def turned(g, q, s):
                act.wait_ge(kt_ps[g].sem, kt_ps[g].at(s, 1))
                a.copy(k_t[g][q][:], ps_t[:, g, 0:PB]).then_inc(kt_sb[g].sem, 1)

            def spread(g, s):
                act.wait_ge(z_ps[g].sem, s + 1)
                act.wait_ge(rstd_sb[g].sem, s)
                for b in range(PB):
                    done = a.activation(square[:, g, b], ps_z[:, g, b * HD:(b + 1) * HD], ACT.Square, accum_out=ssq[g][:, b:b + 1])
                done.then_inc(ssq_sb[g].sem, 1)
                act.wait_ge(ssq_sb[g].sem, s + 1)
                a.activation(std[g][:], ssq[g][:], ACT.Sqrt, bias=eps[:]).then_inc(std_sb[g].sem, 1)

            act.wait_ge(start_ps, 1)
            act.wait_ge(init, 1)
            state_out(0)
            for g in range(GR):
                turned(g, 0, 0)

            def body(s, it, k, sc, part):
                spread(0, s)
                act.wait_ge(state_ps[1].sem, s + 1)
                act.wait_ge(snap_gone[1].sem, (sc + part) * 64 if k == 0 else sc * 64 + 64)
                state_out(1)
                spread(1, s)
                for g in range(GR):
                    turned(g, (k + 1) % 2, s + 1)
                act.wait_ge(state_ps[0].sem, s + 1)
                act.wait_ge(snap_gone[0].sem, sc * 64 + 64)
                state_out(0)

            loop(act, body)

        @block.vector
        def _(dve):
            v = nc.vector
            dve.wait_ge(landed, 16 * loads)
            steps.then(dve, v.tensor_tensor(last[:], tok_in[:, 0:1], tok_in[:, 1:2], ALU.add))
            steps.then(dve, v.tensor_scalar(last[:], last[:], 0.0, -1.0 / 8, ALU.max, ALU.mult))
            steps.then(dve, v.memset(eps[:], HD * 1e-6))
            steps.then(dve, v.memset(step_g[1][:], 0.0))
            steps.then(dve, v.memset(k_pad[1][1][:], 0.0))
            steps.then(dve, v.scalar_tensor_tensor(gain8[:], gain8[:], 8.0, gain8[:], ALU.mult, ALU.mult))
            steps.then(dve, v.tensor_reduce(m0[:], w0_in[:], AX.X, ALU.add))
            steps.then(dve, v.tensor_reduce(mb0[:], b0_in[:], AX.X, ALU.add))
            for b in range(B):
                steps.then(dve, v.scalar_tensor_tensor(w0[:, :, b, :], m0[:].unsqueeze(2).broadcast_to([P, HP, HD]), -1.0 / HD,
                                                       w0_in[:], ALU.mult, ALU.add))
                steps.then(dve, v.scalar_tensor_tensor(b0[:, b, :], mb0[:].broadcast_to([NH, HD]), -1.0 / HD,
                                                       b0_in[:], ALU.mult, ALU.add))
            dve.sem_inc(init, 1)

            def body(s, it, k, sc, part):
                for g in range(GR):
                    n = [0]

                    def link(ins):
                        n[0] += 1
                        ins.then_inc(chain[g].sem, 1)
                        dve.wait_ge(chain[g].sem, chain[g].at(s, n[0]))

                    def wide(x):
                        return x.unsqueeze(2).broadcast_to([P, PB, HD])

                    z = ps_z[:, g, 0:F].rearrange("p (b e) -> p b e", b=PB)
                    dve.wait_ge(ssq_sb[g].sem, s + 1)
                    v.tensor_tensor(zg[g][:], z, gain8[:].unsqueeze(1).broadcast_to([P, PB, HD]), ALU.mult)
                    dve.wait_ge(std_sb[g].sem, s + 1)
                    dve.wait_ge(rate_sb[g].sem, rate_sb[g].at(s, 0))
                    v.reciprocal(rstd[g][:], std[g][:]).then_inc(rstd_sb[g].sem, 1)
                    dve.wait_ge(rstd_sb[g].sem, s + 1)
                    v.tensor_tensor(xh[g][:], z, wide(rstd[g][:]), ALU.mult)
                    link(v.tensor_tensor(zg[g][:], zg[g][:], wide(rstd[g][:]), ALU.mult))
                    v.tensor_tensor(both[g][:, 0], zg[g][:], record[g][k][:, :, HD:2 * HD], ALU.add).then_inc(t_sb[g].sem, 1)
                    dve.wait_ge(t_sb[g].sem, t_sb[g].at(s, 1))
                    link(v.tensor_tensor(both[g][:, 1], both[g][:, 0], xh[g][:], ALU.mult))
                    link(v.tensor_reduce(sums[g][:, 1], both[g][:, 1], AX.X, ALU.add))
                    link(v.tensor_tensor(cx[g][:], xh[g][:], wide(sums[g][:, 1]), ALU.mult))
                    link(v.tensor_tensor(cx[g][:], both[g][:, 0], cx[g][:], ALU.subtract))
                    link(v.tensor_reduce(sums[g][:, 0], cx[g][:], AX.X, ALU.add))
                    dve.wait_ge(stored_sb[g].sem, s)
                    link(v.scalar_tensor_tensor(core[g][:], wide(sums[g][:, 0]), -1.0 / HD, cx[g][:], ALU.mult, ALU.add))
                    dve.sem_inc(core_sb[g].sem, 1)
                    dve.wait_ge(rate_sb[g].sem, rate_sb[g].at(s, 2))
                    dve.wait_ge(state_ps[g].sem, s + g)
                    v.tensor_tensor(step_g[g][:], core[g][:], wide(rate_w[g][:]), ALU.mult).then_inc(step_sb[g].sem, 1)
                    assert n[0] == chain[g].per

            loop(dve, body)

        @block.tensor
        def _(pe):
            pe.wait_ge(init, 1)
            for a in range(HP):
                pe.matmul(ps_w[:, a, 0:B * HD], T.ident[:], w0[:, a].rearrange("p b e -> p (b e)"), start=True, stop=True,
                          skip_group_check=True)
            pe.matmul(ps_b[0:NH, 0:B * HD], T.ident[0:NH, 0:NH], b0[:].rearrange("p b e -> p (b e)"), start=False, stop=True,
                      skip_group_check=True).then_inc(start_ps, 1)

            def turn(g, q, s):
                pe.wait_ge(pad_sb[g].sem, pad_sb[g].at(s, 1))
                pe.wait_ge(kt_sb[g].sem, s)
                for b in range(PB):
                    done = pe.transpose(ps_t[:, g, b], k_pad[g][q][:, b].rearrange("p a e -> p (a e)"), T.ident[:])
                done.then_inc(kt_ps[g].sem, 1)

            def project_k(g, q, s):
                pe.wait_ge(kt_sb[g].sem, s + 1)
                pe.wait_ge(state_sb[g].sem, state_sb[g].at(s, 2))
                pe.wait_ge(t_sb[g].sem, t_sb[g].at(s, 0))
                for a in range(HP):
                    rows = slice(32 * a, 32 * a + 32)
                    for b in range(PB):
                        pe.matmul(ps_z[rows, g, b * HD:(b + 1) * HD], k_t[g][q][:, b, rows], w_sb[g][:, a, b * HD:(b + 1) * HD],
                                  start=b == 0, stop=False, skip_group_check=True)
                pe.matmul(ps_z[:, g, 0:F], ind[:], b_sb[g][:], start=False, stop=True,
                          skip_group_check=True).then_inc(z_ps[g].sem, 1)

            def update(g, q, count):
                pe.wait_ge(step_sb[g].sem, count)
                for a in range(HP):
                    rows = slice(32 * a, 32 * a + 32)
                    for b in range(PB):
                        c = g * F + b * HD
                        pe.matmul(ps_w[:, a, c:c + HD], k_pad[g][q][rows, b].rearrange("p a e -> p (a e)"), step_g[g][rows, b, :],
                                  start=False, stop=True, skip_group_check=True)
                pe.matmul(ps_b[0:NH, g * F:(g + 1) * F], ind_t[:], step_g[g][:].rearrange("p b e -> p (b e)"), start=False, stop=True,
                          skip_group_check=True).then_inc(state_ps[g].sem, 1)

            for g in range(GR):
                turn(g, 0, 0)

            def body(s, it, k, sc, part):
                q = k % 2
                project_k(0, q, s)
                update(1, 1 - q, s)
                project_k(1, q, s)
                for g in range(GR):
                    turn(g, 1 - q, s + 1)
                update(0, q, s + 1)

            loop(pe, body)


def read_out(nc, T, d, x_in, rec, q_in, grad, w_snap, b_snap, x_out):
    HP = NH // 2
    SC = TOK // P
    x_view = x_in.rearrange("b (k c) h w -> b c k (h w)", c=P)
    o_view = x_out.rearrange("b (k c) h w -> b c k (h w)", c=P)
    with ExitStack() as ctx:
        def sb(n, shape):
            return ctx.enter_context(nc.sbuf_tensor(f"read_{n}", shape, F32))

        def two(n, shape):
            return [sb(f"{n}{q}", shape) for q in range(2)]

        def ps(n, shape):
            return ctx.enter_context(nc.psum_tensor(f"read_{n}", shape, F32))

        def sig(n, per=1, credit=0):
            return Signal(ctx, nc, f"read_{n}", per, credit)

        k_sb = two("k", [P, NH, HD])
        q_sb = two("q", [P, NH, HD])
        steps_sb = two("steps", [P, NH, HD])
        w_sb = two("w", [P, HP, HD])
        b_sb = two("b", [1, NH, HD])
        x_sb = two("x", [P, CT, P])
        k_t = sb("k_t", [P, HP, P])
        q_t = sb("q_t", [P, HP, P])
        weigh = two("weigh", [P, HP, P])
        zsq = sb("zsq", [P, NH, HD])
        ssq = sb("ssq", [P, NH])
        std = sb("std", [P, NH])
        rstd = sb("rstd", [P, NH])
        zn = two("zn", [P, NH, HD])
        zg = two("zg", [P, NH, HD])
        qb = two("qb", [P, NH, HD])
        o_sb = two("o", [P, NH * HD])
        on = two("on", [P, NH * HD])
        osq = sb("osq", [P, NH * HD])
        osum = two("osum", [P, 2])
        nmean = two("nmean", [P, 1])
        ovar = two("ovar", [P, 1])
        orstd = two("orstd", [P, 1])
        oshift = two("oshift", [P, 1])
        o_t = sb("o_t", [P, CT, P])
        y_sb = two("y", [P, CT, P])
        mask = sb("mask", [P, P])
        masks_in = sb("masks_in", [P, 2, P])
        tok = sb("tok", [P, 2, P])
        gain8 = sb("gain8", [P, NH * HD])
        eps = sb("eps", [P, 2])
        ones = sb("ones", [1, P])
        ps_kt = ps("ps_kt", [P, HP, P])
        ps_qt = ps("ps_qt", [P, HP, P])
        ps_kq = [ps(f"ps_kq{q}", [P, HP, P]) for q in range(2)]
        ps_z = [ps(f"ps_z{q}", [P, HP, P]) for q in range(2)]
        ps_ot = ps("ps_ot", [P, CT, P])
        ps_y = ps("ps_y", [P, CT, P])

        landed = ctx.enter_context(semaphore(nc, "read_landed"))
        init = ctx.enter_context(semaphore(nc, "read_init"))
        steps = Steps(ctx, nc, "read_steps")
        in_sb = [sig(f"in{q}") for q in range(2)]
        x_in_sb = [sig(f"x_in{q}") for q in range(2)]
        y_gone = [sig(f"y_gone{q}") for q in range(2)]
        turned_ps = sig("turned_ps", 2)
        turned_sb = sig("turned_sb", 2)
        kq_ps = sig("kq_ps", 2)
        weigh_sb = sig("weigh_sb", 2, credit=2)
        z_ps = sig("z_ps", 2, credit=2)
        ssq_in = sig("ssq_in", 2)
        ssq_sb = sig("ssq_sb", 1)
        std_sb = sig("std_sb", 1)
        rstd_sb = sig("rstd_sb", 1)
        zn_sb = sig("zn_sb", 1)
        qb_sb = sig("qb_sb", 1, credit=2)
        zg_sb = sig("zg_sb", 1, credit=2)
        o_done = sig("o_done", 1, credit=2)
        osq_sb = sig("osq_sb", 1)
        small = sig("small", 2)
        ovar_sb = sig("ovar_sb", 1)
        ostd_sb = sig("ostd_sb", 1)
        orstd_sb = sig("orstd_sb", 1)
        oshift_sb = sig("oshift_sb", 1)
        on_sb = sig("on_sb", 1)
        ot_ps = sig("ot_ps", 1)
        ot_sb = sig("ot_sb", 1)
        y_ps = sig("y_ps", 1)
        y_sb_done = sig("y_sb", 1, credit=4)
        block = ctx.enter_context(nc.Block())
        loads = 5
        LAG = 2

        def schedule(eng, both):
            def tile(sc, b):
                return sc * B + b, b, sc

            for b in range(LAG):
                both(tile(0, b), None)
            with eng.Fori(0, SC - 1) as sc:
                for b in range(B):
                    both(tile(sc + (b + LAG) // B, (b + LAG) % B), tile(sc, b))
            for b in range(B):
                both(tile(SC - 1, b + LAG) if b + LAG < B else None, tile(SC - 1, b))

        @block.sync
        def _(sp):
            sp.dma_start(masks_in[:], d["masks"]).then_inc(landed, 16)
            for n in range(2):
                sp.dma_start(tok[:, n], d["tok_rows"][n].partition_broadcast(P)).then_inc(landed, 16)
            sp.dma_start(gain8[:], d["ttt_rows"][0].partition_broadcast(P)).then_inc(landed, 16)
            sp.dma_start(eps[:], d["eps"]).then_inc(landed, 16)
            for free in (z_ps, qb_sb, y_sb_done, zg_sb, o_done):
                free.give(sp)

            def inner(t, b, sc):
                q = b % 2
                sp.dma_start(k_sb[q][:], rec[b, bass.ds(sc * P, P), :, 0:HD]).then_inc(in_sb[q].sem, 16)
                sp.dma_start(q_sb[q][:], q_in[b, bass.ds(sc * P, P)].rearrange("n (h e) -> n h e", h=NH)).then_inc(in_sb[q].sem, 16)
                sp.dma_start(w_sb[q][:], w_snap[bass.ds(sc, 1), b].rearrange("o p a e -> (o p) a e")).then_inc(in_sb[q].sem, 16)
                sp.dma_start(b_sb[q][:], b_snap[bass.ds(sc, 1), b]).then_inc(in_sb[q].sem, 16)
                sp.dma_start(steps_sb[q][:], grad[b, bass.ds(sc * P, P)]).then_inc(in_sb[q].sem, 16)

            def outer(t, b, sc):
                sp.dma_start(x_sb[b % 2][:], x_view[b, :, :, bass.ds(sc * P, P)]).then_inc(x_in_sb[b % 2].sem, 16)

            def both(one, other):
                count = one[0] + 1 if one else other[0] + LAG + 1
                if one:
                    sp.wait_ge(zg_sb.sem, count)
                if other:
                    sp.wait_ge(y_sb_done.sem, count)
                if one:
                    inner(*one)
                if other:
                    outer(*other)

            schedule(sp, both)

        @block.gpsimd
        def _(pool):
            v = nc.gpsimd
            pool.wait_ge(init, 1)

            def inner(t, b, sc):
                q = b % 2
                pool.wait_ge(in_sb[q].sem, 80 * (sc * 2 + b // 2) + 80)
                pool.wait_ge(o_done.sem, o_done.at(t, -1))
                v.tensor_tensor(qb[q][:], q_sb[q][:], T.shift[:].rearrange("p (h e) -> p h e", h=NH), ALU.add).then_inc(qb_sb.sem, 1)
                pool.wait_ge(zn_sb.sem, t + 1)
                v.tensor_tensor(zg[q][:], zn[q][:], gain8[:].rearrange("p (h e) -> p h e", h=NH), ALU.mult).then_inc(zg_sb.sem, 1)

            schedule(pool, lambda one, other: inner(*one) if one else None)

        @block.scalar
        def _(act):
            a = nc.scalar
            act.wait_ge(init, 1)

            def inner(t, b, sc):
                q = b % 2
                for n, (dst, src) in enumerate(((k_t, ps_kt), (q_t, ps_qt))):
                    act.wait_ge(turned_ps.sem, turned_ps.at(t, n + 1))
                    a.copy(dst[:], src[:]).then_inc(turned_sb.sem, 1)

            def norms(t, b, sc):
                q = b % 2
                act.wait_ge(ssq_sb.sem, t)
                for n in range(2):
                    act.wait_ge(z_ps.sem, z_ps.at(t, n + 1))
                    a.activation(zsq[:].rearrange("p (a n) e -> p a n e", n=2)[:, :, n], ps_z[n][:, :, 0:HD], ACT.Square
                                 ).then_inc(ssq_in.sem, 1)
                act.wait_ge(ssq_sb.sem, t + 1)
                act.wait_ge(rstd_sb.sem, t)
                a.activation(std[:], ssq[:], ACT.Sqrt, bias=eps[:, 0:1]).then_inc(std_sb.sem, 1)
                act.wait_ge(o_done.sem, o_done.at(t, 1))
                act.wait_ge(osq_sb.sem, t)
                a.activation(osq[:], o_sb[q][:], ACT.Square, accum_out=osum[q][:, 1:2]).then_inc(osq_sb.sem, 1)
                act.wait_ge(ovar_sb.sem, t + 1)
                a.activation(ovar[q][:], ovar[q][:], ACT.Sqrt, bias=eps[:, 1:2]).then_inc(ostd_sb.sem, 1)
                act.wait_ge(oshift_sb.sem, t + 1)
                a.activation(on[q][:], o_sb[q][:], ACT.Identity, bias=oshift[q][:], scale=orstd[q][:]).then_inc(on_sb.sem, 1)

            def outer(t, b, sc):
                q = b % 2
                act.wait_ge(ot_ps.sem, t + 1)
                a.copy(o_t[:], ps_ot[:]).then_inc(ot_sb.sem, 1)
                act.wait_ge(y_sb_done.sem, y_sb_done.at(t, 1))
                act.dma_start(o_view[b, :, :, bass.ds(sc * P, P)], y_sb[q][:]).then_inc(y_gone[q].sem, 16)

            def both(one, other):
                if one:
                    inner(*one)
                if other:
                    outer(*other)
                if one:
                    norms(*one)

            schedule(act, both)
            for q in range(2):
                act.wait_ge(y_gone[q].sem, 16 * SC * B // 2)

        @block.vector
        def _(dve):
            v = nc.vector
            dve.wait_ge(landed, 16 * loads)
            steps.then(dve, v.tensor_tensor(tok[:, 0], tok[:, 0], tok[:, 1], ALU.add))
            steps.then(dve, v.tensor_scalar(tok[:, 0], tok[:, 0], 0.0, -1.0 / 8, ALU.max, ALU.mult))
            steps.then(dve, v.tensor_tensor(mask[:], masks_in[:, 0], tok[:, 0], ALU.mult))
            steps.then(dve, v.scalar_tensor_tensor(mask[:], masks_in[:, 1], tok[:, 0, CS - 1:CS], mask[:], ALU.mult, ALU.add))
            steps.then(dve, v.tensor_scalar(gain8[:], gain8[:], 8.0, None, ALU.mult))
            steps.then(dve, v.memset(ones[:], 1.0))
            dve.sem_inc(init, 1)
            weigh_sb.give(dve)

            def inner(t, b, sc):
                q = b % 2
                wide_mask = mask[:].unsqueeze(1).broadcast_to([P, HP, P])
                for n in range(2):
                    dve.wait_ge(kq_ps.sem, kq_ps.at(t, n + 1))
                    dve.wait_ge(z_ps.sem, z_ps.at(t, n - 1))
                    v.scalar_tensor_tensor(weigh[n][:], ps_kq[n][:], 1.0, wide_mask, ALU.add, ALU.mult).then_inc(weigh_sb.sem, 1)

            def norms(t, b, sc):
                q = b % 2
                dve.wait_ge(ssq_in.sem, ssq_in.at(t, 2))
                dve.wait_ge(std_sb.sem, t)
                v.tensor_reduce(ssq[:], zsq[:], AX.X, ALU.add).then_inc(ssq_sb.sem, 1)
                dve.wait_ge(std_sb.sem, t + 1)
                v.reciprocal(rstd[:], std[:]).then_inc(rstd_sb.sem, 1)
                dve.wait_ge(rstd_sb.sem, t + 1)
                dve.wait_ge(zg_sb.sem, zg_sb.at(t, -1))
                for n in range(2):
                    last = v.tensor_tensor(zn[q][:].rearrange("p (a n) e -> p a n e", n=2)[:, :, n], ps_z[n][:, :, 0:HD],
                                           rstd[:].rearrange("p (a n) -> p a n", n=2)[:, :, n:n + 1].broadcast_to([P, HP, HD]), ALU.mult)
                last.then_inc(zn_sb.sem, 1)
                dve.wait_ge(zg_sb.sem, zg_sb.at(t, 1))
                dve.wait_ge(qb_sb.sem, qb_sb.at(t, 1))
                v.scalar_tensor_tensor(o_sb[q][:], zg[q][:].rearrange("p h e -> p (h e)"), 1.0,
                                       qb[q][:].rearrange("p h e -> p (h e)"), ALU.mult, ALU.add,
                                       accum_out=osum[q][:, 0:1]).then_inc(o_done.sem, 1)
                dve.wait_ge(o_done.sem, o_done.at(t, 1))
                v.tensor_scalar(nmean[q][:], osum[q][:, 0:1], -1.0 / C, None, ALU.mult).then_inc(small.sem, 1)
                dve.wait_ge(small.sem, small.at(t, 1))
                dve.wait_ge(osq_sb.sem, t + 1)
                v.tensor_tensor(ovar[q][:], nmean[q][:], nmean[q][:], ALU.mult).then_inc(small.sem, 1)
                dve.wait_ge(small.sem, small.at(t, 2))
                v.scalar_tensor_tensor(ovar[q][:], osum[q][:, 1:2], 1.0 / C, ovar[q][:], ALU.mult, ALU.subtract).then_inc(ovar_sb.sem, 1)
                dve.wait_ge(ostd_sb.sem, t + 1)
                v.reciprocal(orstd[q][:], ovar[q][:]).then_inc(orstd_sb.sem, 1)
                dve.wait_ge(orstd_sb.sem, t + 1)
                v.tensor_tensor(oshift[q][:], nmean[q][:], orstd[q][:], ALU.mult).then_inc(oshift_sb.sem, 1)

            def outer(t, b, sc):
                q = b % 2
                dve.wait_ge(y_ps.sem, t + 1)
                dve.wait_ge(x_in_sb[q].sem, 16 * (sc * 2 + b // 2) + 16)
                dve.wait_ge(y_gone[q].sem, 16 * (sc * 2 + b // 2))
                for n in range(CT):
                    last = v.scalar_tensor_tensor(y_sb[q][:, n], ps_y[:, n], T.wo_bias[:, n:n + 1], x_sb[q][:, n], ALU.add, ALU.add)
                last.then_inc(y_sb_done.sem, 1)

            def both(one, other):
                if one:
                    inner(*one)
                if other:
                    outer(*other)
                if one:
                    norms(*one)

            schedule(dve, both)

        @block.tensor
        def _(pe):
            pe.wait_ge(init, 1)

            def tile_turns(t, b, sc):
                q = b % 2
                pe.wait_ge(in_sb[q].sem, 80 * (sc * 2 + b // 2) + 80)
                pe.wait_ge(turned_sb.sem, turned_sb.at(t, 0))
                for a in range(HP):
                    last = pe.transpose(ps_kt[:, a], k_sb[q][:, 2 * a:2 * a + 2].rearrange("p h e -> p (h e)"), T.ident[:])
                last.then_inc(turned_ps.sem, 1)
                for a in range(HP):
                    last = pe.transpose(ps_qt[:, a], q_sb[q][:, 2 * a:2 * a + 2].rearrange("p h e -> p (h e)"), T.ident[:])
                last.then_inc(turned_ps.sem, 1)

            def tile_weights(t, b, sc):
                pe.wait_ge(turned_sb.sem, turned_sb.at(t, 2))
                for n in range(2):
                    rows = slice(64 * n, 64 * n + 64)
                    pe.wait_ge(weigh_sb.sem, weigh_sb.at(t, n - 1))
                    for a in range(HP):
                        last = pe.matmul(ps_kq[n][:, a], k_t[rows, a], q_t[rows, a], start=True, stop=True)
                    last.then_inc(kq_ps.sem, 1)

            def tile_outputs(t, b, sc):
                q = b % 2
                pe.wait_ge(zn_sb.sem, t)
                for n in range(2):
                    rows = slice(64 * n, 64 * n + 64)
                    out = ps_z[n][:, :, 0:HD]
                    pe.matmul(out, ones[:], b_sb[q][:].rearrange("p (a n) e -> p a n e", n=2)[:, :, n], start=True, stop=False,
                              skip_group_check=True)
                    pe.wait_ge(weigh_sb.sem, weigh_sb.at(t, n + 1))
                    for a in range(HP):
                        pe.matmul(out[:, a], weigh[n][:, a], steps_sb[q][:, 2 * a + n], start=False, stop=False, skip_group_check=True)
                    for a in range(HP):
                        last = pe.matmul(out[:, a], q_t[rows, a], w_sb[q][rows, a], start=False, stop=True, skip_group_check=True)
                    last.then_inc(z_ps.sem, 1)

            def tile_back(t, b, sc):
                q = b % 2
                pe.wait_ge(on_sb.sem, t + 1)
                pe.wait_ge(ot_sb.sem, t)
                for n in range(CT):
                    last = pe.transpose(ps_ot[:, n], on[q][:, n * P:(n + 1) * P], T.ident[:])
                last.then_inc(ot_ps.sem, 1)

            def tile_project(t, b, sc):
                pe.wait_ge(ot_sb.sem, t + 1)
                pe.wait_ge(y_sb_done.sem, y_sb_done.at(t, 0))
                for n in range(CT):
                    for ct in range(CT):
                        last = pe.matmul(ps_y[:, n], T.wo[:, ct, n * P:(n + 1) * P], o_t[:, ct], start=ct == 0, stop=ct == CT - 1)
                last.then_inc(y_ps.sem, 1)

            def both(one, other):
                if one:
                    tile_turns(*one)
                if other:
                    tile_back(*other)
                if one:
                    tile_weights(*one)
                if other:
                    tile_project(*other)
                if one:
                    tile_outputs(*one)

            schedule(pe, both)


def norm_factors(nc, name, gmean, grstd, gn, coef):
    with ExitStack() as ctx:
        steps = Steps(ctx, nc, f"{name}_steps")
        block = ctx.enter_context(nc.Block())

        @block.vector
        def _(dve):
            v = nc.vector
            steps.then(dve, v.tensor_copy(gn[:, :, 0], grstd[:]))
            steps.then(dve, v.scalar_tensor_tensor(gn[:, :, 1], gmean[:], -1.0, grstd[:], ALU.mult, ALU.mult))
            if coef is not None:
                steps.then(dve, v.tensor_copy(coef[:, :, 0], grstd[:]))
                steps.then(dve, v.tensor_scalar(coef[:, :, 1], gn[:, :, 1], 64.0, None, ALU.mult))
                steps.then(dve, v.memset(coef[:, :, 2], 1.0))
                steps.then(dve, v.memset(coef[:, :, 3], 0.0))


def gate_channels(nc, d, chan_stats, block_sums, gn, keep, rest, next_stats):
    HID = C // 16
    NBLK = 16
    with ExitStack() as ctx:
        def sb(n, shape):
            return ctx.enter_context(nc.sbuf_tensor(f"gating_{n}", shape, F32))

        w1 = sb("w1", [P, 3, 9])
        w2 = sb("w2", [P, 9])
        fc1 = sb("fc1", [P, CT, HID])
        fc2 = sb("fc2", [HID, C])
        by_scale = sb("by_scale", [P, 3, 4, 4])
        quads = sb("quads", [P, 2, 2])
        rows = sb("rows", [P, 2, 4])
        whole = sb("whole", [P, 1])
        weight = sb("weight", [P, NBLK])
        weight_sum = sb("weight_sum", [P, 1])
        terms = sb("terms", [P, UNITS, NBLK])
        z = sb("z", [P, UNITS])
        hid = sb("hid", [HID, B])
        gate = sb("gate", [P, B, CT])
        ps_hid = ctx.enter_context(nc.psum_tensor("gate_ps_hid", [HID, B], F32))
        ps_gate = ctx.enter_context(nc.psum_tensor("gate_ps_gate", [P, CT, B], F32))
        landed = ctx.enter_context(semaphore(nc, "gate_landed"))
        z_made = ctx.enter_context(semaphore(nc, "gate_z_made"))
        hid_ps = ctx.enter_context(semaphore(nc, "gate_hid_ps"))
        hid_sb = ctx.enter_context(semaphore(nc, "gate_hid_sb"))
        gate_ps = ctx.enter_context(semaphore(nc, "gate_gate_ps"))
        gate_sb = ctx.enter_context(semaphore(nc, "gate_gate_sb"))
        steps = Steps(ctx, nc, "gate_steps")
        block = ctx.enter_context(nc.Block())

        @block.sync
        def _(sp):
            sp.dma_start(w1[:], d["gate_w1"].partition_broadcast(P)).then_inc(landed, 16)
            sp.dma_start(w2[:], d["gate_w2"].partition_broadcast(P)).then_inc(landed, 16)
            sp.dma_start(fc1[:], d["fc1_wT"]).then_inc(landed, 16)
            sp.dma_start(fc2[:], d["fc2_wT"]).then_inc(landed, 16)

        @block.vector
        def _(dve):
            v = nc.vector

            def then(ins):
                steps.then(dve, ins)

            dve.wait_ge(landed, 64)
            then(v.memset(by_scale[:], 0.0))
            for i in range(2):
                for j in range(2):
                    tap = (i + 1) * 3 + j + 1
                    for s in range(3):
                        part = by_scale[:, s, i:i + 3, j:j + 3]
                        then(v.scalar_tensor_tensor(part, w1[:, s].rearrange("p (a b) -> p a b", b=3), w2[:, tap:tap + 1],
                                                    part, ALU.mult, ALU.add))
            then(v.tensor_reduce(whole[:], by_scale[:, 0].rearrange("p a b -> p (a b)"), AX.X, ALU.add))
            for q in range(2):
                then(v.tensor_tensor(rows[:, q], by_scale[:, 1, 2 * q], by_scale[:, 1, 2 * q + 1], ALU.add))
            then(v.tensor_tensor(quads[:], rows[:, :, 0:4:2], rows[:, :, 1:4:2], ALU.add))
            for q in range(2):
                for i in range(2):
                    then(v.scalar_tensor_tensor(weight[:, 8 * q + 4 * i:8 * q + 4 * i + 4].rearrange("p (a b) -> p a b", b=2),
                                                quads[:, q].unsqueeze(2).broadcast_to([P, 2, 2]), 0.25,
                                                by_scale[:, 2, 2 * q + i].rearrange("p (a b) -> p a b", b=2), ALU.mult, ALU.add))
            then(v.scalar_tensor_tensor(weight[:], whole[:].broadcast_to([P, NBLK]), 1.0 / NBLK, weight[:], ALU.mult, ALU.add))
            then(v.tensor_reduce(weight_sum[:], weight[:], AX.X, ALU.add))
            then(v.tensor_tensor(terms[:], block_sums[:], weight[:].unsqueeze(1).broadcast_to([P, UNITS, NBLK]), ALU.mult))
            then(v.tensor_reduce(z[:], terms[:], AX.X, ALU.add))
            then(v.scalar_tensor_tensor(z[:], z[:], 1.0 / 256, gn[:, :, 0], ALU.mult, ALU.mult))
            v.scalar_tensor_tensor(z[:], gn[:, :, 1], weight_sum[:, 0:1], z[:], ALU.mult, ALU.add).then_inc(z_made, 1)
            dve.wait_ge(hid_ps, 1)
            v.tensor_scalar(hid[:], ps_hid[:], 0.0, None, ALU.max).then_inc(hid_sb, 1)
            dve.wait_ge(gate_sb, 1)
            flat = gate[:].rearrange("p b k -> p (b k)")
            then(v.tensor_tensor(keep[:], flat, gn[:, :, 0], ALU.mult))
            then(v.tensor_scalar(keep[:], keep[:], 1.0, None, ALU.add))
            then(v.tensor_tensor(rest[:], flat, gn[:, :, 1], ALU.mult))
            then(v.tensor_tensor(next_stats[:, :, 0], keep[:], chan_stats[:, :, 0], ALU.mult))
            then(v.tensor_tensor(next_stats[:, :, 0], next_stats[:, :, 0], rest[:], ALU.add))
            then(v.tensor_tensor(next_stats[:, :, 1], keep[:], chan_stats[:, :, 1], ALU.mult))
            then(v.tensor_tensor(next_stats[:, :, 1], next_stats[:, :, 1], keep[:], ALU.mult))

        @block.tensor
        def _(pe):
            pe.wait_ge(landed, 64)
            pe.wait_ge(z_made, 1)
            for ct in range(CT):
                last = pe.matmul(ps_hid[:], fc1[:, ct], z[:, ct:UNITS:CT], start=ct == 0, stop=ct == CT - 1)
            last.then_inc(hid_ps, 1)
            pe.wait_ge(hid_sb, 1)
            for ct in range(CT):
                last = pe.matmul(ps_gate[:, ct], fc2[:, ct * P:(ct + 1) * P], hid[:], start=True, stop=True)
            last.then_inc(gate_ps, 1)

        @block.scalar
        def _(act):
            act.wait_ge(gate_ps, 1)
            nc.scalar.activation(gate[:].rearrange("p b k -> p k b"), ps_gate[:], ACT.Sigmoid).then_inc(gate_sb, 1)


def last_coefficients(nc, gmean, grstd, keep, rest, coef):
    with ExitStack() as ctx:
        off = ctx.enter_context(nc.sbuf_tensor("last_off", [P, UNITS], F32))
        steps = Steps(ctx, nc, "last_steps")
        block = ctx.enter_context(nc.Block())

        @block.vector
        def _(dve):
            v = nc.vector
            steps.then(dve, v.tensor_tensor(coef[:, :, 0], grstd[:], keep[:], ALU.mult))
            steps.then(dve, v.tensor_tensor(off[:], rest[:], gmean[:], ALU.subtract))
            steps.then(dve, v.scalar_tensor_tensor(coef[:, :, 1], off[:], 64.0, grstd[:], ALU.mult, ALU.mult))
            steps.then(dve, v.tensor_copy(coef[:, :, 2], keep[:]))
            steps.then(dve, v.tensor_scalar(coef[:, :, 3], rest[:], 64.0, None, ALU.mult))


def load_constants(nc, group_mean, d):
    with ExitStack() as ctx:
        landed = ctx.enter_context(semaphore(nc, "const_landed"))
        block = ctx.enter_context(nc.Block())

        @block.sync
        def _(sp):
            sp.dma_start(group_mean[:], d["group_mean"]).then_inc(landed, 16)
            sp.wait_ge(landed, 16)


class Projections:

    def __init__(self, ctx, nc):
        def sb(n, shape):
            return ctx.enter_context(nc.sbuf_tensor(f"proj_{n}_sb", shape, F32))

        self.w = sb("w", [P, 3, CT, C])
        self.wo = sb("wo", [P, CT, C])
        self.lrw = sb("lrw", [P, CT, NH + 1])
        self.gain = sb("gain", [P, C])
        self.shift = sb("shift", [P, C])
        self.wbias = sb("wbias", [P, 3, C])
        self.lrb = sb("lrb", [P, NH])
        self.wo_bias = sb("wo_bias", [P, CT])
        self.mean_col = sb("mean_col", [P, 1])
        self.ident = sb("ident", [P, P])


def network(nc, d, out):
    def dram(n, shape):
        return nc.dram_tensor(n, shape, F32, kind="Internal").ap()

    rec = dram("records", (B, TOK + 2 * CS, NH, RW))
    q = dram("queries", (B, TOK, C))
    grad = dram("gradients", (B, TOK, NH, HD))
    w_snap = dram("w_snapshots", (TOK // P, B, P, NH // 2, HD))
    b_snap = dram("b_snapshots", (TOK // P, B, NH, HD))
    x1 = dram("x1", (B, C, H, W))
    x2 = dram("x2", (B, C, H, W))
    with ExitStack() as ctx:
        def sb(n, shape):
            return ctx.enter_context(nc.sbuf_tensor(n, shape, F32))

        chan_stats = sb("chan_stats", [P, UNITS, 2])
        gn = sb("gn", [P, UNITS, 2])
        gmean = sb("gmean", [P, UNITS])
        grstd = sb("grstd", [P, UNITS])
        group_mean = sb("group_mean_sb", [P, P])
        coef = sb("coef", [P, UNITS, 4])
        load_constants(nc, group_mean, d)
        with ExitStack() as layer0:
            T = Projections(layer0, nc)
            channel_statistics(nc, "stats0", d["x"], chan_stats)
            group_norm(nc, "norm0", chan_stats, group_mean, 1e-5, gmean, grstd)
            norm_factors(nc, "factors0", gmean, grstd, gn, None)
            prepare_projections(nc, T, d)
            project(nc, T, d["x"], d["rope"], gn, rec, q)
            scan_chunks(nc, T, d, rec, grad, w_snap, b_snap)
            read_out(nc, T, d, d["x"], rec, q, grad, w_snap, b_snap, x1)
        block_sums = sb("block_sums", [P, UNITS, 16])
        keep = sb("keep", [P, UNITS])
        rest = sb("rest", [P, UNITS])
        next_stats = sb("next_stats", [P, UNITS, 2])
        channel_statistics(nc, "stats1", x1, chan_stats)
        group_norm(nc, "norm1", chan_stats, group_mean, 1e-5, gmean, grstd)
        norm_factors(nc, "factors1", gmean, grstd, gn, coef)
        fourier_layer(nc, "fourier1", x1, x2, d["f1_w"], d["f1_b"], d["dft"], coef, chan_stats, block_sums)
        group_norm(nc, "norm2", chan_stats, group_mean, 1e-5, gmean, grstd)
        norm_factors(nc, "factors2", gmean, grstd, gn, None)
        gate_channels(nc, d, chan_stats, block_sums, gn, keep, rest, next_stats)
        group_norm(nc, "norm3", next_stats, group_mean, 1e-5, gmean, grstd)
        last_coefficients(nc, gmean, grstd, keep, rest, coef)
        fourier_layer(nc, "fourier3", x2, out, d["f3_w"], d["f3_b"], d["dft"], coef, None, None)


def rope_table():
    inv = (1.0 / 10000.0 ** (np.arange(0, HD, 2, dtype=np.float32) / np.float32(HD))).astype(np.float32)
    angle = np.arange(TOK, dtype=np.float32)[:, None] * inv[None]
    return np.concatenate([np.cos(angle), -np.sin(angle), np.sin(angle)], 1).astype(np.float32)


def shape_constants():
    j = np.arange(P)
    chunk = j // CS
    same = (chunk[:, None] == chunk[None]) & (j[:, None] <= j[None])
    earlier = chunk[:, None] < chunk[None]
    ind = np.kron(np.eye(NH), np.ones((1, CS)))
    constants = {
        "dft": dft_matrices(),
        "rope": rope_table(),
        "group_mean": np.kron(np.eye(P // 16), np.full((16, 16), 1 / 16)),
        "masks": np.stack([same, earlier], 1),
        "place": np.tile(np.repeat(np.eye(2), CS, 0), (NH // 2, 1)),
        "ind": ind,
        "ind_t": ind.T,
        "tok_inv": np.tile(1.0 / np.arange(1, CS + 1, dtype=np.float32), NH),
        "eps": np.tile(np.array([[HD * 1e-6, 1e-6]]), (P, 1)),
    }
    return {n: a.astype(np.float32) for n, a in constants.items()}


def layout(i):
    def rows_of(w):
        return w.T.reshape(CT, P, w.shape[0]).transpose(1, 0, 2)

    def columns(v):
        return v.reshape(CT, P).T

    def fourier(n):
        w1, w2, b1, b2 = (i[f"{n}_conv_{k}"] for k in ("w1", "w2", "b1", "b2"))
        return (np.stack([w1[0], w1[1], w2[0], w2[1]], axis=2), np.stack([b1[0], b1[1], b2[0], b2[1]], axis=2))

    L0 = {k[8:]: i[k] for k in i if k.startswith("L0_conv_")}
    d = shape_constants()
    d["x"] = i["x"]
    d["wT"] = np.stack([rows_of(L0[n]) for n in ("q_w", "k_w", "v_w", "o_w")])
    d["lr_wT"] = rows_of(L0["lr_w"].reshape(NH, C))
    d["vecs"] = np.stack([columns(L0[n]) for n in ("ln_w", "ln_b", "post_w", "post_b")], 1)
    d["ttt_rows"] = np.stack([L0["ttt_ln_w"].reshape(-1), L0["ttt_ln_b"].reshape(-1)])
    d["lr_b_row"] = L0["lr_b"].reshape(-1)
    d["tok_rows"] = np.stack([d.pop("tok_inv"), np.tile(L0["tok_idx_delta"], NH)])
    d["gain_rows"] = np.repeat(L0["ttt_ln_w"], CS, 0)
    d["w0"] = L0["W1"].reshape(NH // 2, 2, HD, HD).transpose(1, 2, 0, 3).reshape(P, NH // 2, HD)
    d["b0"] = L0["b1"].reshape(NH, HD)
    d["f1_w"], d["f1_b"] = fourier("L1")
    d["f3_w"], d["f3_b"] = fourier("L3")
    d["gate_w1"] = i["L2_conv_w1"].reshape(3, 9)
    d["gate_w2"] = i["L2_conv_w2"].reshape(9)
    d["fc1_wT"] = rows_of(i["L2_conv_fc1_w"])
    d["fc2_wT"] = i["L2_conv_fc2_w"].T
    return {n: np.ascontiguousarray(a) for n, a in d.items()}


def kernel(**inputs):
    import concourse.bacc as bacc
    from concourse.bass_utils import run_bass_kernel_spmd

    arrays = layout({n: np.asarray(a) for n, a in inputs.items()})
    nc = bacc.Bacc("TRN2", target_bir_lowering=False, num_devices=1)
    d = {n: nc.dram_tensor(n, a.shape, F32, kind="ExternalInput").ap() for n, a in arrays.items()}
    out = nc.dram_tensor("out", (B, C, H, W), F32, kind="ExternalOutput").ap()
    network(nc, d, out)
    r = run_bass_kernel_spmd(nc, [arrays], core_ids=[0])
    return r.results[0]["out"]
```

```python
from contextlib import ExitStack, contextmanager

import numpy as np

import concourse.bass as bass
from concourse import mybir

F32 = mybir.dt.float32
ALU = mybir.AluOpType
ACT = mybir.ActivationFunctionType
AX = mybir.AxisListType

P = 128
B, C, H, W = 4, 512, 64, 64
TOK = H * W
CT = C // P
UNITS = B * CT
NH, HD, CS = 8, 64, 16
RW = 2 * HD + 4


def dft_matrices():
    k = np.arange(64)
    ang = 2 * np.pi * np.outer(k, k) / 64
    cos, sin = np.cos(ang) / 8, np.sin(ang) / 8
    rows = np.zeros((64, 32, 2))
    rows[:, :, 0], rows[:, :, 1] = cos[:, :32], -sin[:, :32]
    rows[:, 0, 1] = cos[:, 32]
    back = np.zeros((32, 2, 64))
    back[:, 0], back[:, 1] = 2 * cos[:32], -2 * sin[:32]
    back[0, 0], back[0, 1] = cos[0], cos[32]
    F1 = np.zeros((2, 64, 32, 2, 2))
    G1 = np.zeros((2, 32, 2, 2, 64))
    for r in range(2):
        F1[r, :, :, r, :] = rows
        G1[r, :, :, r, :] = back
    F2 = np.zeros((64, 2, 2, 64))
    F2[:, 0, 0], F2[:, 1, 0], F2[:, 0, 1], F2[:, 1, 1] = cos, sin, -sin, cos
    F2a, F2b = np.zeros_like(F2), np.zeros_like(F2)
    F2a[:, 0], F2b[:, 1] = F2[:, 0], F2[:, 0]
    G2 = np.zeros((2, 64, 64, 2))
    G2[0, :, :, 0], G2[1, :, :, 0], G2[0, :, :, 1], G2[1, :, :, 1] = cos, -sin, sin, cos
    G2a, G2b = np.zeros_like(G2), np.zeros_like(G2)
    G2a[..., 0], G2b[..., 1] = G2[..., 0], G2[..., 0]
    mats = [F1, F2, F2a, F2b, G2, G2a, G2b, G1, np.eye(128)]
    return np.stack([m.reshape(128, 128) for m in mats]).astype(np.float32)




@contextmanager
def semaphore(nc, name):
    sem = nc.alloc_semaphore(name=name)
    yield sem
    nc.gpsimd.sem_clear(sem)
    nc.release_semaphore(sem)
class Signal:

    def __init__(self, ctx, nc, name, per=1, credit=0):
        self.sem = ctx.enter_context(semaphore(nc, name))
        self.per, self.credit = per, credit + 1
        nc.sync.sem_inc(self.sem, self.credit)

    def at(self, step, n):
        return step * self.per + (n + self.credit)


def spectral_batches():
    packed, slots = [(0, 3)], [(0, 4)]
    while slots[-1][0] + slots[-1][1] < W // 2 + 1:
        s = slots[-1][0] + slots[-1][1]
        n = min(4, W // 2 + 1 - s)
        packed.append((s - 1, n))
        slots.append((s, n))
    return packed, slots


def fourier_layer(nc, name, x_in, x_out, weights, biases, dft, coef, chan_stats, block_sums, units_outer=B):
    x_view = x_in.rearrange("b (k c) h w -> (b k) c (h w)", c=P)
    o_view = x_out.rearrange("b (k c) h w -> (b k) c (h w)", c=P)
    packed, slots = spectral_batches()
    NB1 = TOK // 512
    NB2 = len(slots)
    NT = 2 * (NB1 + NB2)
    chunks = [(0, 7), (7, 14), (14, 21), (21, 27), (27, 33)]
    NCH = len(chunks)
    CW = 7 * H

    with ExitStack() as ctx:
        def sb(n, shape):
            return ctx.enter_context(nc.sbuf_tensor(f"{name}_{n}", shape, F32))

        def ps(n, shape):
            return ctx.enter_context(nc.psum_tensor(f"{name}_{n}", shape, F32))

        def sig(n, per=1, credit=0):
            return Signal(ctx, nc, f"{name}_{n}", per, credit)

        xb = [sb(f"x{k}", [P, TOK]) for k in range(2)]
        wt = [sb(f"weights{k}", [P, 4, P]) for k in range(2)]
        wneg = [sb(f"weights_neg{k}", [P, 2, P]) for k in range(2)]
        bias = [sb(f"bias{k}", [P, 4]) for k in range(2)]
        half = sb("half", [P, TOK])
        spec = sb("spec", [P, W // 2 + 1, 2, H])
        turned = [sb(f"turned{k}", [P, 512]) for k in range(2)]
        hidden = [sb(f"hidden{k}", [P, 2, CW]) for k in range(2)]
        prod = [sb(f"prod{k}", [P, 4, CW]) for k in range(2)]
        mats = sb("mats", [P, 9, P])
        ident = sb("ident", [P, P])
        stats6 = sb("stats6", [P, UNITS + 1, NB1 * 6])
        blocks = sb("blocks", [P, UNITS + 1, 16])
        zeros = sb("zeros", [P, 2, P])
        rowsum = sb("rowsum", [P, H * 4])
        psT = [ps(f"psT{k}", [P, 512]) for k in range(2)]
        psD = [ps(f"psD{k}", [P, 512]) for k in range(2)]
        psA = [ps(f"psA{k}", [P, 512]) for k in range(2)]
        psB = [ps(f"psB{k}", [P, 512]) for k in range(2)]

        const_in = sig("const_in")
        x_loaded = [sig(f"x_loaded{k}", 16) for k in range(2)]
        w_loaded = [sig(f"w_loaded{k}", 32) for k in range(2)]
        x_stored = [sig(f"x_stored{k}", 16) for k in range(2)]
        neg_made = sig("neg_made", 1)
        turned_ps = sig("turned_ps", NT)
        turned_sb = sig("turned_sb", NT, credit=2)
        dft_ps = sig("dft_ps", NT, credit=2)
        dft_sb = sig("dft_sb", NT, credit=2 * NT)
        dc_added = sig("dc_added", 1)
        mix1_ps = sig("mix1_ps", 2 * NCH)
        hidden_sb = sig("hidden_sb", 2 * NCH)
        mix2_ps = sig("mix2_ps", 2 * NCH)
        terms_sb = sig("terms_sb", NCH)
        prod_sb = sig("prod_sb", NCH, credit=2)
        rest_added = sig("rest_added", 1)
        rows_summed = sig("rows_summed", NB1)
        cleared = sig("cleared")
        zeroed = sig("zeroed")
        stat_done = sig("stat_done", NB1 + 1)

        F1, F2, F2a, F2b, G2, G2a, G2b, G1 = (mats[:, n, :] for n in range(8))
        block = ctx.enter_context(nc.Block())

        def loop(eng, body):
            with eng.Fori(0, units_outer) as b:
                with eng.Fori(0, 2) as pair:
                    for k in range(2):
                        body(b * 4 + pair * 2 + k, b * 2 + pair, k, pair * 2 + k)

        @block.sync
        def _(sp):
            sp.dma_start(mats[:, 0:8, :], dft.rearrange("n p m -> p n m")[:, 0:8, :]).then_inc(const_in.sem, 16)
            sp.dma_start(ident[:], dft[8]).then_inc(const_in.sem, 16)

            def unit(u, it, k, ct):
                sp.wait_ge(x_stored[k].sem, x_stored[k].at(it, 0))
                if chan_stats is not None:
                    sp.wait_ge(stat_done.sem, stat_done.at(u, 0))
                sp.wait_ge(dft_sb.sem, dft_sb.at(u, -NT))
                sp.dma_start(xb[k][:], x_view[bass.ds(u, 1)].rearrange("o c n -> (o c) n")).then_inc(x_loaded[k].sem, 16)
                sp.dma_start(wt[k][:], weights[bass.ds(ct, 1)].rearrange("q i r o -> (q i) r o")).then_inc(w_loaded[k].sem, 16)
                sp.dma_start(bias[k][:], biases[bass.ds(ct, 1)].rearrange("q c r -> (q c) r")).then_inc(w_loaded[k].sem, 16)

            def store(u, k):
                sp.wait_ge(dft_sb.sem, dft_sb.at(u, NT))
                sp.dma_start(o_view[bass.ds(u, 1)].rearrange("o c n -> (o c) n"), xb[k][:]).then_inc(x_stored[k].sem, 16)

            for u in range(CT):
                unit(u, u // 2, u % 2, u)
                if u:
                    store(u - 1, 1 - u % 2)
            if units_outer > 1:
                with sp.Fori(1, units_outer) as b:
                    with sp.Fori(0, 2) as pair:
                        for k in range(2):
                            u = b * CT + pair * 2 + k
                            unit(u, b * 2 + pair, k, pair * 2 + k)
                            store(u - 1, 1 - k)
            store(units_outer * CT - 1, 1)
            for k in range(2):
                sp.wait_ge(x_stored[k].sem, x_stored[k].at(2 * units_outer, 0))

        @block.gpsimd
        def _(pool):
            def unit(u, it, k, ct):
                pool.wait_ge(w_loaded[k].sem, w_loaded[k].at(it, 32))
                nc.gpsimd.tensor_tensor(wneg[k][:], zeros[:], wt[k][:, 1:4:2, :], ALU.subtract).then_inc(neg_made.sem, 1)
                for c, (s0, s1) in enumerate(chunks):
                    n = (s1 - s0) * H
                    q = (k * NCH + c) % 2
                    pool.wait_ge(terms_sb.sem, terms_sb.at(u, c + 1))
                    re = spec[:, s0:s1, 0, :]
                    im = spec[:, s0:s1, 1, :]
                    pv = prod[q][:, :, 0:n].rearrange("p t (s h) -> p t s h", h=H)
                    nc.gpsimd.tensor_tensor(re, pv[:, 0], pv[:, 1], ALU.subtract)
                    nc.gpsimd.tensor_tensor(im, pv[:, 2], pv[:, 3], ALU.add).then_inc(prod_sb.sem, 1)
            nc.gpsimd.memset(zeros[:], 0.0).then_inc(zeroed.sem, 1)
            pool.wait_ge(zeroed.sem, zeroed.at(0, 1))
            loop(pool, unit)

        @block.scalar
        def _(act):
            def evacuate(u, t, width=512):
                act.wait_ge(turned_ps.sem, turned_ps.at(u, t + 1))
                act.wait_ge(dft_ps.sem, dft_ps.at(u, t - 1))
                nc.scalar.copy(turned[t % 2][:, 0:width], psT[t % 2][:, 0:width]).then_inc(turned_sb.sem, 1)

            def unit(u, it, k, ct):
                for t in range(NB1):
                    evacuate(u, t)
                for n in range(NB2):
                    evacuate(u, NB1 + n, packed[n][1] * P)
                for c, (s0, s1) in enumerate(chunks):
                    n = (s1 - s0) * H
                    q = (k * NCH + c) % 2
                    if c >= 2:
                        act.wait_ge(mix2_ps.sem, mix2_ps.at(u, 2 * (c - 1)))
                    for r in range(2):
                        act.wait_ge(mix1_ps.sem, mix1_ps.at(u, 2 * c + r + 1))
                        nc.scalar.activation(hidden[q][:, r, 0:n], psA[r][:, 0:n], ACT.Relu,
                                             bias=bias[k][:, r:r + 1]).then_inc(hidden_sb.sem, 1)
                for n in range(NB2):
                    evacuate(u, NB1 + NB2 + n, slots[n][1] * P)
                for t in range(NB1):
                    evacuate(u, NB1 + 2 * NB2 + t)
            loop(act, unit)

        @block.vector
        def _(dve):
            def moments_of_last(u, q, n):
                nc.vector.bn_stats(stats6[:, bass.ds(u, 1), 6 * n:6 * n + 6].rearrange("p o e -> p (o e)"),
                                   xb[q][:, 512 * n:512 * n + 512]).then_inc(stat_done.sem, 1)

            def row_sums_of_last(u, q, n):
                if n == 0:
                    dve.wait_ge(stat_done.sem, stat_done.at(u, 0))
                nc.vector.tensor_reduce(rowsum[:, 32 * n:32 * n + 32],
                                        xb[q][:, 512 * n:512 * n + 512].rearrange("p (a w) -> p a w", w=16),
                                        AX.X, ALU.add).then_inc(rows_summed.sem, 1)

            def block_sums_of_last(u):
                dve.wait_ge(rows_summed.sem, rows_summed.at(u, NB1))
                nc.vector.tensor_reduce(blocks[:, bass.ds(u, 1), :].rearrange("p o (a b) -> p (o a) b", b=4),
                                        rowsum[:, :].rearrange("p (a h b) -> p a b h", a=4, b=4),
                                        AX.X, ALU.add).then_inc(stat_done.sem, 1)

            def unit(u, it, k, ct):
                cf = coef[:, bass.ds(u, 1), :].rearrange("p o e -> p (o e)")
                if chan_stats is not None:
                    dve.wait_ge(dft_sb.sem, dft_sb.at(u, 0))
                for t in range(NB1):
                    dve.wait_ge(dft_ps.sem, dft_ps.at(u, t + 1))
                    dst = half[:, :].rearrange("p (w j e) -> p w j e", w=32, e=4)[:, :, 4 * t:4 * t + 4, :]
                    nc.vector.tensor_scalar(dst, psD[t % 2][:, :].rearrange("p (j w e) -> p w j e", j=4, e=4),
                                            cf[:, 0:1], None, ALU.mult).then_inc(dft_sb.sem, 1)
                    if chan_stats is not None:
                        moments_of_last(u, 1 - k, t)
                for n, (s, m) in enumerate(slots):
                    t = NB1 + n
                    dve.wait_ge(dft_ps.sem, dft_ps.at(u, t + 1))
                    nc.vector.tensor_copy(spec[:, s:s + m].rearrange("p s r h -> p (s r h)"),
                                          psD[t % 2][:, 0:m * P]).then_inc(dft_sb.sem, 1)
                    if chan_stats is not None and n < NB1:
                        row_sums_of_last(u, 1 - k, n)
                        if n == NB1 - 1:
                            block_sums_of_last(u)
                    if n == 0:
                        dve.wait_ge(dft_sb.sem, dft_sb.at(u, t + 1))
                        nc.vector.tensor_tensor(spec[:, 0, 0, 0:1], spec[:, 0, 0, 0:1], cf[:, 1:2],
                                                ALU.add).then_inc(dc_added.sem, 1)
                for c, (s0, s1) in enumerate(chunks):
                    n = (s1 - s0) * H
                    q = (k * NCH + c) % 2
                    dve.wait_ge(prod_sb.sem, prod_sb.at(u, c - 1))
                    re = spec[:, s0:s1, 0, :]
                    im = spec[:, s0:s1, 1, :]
                    if c == 0:
                        dve.wait_ge(dc_added.sem, dc_added.at(u, 1))
                        dve.wait_ge(dft_sb.sem, dft_sb.at(u, NB1 + NB2))
                    for r, (b0, b1_) in enumerate(((re, im), (im, re))):
                        dve.wait_ge(mix2_ps.sem, mix2_ps.at(u, 2 * c + r + 1))
                        src = psB[r][:, 0:n].rearrange("p (s h) -> p s h", h=H)
                        for term, with_ in ((0, re), (3, im)) if r == 0 else ((1, im), (2, re)):
                            last = nc.vector.scalar_tensor_tensor(
                                prod[q][:, term, 0:n].rearrange("p (s h) -> p s h", h=H), src,
                                bias[k][:, 2 + r:3 + r], with_, ALU.add, ALU.mult)
                    last.then_inc(terms_sb.sem, 1)
                    if c == 0:
                        dve.wait_ge(prod_sb.sem, prod_sb.at(u, c + 1))
                        nc.vector.tensor_tensor(spec[:, 0, 0, 0:1], spec[:, 0, 0, 0:1], cf[:, 3:4],
                                                ALU.add).then_inc(rest_added.sem, 1)
                for n, (p0, m) in enumerate(packed):
                    t = NB1 + NB2 + n
                    dve.wait_ge(dft_ps.sem, dft_ps.at(u, t + 1))
                    dst = half[:, :].rearrange("p (h w e) -> p h w e", h=H, e=2)[:, :, p0:p0 + m, :]
                    nc.vector.tensor_copy(dst, psD[t % 2][:, 0:m * P].rearrange("p (w h e) -> p h w e", h=H, e=2)
                                          ).then_inc(dft_sb.sem, 1)
                for n in range(NB1):
                    t = NB1 + 2 * NB2 + n
                    dve.wait_ge(dft_ps.sem, dft_ps.at(u, t + 1))
                    part = xb[k][:, 512 * n:512 * n + 512]
                    nc.vector.scalar_tensor_tensor(part, part, cf[:, 2:3], psD[t % 2][:, :],
                                                   ALU.mult, ALU.add).then_inc(dft_sb.sem, 1)
            dve.wait_ge(const_in.sem, const_in.at(0, 32))
            if chan_stats is not None:
                nc.vector.memset(xb[1][:], 0.0).then_inc(cleared.sem, 1)
                dve.wait_ge(cleared.sem, cleared.at(0, 1))
            loop(dve, unit)
            if chan_stats is not None:
                units = units_outer * CT
                dve.wait_ge(dft_sb.sem, dft_sb.at(units, 0))
                for n in range(NB1):
                    moments_of_last(units, 1, n)
                for n in range(NB1):
                    row_sums_of_last(units, 1, n)
                block_sums_of_last(units)
                dve.wait_ge(stat_done.sem, stat_done.at(units + 1, 0))
                nc.vector.tensor_copy(block_sums[:, 0:units], blocks[:, 1:units + 1])
                for u in range(units):
                    nc.vector.bn_aggr(chan_stats[:, u, :], stats6[:, u + 1, :])

        @block.tensor
        def _(pe):
            def transposes(u, t, blocks):
                pe.wait_ge(turned_sb.sem, turned_sb.at(u, t - 1))
                for j, src in enumerate(blocks):
                    last = pe.transpose(psT[t % 2][:, j * P:(j + 1) * P], src, ident[:])
                last.then_inc(turned_ps.sem, 1)

            def transforms(u, t, products):
                pe.wait_ge(turned_sb.sem, turned_sb.at(u, t + 1))
                pe.wait_ge(dft_sb.sem, dft_sb.at(u, t - 1))
                for col, width, terms in products:
                    for n, (j, mat) in enumerate(terms):
                        last = pe.matmul(psD[t % 2][:, col:col + width], turned[t % 2][:, j * P:(j + 1) * P], mat,
                                         start=n == 0, stop=n == len(terms) - 1)
                last.then_inc(dft_ps.sem, 1)

            def stage(u, t0, turns, trans):
                turns[0]()
                for n in range(len(turns)):
                    if n + 1 < len(turns):
                        turns[n + 1]()
                    trans[n]()

            def unit(u, it, k, ct):
                pe.wait_ge(x_loaded[k].sem, x_loaded[k].at(it, 16))
                stage(u, 0,
                      [lambda n=n: transposes(u, n, [xb[k][:, (4 * n + j) * P:(4 * n + j + 1) * P] for j in range(4)])
                       for n in range(NB1)],
                      [lambda n=n: transforms(u, n, [(j * P, P, [(j, F1)]) for j in range(4)]) for n in range(NB1)])
                pe.wait_ge(dft_sb.sem, dft_sb.at(u, NB1))
                t0 = NB1
                stage(u, t0,
                      [lambda n=n, p0=p0, m=m: transposes(u, t0 + n, [half[:, (p0 + j) * P:(p0 + j + 1) * P] for j in range(m)])
                       for n, (p0, m) in enumerate(packed)],
                      [lambda n=n, m=m: transforms(u, t0 + n, ([(0, P, [(0, F2a)]), (P, P, [(0, F2b)])] +
                                                          [(j * P + P, P, [(j, F2)]) for j in range(1, m)]) if n == 0 else
                                              [(j * P, P, [(j, F2)]) for j in range(m)])
                       for n, (p0, m) in enumerate(packed)])
                pe.wait_ge(w_loaded[k].sem, w_loaded[k].at(it, 32))
                pe.wait_ge(neg_made.sem, neg_made.at(u, 1))

                def mix1(c):
                    s0, s1 = chunks[c]
                    n = (s1 - s0) * H
                    re = spec[:, s0:s1, 0, :]
                    im = spec[:, s0:s1, 1, :]
                    if c == 0:
                        pe.wait_ge(dc_added.sem, dc_added.at(u, 1))
                    pe.wait_ge(dft_sb.sem, dft_sb.at(u, NB1 + min(NB2, -(-s1 // 4))))
                    for r, (wa, wb) in enumerate(((wt[k][:, 0], wneg[k][:, 0]), (wt[k][:, 1], wt[k][:, 0]))):
                        if c:
                            pe.wait_ge(hidden_sb.sem, hidden_sb.at(u, 2 * c - 1 + r))
                        pe.matmul(psA[r][:, 0:n], wa, re, start=True, stop=False)
                        pe.matmul(psA[r][:, 0:n], wb, im, start=False, stop=True).then_inc(mix1_ps.sem, 1)

                def mix2(c):
                    s0, s1 = chunks[c]
                    n = (s1 - s0) * H
                    q = (k * NCH + c) % 2
                    pe.wait_ge(hidden_sb.sem, hidden_sb.at(u, 2 * c + 2))
                    if c:
                        pe.wait_ge(terms_sb.sem, terms_sb.at(u, c))
                    for r, (wa, wb) in enumerate(((wt[k][:, 2], wneg[k][:, 1]), (wt[k][:, 3], wt[k][:, 2]))):
                        pe.matmul(psB[r][:, 0:n], wa, hidden[q][:, 0, 0:n], start=True, stop=False)
                        pe.matmul(psB[r][:, 0:n], wb, hidden[q][:, 1, 0:n], start=False, stop=True).then_inc(mix2_ps.sem, 1)

                mix1(0)
                for c in range(NCH):
                    if c + 1 < NCH:
                        mix1(c + 1)
                    mix2(c)

                t1 = NB1 + NB2

                def turn_back(n):
                    s, m = slots[n]
                    chunk = next(c for c, (a, b) in enumerate(chunks) if s + m <= b)
                    if n == 0:
                        pe.wait_ge(rest_added.sem, rest_added.at(u, 1))
                    pe.wait_ge(prod_sb.sem, prod_sb.at(u, chunk + 1))
                    transposes(u, t1 + n, [spec[:, s + j].rearrange("p r h -> p (r h)") for j in range(m)])

                stage(u, t1,
                      [lambda n=n: turn_back(n) for n in range(NB2)],
                      [lambda n=n: transforms(u, t1 + n, ([(0, P, [(0, G2a), (1, G2b)])] +
                                                          [(j * P - P, P, [(j, G2)]) for j in range(2, 4)]) if n == 0 else
                                              [(j * P, P, [(j, G2)]) for j in range(slots[n][1])])
                       for n in range(NB2)])
                pe.wait_ge(dft_sb.sem, dft_sb.at(u, NB1 + 2 * NB2))
                t2 = NB1 + 2 * NB2
                stage(u, t2,
                      [lambda n=n: transposes(u, t2 + n, [half[:, (4 * n + j) * P:(4 * n + j + 1) * P] for j in range(4)])
                       for n in range(NB1)],
                      [lambda n=n: transforms(u, t2 + n, [(j * P, P, [(j, G1)]) for j in range(4)]) for n in range(NB1)])

            pe.wait_ge(const_in.sem, const_in.at(0, 32))
            loop(pe, unit)


class Steps:

    def __init__(self, ctx, nc, name):
        self.sem = ctx.enter_context(semaphore(nc, name))
        self.count = 0

    def then(self, eng, ins):
        self.count += 1
        ins.then_inc(self.sem, 1)
        eng.wait_ge(self.sem, self.count)


def channel_statistics(nc, name, x_in, chan_stats):
    x_view = x_in.rearrange("b (k c) h w -> (b k) c (h w)", c=P)
    parts = TOK // 512
    with ExitStack() as ctx:
        xb = [ctx.enter_context(nc.sbuf_tensor(f"{name}_x{k}", [P, TOK], F32)) for k in range(2)]
        stats6 = ctx.enter_context(nc.sbuf_tensor(f"{name}_s", [P, UNITS, parts * 6], F32))
        loaded = [Signal(ctx, nc, f"{name}_loaded{k}", 16) for k in range(2)]
        read = [Signal(ctx, nc, f"{name}_read{k}", credit=1) for k in range(2)]
        block = ctx.enter_context(nc.Block())

        @block.sync
        def _(sp):
            with sp.Fori(0, UNITS // 2) as it:
                for k in range(2):
                    sp.wait_ge(read[k].sem, read[k].at(it, 0))
                    sp.dma_start(xb[k][:], x_view[bass.ds(it * 2 + k, 1)].rearrange("o c n -> (o c) n")).then_inc(loaded[k].sem, 16)

        @block.vector
        def _(dve):
            with dve.Fori(0, UNITS // 2) as it:
                for k in range(2):
                    dve.wait_ge(loaded[k].sem, loaded[k].at(it, 16))
                    for n in range(parts):
                        last = nc.vector.bn_stats(stats6[:, bass.ds(it * 2 + k, 1), 6 * n:6 * n + 6].rearrange("p o e -> p (o e)"),
                                                  xb[k][:, 512 * n:512 * n + 512])
                    last.then_inc(read[k].sem, 1)
            for k in range(2):
                dve.wait_ge(read[k].sem, read[k].at(UNITS // 2, 0))
            for u in range(UNITS):
                nc.vector.bn_aggr(chan_stats[:, u, :], stats6[:, u, :])


def group_norm(nc, name, chan_stats, group_mean, eps, gmean, grstd):
    with ExitStack() as ctx:
        moments = ctx.enter_context(nc.sbuf_tensor(f"{name}_moments", [P, 2, UNITS], F32))
        var = ctx.enter_context(nc.sbuf_tensor(f"{name}_var", [P, UNITS], F32))
        ps = ctx.enter_context(nc.psum_tensor(f"{name}_ps", [P, 2, UNITS], F32))
        made = ctx.enter_context(semaphore(nc, f"{name}_moments_made"))
        averaged = ctx.enter_context(semaphore(nc, f"{name}_averaged"))
        var_made = ctx.enter_context(semaphore(nc, f"{name}_var_made"))
        std_made = ctx.enter_context(semaphore(nc, f"{name}_std_made"))
        steps = Steps(ctx, nc, f"{name}_steps")
        block = ctx.enter_context(nc.Block())
        mean, cvar = chan_stats[:, :, 0], chan_stats[:, :, 1]

        @block.vector
        def _(dve):
            steps.then(dve, nc.vector.tensor_tensor(moments[:, 1, :], mean, mean, ALU.mult))
            steps.then(dve, nc.vector.tensor_tensor(moments[:, 1, :], moments[:, 1, :], cvar, ALU.add))
            nc.vector.tensor_copy(moments[:, 0, :], mean).then_inc(made, 1)
            dve.wait_ge(averaged, 1)
            steps.then(dve, nc.vector.tensor_copy(gmean[:], ps[:, 0, :]))
            steps.then(dve, nc.vector.tensor_tensor(var[:], gmean[:], gmean[:], ALU.mult))
            steps.then(dve, nc.vector.tensor_tensor(var[:], ps[:, 1, :], var[:], ALU.subtract))
            nc.vector.tensor_scalar(var[:], var[:], 0.0, eps, ALU.max, ALU.add).then_inc(var_made, 1)
            dve.wait_ge(std_made, 1)
            steps.then(dve, nc.vector.reciprocal(grstd[:], var[:]))

        @block.scalar
        def _(act):
            act.wait_ge(var_made, 1)
            nc.scalar.activation(var[:], var[:], ACT.Sqrt).then_inc(std_made, 1)

        @block.tensor
        def _(pe):
            pe.wait_ge(made, 1)
            pe.matmul(ps[:].rearrange("p a b -> p (a b)"), group_mean[:], moments[:].rearrange("p a b -> p (a b)"),
                      start=True, stop=True).then_inc(averaged, 1)


def prepare_projections(nc, T, d):
    with ExitStack() as ctx:
        vecs = ctx.enter_context(nc.sbuf_tensor("prep_vecs", [P, 4, CT], F32))
        lnb = ctx.enter_context(nc.sbuf_tensor("prep_lnb", [P, CT, P], F32))
        mean_mat = ctx.enter_context(nc.sbuf_tensor("prep_mean", [P, P], F32))
        lr_b = ctx.enter_context(nc.sbuf_tensor("prep_lr_b", [P, NH], F32))
        ps = [ctx.enter_context(nc.psum_tensor(f"prep_ps{n}", [P, 512], F32)) for n in range(5)]
        landed = ctx.enter_context(semaphore(nc, "prep_landed"))
        ready = ctx.enter_context(semaphore(nc, "prep_lnb_ready"))
        biases = ctx.enter_context(semaphore(nc, "prep_biases"))
        scaled = ctx.enter_context(semaphore(nc, "prep_scaled"))
        means = ctx.enter_context(semaphore(nc, "prep_means"))
        steps = Steps(ctx, nc, "prep_steps")
        block = ctx.enter_context(nc.Block())
        loads = 10

        @block.sync
        def _(sp):
            def load(dst, src):
                sp.dma_start(dst, src).then_inc(landed, 16)
            for n in range(3):
                load(T.w[:, n], d["wT"][n])
            load(T.wo[:], d["wT"][3])
            load(T.lrw[:, :, 0:NH], d["lr_wT"])
            load(vecs[:], d["vecs"])
            load(T.gain[:], d["ttt_rows"][0].partition_broadcast(P))
            load(T.shift[:], d["ttt_rows"][1].partition_broadcast(P))
            load(lr_b[:], d["lr_b_row"].partition_broadcast(P))
            load(T.ident[:], d["dft"][8])

        @block.vector
        def _(dve):
            v = nc.vector
            dve.wait_ge(landed, 16 * loads)
            steps.then(dve, v.memset(lnb[:], 1.0))
            steps.then(dve, v.memset(mean_mat[:], 1.0 / C))
            steps.then(dve, v.memset(T.mean_col[:], 1.0 / C))
            steps.then(dve, v.memset(T.lrw[:, :, NH:NH + 1], 1.0 / C))
            for ct in range(CT):
                last = v.tensor_scalar(lnb[:, ct], lnb[:, ct], vecs[:, 1, ct:ct + 1], None, ALU.mult)
            last.then_inc(ready, 1)
            dve.wait_ge(biases, 1)
            for n in range(2):
                steps.then(dve, v.tensor_copy(T.wbias[:, n], ps[n][:]))
            steps.then(dve, v.tensor_tensor(T.wbias[:, 2], T.shift[:], ps[2][:], ALU.subtract))
            steps.then(dve, v.tensor_tensor(T.wbias[:, 2], T.wbias[:, 2], T.gain[:], ALU.mult))
            steps.then(dve, v.tensor_tensor(T.lrb[:], ps[3][:, 0:NH], lr_b[:], ALU.add))
            steps.then(dve, v.tensor_copy(T.wo_bias[:], ps[4][:, 0:CT]))
            for ct in range(CT):
                for n in range(3):
                    steps.then(dve, v.tensor_scalar(T.w[:, n, ct], T.w[:, n, ct], vecs[:, 0, ct:ct + 1], None, ALU.mult))
                steps.then(dve, v.scalar_tensor_tensor(T.w[:, 2, ct], T.w[:, 2, ct], -1.0, T.gain[:], ALU.mult, ALU.mult))
                steps.then(dve, v.tensor_scalar(T.wo[:, ct], T.wo[:, ct], vecs[:, 2, ct:ct + 1], None, ALU.mult))
                steps.then(dve, v.tensor_scalar(T.lrw[:, ct, 0:NH], T.lrw[:, ct, 0:NH], vecs[:, 0, ct:ct + 1], None, ALU.mult))
            dve.sem_inc(scaled, 1)
            dve.wait_ge(means, 1)
            for ct in range(CT):
                for n in range(3):
                    steps.then(dve, v.tensor_tensor(T.w[:, n, ct], T.w[:, n, ct], ps[n][:], ALU.subtract))
                steps.then(dve, v.tensor_tensor(T.lrw[:, ct, 0:NH], T.lrw[:, ct, 0:NH], ps[3][:, 0:NH], ALU.subtract))

        @block.tensor
        def _(pe):
            pe.wait_ge(landed, 16 * loads)
            pe.wait_ge(ready, 1)
            for ct in range(CT):
                for n in range(3):
                    pe.matmul(ps[n][:], lnb[:, ct], T.w[:, n, ct], start=ct == 0, stop=ct == CT - 1)
                pe.matmul(ps[3][:, 0:NH], lnb[:, ct], T.lrw[:, ct, 0:NH], start=ct == 0, stop=ct == CT - 1)
            for ot in range(CT):
                for ct in range(CT):
                    last = pe.matmul(ps[4][:, ot:ot + 1], T.wo[:, ct, ot * P:(ot + 1) * P], vecs[:, 3, ct:ct + 1],
                                     start=ct == 0, stop=ct == CT - 1)
            last.then_inc(biases, 1)
            pe.wait_ge(scaled, 1)
            for ct in range(CT):
                for n in range(3):
                    pe.matmul(ps[n][:], mean_mat[:], T.w[:, n, ct], start=ct == 0, stop=ct == CT - 1)
                last = pe.matmul(ps[3][:, 0:NH], mean_mat[:], T.lrw[:, ct, 0:NH], start=ct == 0, stop=ct == CT - 1)
            last.then_inc(means, 1)


def project(nc, T, x_in, rope, gn, rec, q_out, images=B, groups=TOK // 512):
    x_view = x_in.rearrange("b (k c) h w -> b c k (h w)", c=P)
    SUB = 4
    with ExitStack() as ctx:
        def sb(n, shape):
            return ctx.enter_context(nc.sbuf_tensor(f"proj_{n}", shape, F32))

        def sig(n, per=1, credit=0):
            return Signal(ctx, nc, f"proj_{n}", per, credit)

        h = [sb(f"h{k}", [P, CT, 512]) for k in range(2)]
        table = [sb(f"rope{k}", [P, SUB, 96]) for k in range(2)]
        gn_steps = sb("gn_steps", [P, images * groups, CT, 2])
        gn_now = [sb(f"gn_now{k}", [P, CT, 2]) for k in range(2)]
        sq = sb("sq", [P, CT, 512])
        st = sb("st", [P, SUB, NH + 2])
        small = sb("small", [P, 4, SUB])
        lr = sb("lr", [P, SUB, NH])
        rate = [sb(f"rate{k}", [P, SUB, NH]) for k in range(2)]
        rstd = [sb(f"rstd{k}", [P, SUB]) for k in range(2)]
        lin = [sb(f"lin{k}", [P, 3, 512]) for k in range(2)]
        by_cos = [sb(f"by_cos{k}", [P, 2, 512]) for k in range(2)]
        by_sin = [sb(f"by_sin{k}", [P, 2, 512]) for k in range(2)]
        gk = [sb(f"gk{k}", [P, 512]) for k in range(2)]
        rec_sb = sb("rec", [P, SUB, NH, RW])
        q_sb = sb("q", [P, SUB, 512])
        zero = sb("zero", [2 * CS, NH * RW])
        ps = [[ctx.enter_context(nc.psum_tensor(f"proj_ps{k}{n}", [P, 512], F32)) for n in range(3)] for k in range(2)]
        ps_st = ctx.enter_context(nc.psum_tensor("proj_ps_st", [P, SUB, NH + 2], F32))

        x_loaded = [sig(f"x_loaded{k}", 32) for k in range(2)]
        gn_spread = sig("gn_spread")
        gn_ready = sig("gn_ready")
        normed = sig("normed", CT)
        squared = sig("squared", 1)
        st_ps = sig("st_ps", 1)
        st_sb = sig("st_sb", 1)
        small_steps = sig("small_steps", 3)
        var_sb = sig("var_sb", 1)
        std_sb = sig("std_sb", 1)
        rstd_sb = sig("rstd_sb", 1)
        lr_sb = sig("lr_sb", 1)
        rate_sb = sig("rate_sb", 1)
        prod_ps = sig("prod_ps", 3 * SUB)
        lin_sb = sig("lin_sb", 3 * SUB, credit=6)
        cos_sb = sig("cos_sb", 2 * SUB, credit=4)
        sin_sb = sig("sin_sb", 2 * SUB)
        rot_sb = sig("rot_sb", 2 * SUB, credit=4)
        gk_sb = sig("gk_sb", SUB, credit=SUB)
        u_sb = sig("u_sb", SUB, credit=SUB)
        rec_out = [sig(f"rec_out{j}", 16) for j in range(SUB)]
        q_gone = [sig(f"q_out{j}", 16) for j in range(SUB)]
        init = sig("init")
        pad_out = sig("pad_out")
        block = ctx.enter_context(nc.Block())
        steps_total = images * groups

        def loop(eng, body):
            half = groups // 2

            def pair(b, g2, last=False):
                for k in range(2):
                    body(b * groups + g2 * 2 + k, b * half + g2, k, b, g2 * 2 + k, last and k == 1)

            if images > 1:
                with eng.Fori(0, images - 1) as b:
                    with eng.Fori(0, half) as g2:
                        pair(b, g2)
            if half > 1:
                with eng.Fori(0, half - 1) as g2:
                    pair(images - 1, g2)
            pair(images - 1, half - 1, True)

        @block.sync
        def _(sp):
            def body(s, it, k, b, g, last):
                sp.wait_ge(u_sb.sem, u_sb.at(s, -SUB))
                sp.dma_start(h[k][:], x_view[bass.ds(b, 1), :, :, bass.ds(g * 512, 512)].rearrange("o c k n -> (o c) k n")).then_inc(x_loaded[k].sem, 16)
                sp.dma_start(table[k][:], rope[bass.ds(g * 512, 512), :].rearrange("(j p) e -> p j e", p=P)).then_inc(x_loaded[k].sem, 16)
            loop(sp, body)

        @block.scalar
        def _(act):
            def normalise(s, it, k):
                nc.scalar.copy(gn_now[k][:], gn_steps[:, bass.ds(s, 1)].rearrange("p s a e -> p (s a) e")).then_inc(gn_ready.sem, 1)
                act.wait_ge(gn_ready.sem, gn_ready.at(s, 1))
                act.wait_ge(x_loaded[k].sem, x_loaded[k].at(it, 32))
                for ct in range(CT):
                    nc.scalar.activation(h[k][:, ct], h[k][:, ct], ACT.Identity, bias=gn_now[k][:, ct, 1:2],
                                         scale=gn_now[k][:, ct, 0:1]).then_inc(normed.sem, 1)

            def spread(s):
                act.wait_ge(var_sb.sem, var_sb.at(s, 1))
                nc.scalar.activation(small[:, 2, :], small[:, 1, :], ACT.Sqrt).then_inc(std_sb.sem, 1)

            def rates(s, k):
                act.wait_ge(gk_sb.sem, gk_sb.at(s, -SUB))
                act.wait_ge(lr_sb.sem, lr_sb.at(s, 1))
                nc.scalar.activation(rate[k][:], lr[:], ACT.Sigmoid).then_inc(rate_sb.sem, 1)

            def body(s, it, k, b, g, last):
                def store(j):
                    act.wait_ge(u_sb.sem, u_sb.at(s, j + 1))
                    act.dma_start(rec[bass.ds(b, 1), bass.ds(g * 512 + j * P, P), :, :].rearrange("o n h e -> (o n) h e"),
                                  rec_sb[:, j]).then_inc(rec_out[j].sem, 16)
                    act.dma_start(q_out[bass.ds(b, 1), bass.ds(g * 512 + j * P, P), :].rearrange("o n e -> (o n) e"),
                                  q_sb[:, j]).then_inc(q_gone[j].sem, 16)

                if not last:
                    normalise(s + 1, it + k, 1 - k)
                store(0)
                store(1)
                if not last:
                    spread(s + 1)
                store(2)
                if not last:
                    rates(s + 1, 1 - k)
                store(3)

            for b in range(images):
                nc.scalar.copy(gn_steps[:, b * groups:(b + 1) * groups],
                               gn[:, b * CT:(b + 1) * CT].unsqueeze(1).broadcast_to([P, groups, CT, 2])).then_inc(gn_spread.sem, 1)
            act.wait_ge(gn_spread.sem, gn_spread.at(images, 0))
            normalise(0, 0, 0)
            spread(0)
            rates(0, 0)
            loop(act, body)
            act.wait_ge(init.sem, init.at(0, 1))
            for b in range(B):
                act.dma_start(rec[b, TOK:TOK + 2 * CS].rearrange("n h e -> n (h e)"), zero[:]).then_inc(pad_out.sem, 16)
            act.wait_ge(pad_out.sem, pad_out.at(0, 16 * B))
            for j in range(SUB):
                act.wait_ge(rec_out[j].sem, rec_out[j].at(steps_total, 0))
                act.wait_ge(q_gone[j].sem, q_gone[j].at(steps_total, 0))

        @block.gpsimd
        def _(pool):
            g_ = nc.gpsimd

            def squares(s, k):
                pool.wait_ge(normed.sem, normed.at(s, CT))
                pool.wait_ge(st_ps.sem, st_ps.at(s, 0))
                g_.tensor_tensor(sq[:].rearrange("p a b -> p (a b)"), h[k][:].rearrange("p a b -> p (a b)"),
                                 h[k][:].rearrange("p a b -> p (a b)"), ALU.mult).then_inc(squared.sem, 1)

            def body(s, it, k, b, g, last):
                pool.wait_ge(rate_sb.sem, rate_sb.at(s, 1))
                for j in range(SUB):
                    q = j % 2
                    cos = table[k][:, j:j + 1, 0:32].broadcast_to([P, NH * 2, 32])
                    for n in range(2):
                        pool.wait_ge(lin_sb.sem, lin_sb.at(s, 3 * j + n + 1))
                        pool.wait_ge(rot_sb.sem, rot_sb.at(s, 2 * (j - 2) + n + 1))
                        g_.tensor_tensor(by_cos[q][:, n].rearrange("p (a e) -> p a e", e=32),
                                         lin[q][:, n].rearrange("p (a e) -> p a e", e=32), cos, ALU.mult).then_inc(cos_sb.sem, 1)
                    pool.wait_ge(rot_sb.sem, rot_sb.at(s, 2 * j + 2))
                    pool.wait_ge(u_sb.sem, u_sb.at(s, j - 1))
                    g_.tensor_tensor(gk[q][:].rearrange("p (h e) -> p h e", h=NH), rec_sb[:, j, :, 0:HD],
                                     T.gain[:].rearrange("p (h e) -> p h e", h=NH), ALU.mult)
                    g_.tensor_copy(rec_sb[:, j, :, 2 * HD], rate[k][:, j, :]).then_inc(gk_sb.sem, 1)
                    if j == 0 and not last:
                        squares(s + 1, 1 - k)
            pool.wait_ge(init.sem, init.at(0, 1))
            squares(0, 0)
            loop(pool, body)

        @block.vector
        def _(dve):
            v = nc.vector

            def variance(s):
                dve.wait_ge(st_ps.sem, st_ps.at(s, 1))
                v.tensor_copy(st[:], ps_st[:]).then_inc(st_sb.sem, 1)
                dve.wait_ge(st_sb.sem, st_sb.at(s, 1))
                v.tensor_tensor(small[:, 0, :], st[:, :, NH], st[:, :, NH], ALU.mult).then_inc(small_steps.sem, 1)
                dve.wait_ge(small_steps.sem, small_steps.at(s, 1))
                v.tensor_tensor(small[:, 1, :], st[:, :, NH + 1], small[:, 0, :], ALU.subtract).then_inc(small_steps.sem, 1)
                dve.wait_ge(small_steps.sem, small_steps.at(s, 2))
                v.tensor_scalar(small[:, 1, :], small[:, 1, :], 0.0, 1e-5, ALU.max, ALU.add).then_inc(var_sb.sem, 1)

            def inverse(s, k):
                dve.wait_ge(std_sb.sem, std_sb.at(s, 1))
                v.reciprocal(rstd[k][:], small[:, 2, :]).then_inc(rstd_sb.sem, 1)
                dve.wait_ge(rstd_sb.sem, rstd_sb.at(s, 1))
                dve.wait_ge(rate_sb.sem, rate_sb.at(s, 0))
                v.tensor_tensor(lr[:], st[:, :, 0:NH], rstd[k][:].unsqueeze(2).broadcast_to([P, SUB, NH]),
                                ALU.mult).then_inc(small_steps.sem, 1)
                dve.wait_ge(small_steps.sem, small_steps.at(s, 3))
                v.tensor_tensor(lr[:], lr[:], T.lrb[:].unsqueeze(1).broadcast_to([P, SUB, NH]), ALU.add).then_inc(lr_sb.sem, 1)

            def body(s, it, k, b, g, last_step):
                def target(j):
                    dve.wait_ge(gk_sb.sem, gk_sb.at(s, j + 1))
                    v.tensor_tensor(rec_sb[:, j, :, HD:2 * HD], gk[j % 2][:].rearrange("p (h e) -> p h e", h=NH),
                                    lin[j % 2][:, 2].rearrange("p (h e) -> p h e", h=NH), ALU.add).then_inc(u_sb.sem, 1)

                for j in range(SUB):
                    q = j % 2
                    for n in range(3):
                        dve.wait_ge(prod_ps.sem, prod_ps.at(s, 3 * j + n + 1))
                        if n < 2:
                            dve.wait_ge(cos_sb.sem, cos_sb.at(s, 2 * (j - 2) + n + 1))
                        v.scalar_tensor_tensor(lin[q][:, n], ps[q][n][:], rstd[k][:, j:j + 1], T.wbias[:, n],
                                               ALU.mult, ALU.add).then_inc(lin_sb.sem, 1)
                    if j:
                        target(j - 1)
                    for n in range(2):
                        dve.wait_ge(lin_sb.sem, lin_sb.at(s, 3 * j + n + 1))
                        x2 = lin[q][:, n].rearrange("p (h t e) -> p h t e", t=2, e=32)
                        o2 = by_sin[q][:, n].rearrange("p (h t e) -> p h t e", t=2, e=32)
                        for t in range(2):
                            sin = table[k][:, j:j + 1, 32 + 32 * t:64 + 32 * t].broadcast_to([P, NH, 32])
                            last = v.tensor_tensor(o2[:, :, t], x2[:, :, 1 - t], sin, ALU.mult)
                        last.then_inc(sin_sb.sem, 1)
                    dve.wait_ge(rec_out[j].sem, rec_out[j].at(s, 0))
                    dve.wait_ge(q_gone[j].sem, q_gone[j].at(s, 0))
                    for n, dst in enumerate((q_sb[:, j].rearrange("p (h e) -> p h e", h=NH), rec_sb[:, j, :, 0:HD])):
                        dve.wait_ge(sin_sb.sem, sin_sb.at(s, 2 * j + n + 1))
                        dve.wait_ge(cos_sb.sem, cos_sb.at(s, 2 * j + n + 1))
                        v.tensor_tensor(dst, by_cos[q][:, n].rearrange("p (h e) -> p h e", h=NH),
                                        by_sin[q][:, n].rearrange("p (h e) -> p h e", h=NH), ALU.add).then_inc(rot_sb.sem, 1)
                    if j == SUB - 2 and not last_step:
                        variance(s + 1)
                if not last_step:
                    inverse(s + 1, 1 - k)
                target(SUB - 1)

            v.memset(zero[:], 0.0)
            v.memset(rec_sb[:], 0.0).then_inc(init.sem, 1)
            dve.wait_ge(init.sem, init.at(0, 1))
            variance(0)
            inverse(0, 0)
            loop(dve, body)

        @block.tensor
        def _(pe):
            def sums(s, k):
                pe.wait_ge(st_sb.sem, st_sb.at(s, 0))
                pe.wait_ge(normed.sem, normed.at(s, CT))
                for j in range(SUB):
                    for ct in range(CT):
                        pe.matmul(ps_st[:, j, 0:NH + 1], h[k][:, ct, j * P:(j + 1) * P], T.lrw[:, ct],
                                  start=ct == 0, stop=ct == CT - 1)

            def square_sums(s):
                pe.wait_ge(squared.sem, squared.at(s, 1))
                for j in range(SUB):
                    for ct in range(CT):
                        last = pe.matmul(ps_st[:, j, NH + 1:NH + 2], sq[:, ct, j * P:(j + 1) * P], T.mean_col[:],
                                         start=ct == 0, stop=ct == CT - 1)
                last.then_inc(st_ps.sem, 1)

            def body(s, it, k, b, g, last):
                for j in range(SUB):
                    products(s, k, j, (0, 1, 2))
                    if j == 1 and not last:
                        sums(s + 1, 1 - k)
                    if j == 2 and not last:
                        square_sums(s + 1)

            def products(s, k, j, which):
                for n in which:
                    pe.wait_ge(lin_sb.sem, lin_sb.at(s, 3 * (j - 2) + n + 1))
                    for ct in range(CT):
                        last = pe.matmul(ps[j % 2][n][:], h[k][:, ct, j * P:(j + 1) * P], T.w[:, n, ct],
                                         start=ct == 0, stop=ct == CT - 1)
                    last.then_inc(prod_ps.sem, 1)

            sums(0, 0)
            square_sums(0)
            loop(pe, body)


def scan_chunks(nc, T, d, rec, grad_out, w_snap, b_snap, superchunks=TOK // P):
    GR = 2
    PB = B // GR
    HP = NH // 2
    F = PB * HD
    UNROLL = 4
    with ExitStack() as ctx:
        def sb(n, shape):
            return ctx.enter_context(nc.sbuf_tensor(f"scan_{n}", shape, F32))

        def sig(n, per=1, credit=0):
            return [Signal(ctx, nc, f"scan_{n}{g}", per, credit) for g in range(GR)]

        def many(n, shape, count):
            return [[sb(f"{n}{g}{q}", shape) for q in range(count)] for g in range(GR)]

        def each(n, shape):
            return [sb(f"{n}{g}", shape) for g in range(GR)]

        record = many("record", [P, PB, RW], UNROLL)
        k_pad = many("k_pad", [P, PB, 2, HD], 2)
        k_t = many("k_t", [P, PB, P], 2)
        stored = many("stored", [P, PB, HD], 2)
        w_sb = each("state_w", [P, PB, HP, HD])
        b_sb = each("state_b", [NH, F])
        zg = each("zg", [P, PB, HD])
        xh = each("xh", [P, PB, HD])
        t_row = each("t_row", [P, PB, HD])
        tx = each("tx", [P, PB, HD])
        cx = each("cx", [P, PB, HD])
        core = each("core", [P, PB, HD])
        step = each("step", [P, PB, HP, HD])
        sum_tx = each("sum_tx", [P, PB])
        sum_cx = each("sum_cx", [P, PB])
        ssq = each("ssq", [P, PB])
        std = each("std", [P, PB])
        rstd = each("rstd", [P, PB])
        rate = each("rate", [P, PB])
        rate_pair = each("rate_pair", [P, PB, HP])
        square = sb("square", [P, GR, PB, HD])
        gain8 = sb("gain8", [P, HD])
        place = sb("place", [P, 2])
        eps = sb("eps", [P, 1])
        spare = sb("spare", [P, 1])
        tok_in = sb("tok_in", [P, 2])
        last = sb("last", [P, 1])
        pair_in = sb("pair_in", [P, HP])
        pair_last = sb("pair_last", [P, HP])
        ind = sb("ind", [NH, P])
        ind_t = sb("ind_t", [P, NH])
        w0 = sb("w0", [P, B, HP, HD])
        w0_in = sb("w0_in", [P, HP, HD])
        b0 = sb("b0", [NH, B, HD])
        b0_in = sb("b0_in", [NH, HD])
        m0 = sb("m0", [P, HP])
        mb0 = sb("mb0", [NH, 1])
        ps_w = [ctx.enter_context(nc.psum_tensor(f"scan_ps_w{g}", [P, PB * HP * HD], F32)) for g in range(GR)]
        ps_b = [ctx.enter_context(nc.psum_tensor(f"scan_ps_b{g}", [NH, 512], F32)) for g in range(GR)]
        ps_z = ctx.enter_context(nc.psum_tensor("scan_ps_z", [P, GR, 512], F32))
        ps_t = ctx.enter_context(nc.psum_tensor("scan_ps_t", [P, GR, 4, P], F32))

        landed = ctx.enter_context(semaphore(nc, "scan_landed"))
        init = ctx.enter_context(semaphore(nc, "scan_init"))
        start_ps = ctx.enter_context(semaphore(nc, "scan_start_ps"))
        steps = Steps(ctx, nc, "scan_steps")
        opened = Signal(ctx, nc, "scan_opened")
        rec_in = [[Signal(ctx, nc, f"scan_rec_in{g}{q}", 32) for q in range(UNROLL)] for g in range(GR)]
        grad_gone = [[Signal(ctx, nc, f"scan_grad_gone{g}{q}", 32) for q in range(2)] for g in range(GR)]
        snap_gone = sig("snap_gone", 64)
        pad_sb = sig("pad_sb")
        kt_ps = sig("kt_ps")
        kt_sb = sig("kt_sb")
        z_ps = sig("z_ps")
        ssq_sb = sig("ssq_sb", PB)
        std_sb = sig("std_sb")
        rstd_sb = sig("rstd_sb")
        rate_sb = sig("rate_sb", 2, credit=2)
        xh_sb = sig("xh_sb")
        t_sb = sig("t_sb", PB, credit=PB)
        tx_sb = sig("tx_sb", PB)
        cx_sb = sig("cx_sb", PB)
        core_sb = sig("core_sb")
        stored_sb = sig("stored_sb")
        step_sb = sig("step_sb")
        state_ps = sig("state_ps")
        state_sb = sig("state_sb", 2)
        block = ctx.enter_context(nc.Block())
        loads = 9


        def loop(eng, body, outer=None):
            with eng.Fori(0, superchunks) as sc:
                if outer:
                    outer(sc)
                with eng.Fori(0, P // CS // UNROLL) as part:
                    for k in range(UNROLL):
                        body(sc * 8 + part * UNROLL + k, sc * 2 + part, k, sc, part)

        def load(sp, g, r, s):
            for b in range(PB):
                sp.dma_start(record[g][r][:, b, :], rec[PB * g + b, bass.ds(s * CS, CS)].rearrange("t h e -> h t e")
                             ).then_inc(rec_in[g][r].sem, 16)

        @block.sync
        def _(sp):
            for dst, src in ((gain8, d["gain_rows"]), (place, d["place"]), (ind, d["ind"]), (ind_t, d["ind_t"]),
                             (w0_in, d["w0"]), (b0_in, d["b0"]), (pair_in, d["pairs"])):
                sp.dma_start(dst[:], src).then_inc(landed, 16)
            for n in range(2):
                sp.dma_start(tok_in[:, n:n + 1], d["tok_rows"][n, CS - 1:CS].partition_broadcast(P)).then_inc(landed, 16)
            for s in range(2):
                for g in range(GR):
                    load(sp, g, s, s)

            def snapshot(sc):
                for g in range(GR):
                    sp.wait_ge(state_sb[g].sem, state_sb[g].at(sc * 8, 2))
                    for b in range(PB):
                        sp.dma_start(w_snap[bass.ds(sc, 1), PB * g + b].rearrange("o p a e -> (o p) a e"),
                                     w_sb[g][:, b]).then_inc(snap_gone[g].sem, 16)
                        sp.dma_start(b_snap[bass.ds(sc, 1), PB * g + b].rearrange("o h e -> (o h) e"),
                                     b_sb[g][:, b * HD:(b + 1) * HD]).then_inc(snap_gone[g].sem, 16)

            def body(s, it, k, sc, part):
                for g in range(GR):
                    sp.wait_ge(t_sb[g].sem, t_sb[g].at(s, -PB))
                    sp.wait_ge(rate_sb[g].sem, rate_sb[g].at(s, -2))
                    load(sp, g, (k + 2) % UNROLL, s + 2)
                for g in range(GR):
                    sp.wait_ge(stored_sb[g].sem, stored_sb[g].at(s, 1))
                    for b in range(PB):
                        sp.dma_start(grad_out[PB * g + b, bass.ds(s * CS, CS)].rearrange("t h e -> h t e"),
                                     stored[g][k % 2][:, b, :]).then_inc(grad_gone[g][k % 2].sem, 16)

            loop(sp, body, snapshot)
            steps_of = 8 * superchunks // UNROLL
            for g in range(GR):
                sp.wait_ge(snap_gone[g].sem, snap_gone[g].at(superchunks, 0))
                for r in range(UNROLL):
                    sp.wait_ge(rec_in[g][r].sem, rec_in[g][r].at(steps_of + (r < 2), 0))
                for q in range(2):
                    sp.wait_ge(grad_gone[g][q].sem, grad_gone[g][q].at(steps_of * UNROLL // 2, 0))

        @block.gpsimd
        def _(pool):
            v = nc.gpsimd

            def pad(g, k, s, it):
                pool.wait_ge(rec_in[g][k].sem, rec_in[g][k].at(it, 32))
                v.tensor_tensor(k_pad[g][k % 2][:], record[g][k][:, :, 0:HD].unsqueeze(2).broadcast_to([P, PB, 2, HD]),
                                place[:].unsqueeze(1).unsqueeze(3).broadcast_to([P, PB, 2, HD]), ALU.mult).then_inc(pad_sb[g].sem, 1)

            pool.wait_ge(landed, 16 * loads)
            pool.wait_ge(init, 1)
            for g in range(GR):
                pad(g, 0, 0, 0)

            def body(s, it, k, sc, part):
                for g in range(GR):
                    pool.wait_ge(state_ps[g].sem, state_ps[g].at(s, g))
                    pad(g, (k + 1) % UNROLL, s + 1, it + (k + 1) // UNROLL)
                    pool.wait_ge(rstd_sb[g].sem, rstd_sb[g].at(s, 1))
                    v.tensor_tensor(rate[g][:], rstd[g][:], record[g][k][:, :, 2 * HD], ALU.mult).then_inc(rate_sb[g].sem, 1)
                    pool.wait_ge(step_sb[g].sem, step_sb[g].at(s, 0))
                    pool.wait_ge(rate_sb[g].sem, rate_sb[g].at(s, 1))
                    v.tensor_tensor(rate_pair[g][:], rate[g][:].unsqueeze(2).broadcast_to([P, PB, HP]),
                                    pair_last[:].unsqueeze(1).broadcast_to([P, PB, HP]), ALU.mult).then_inc(rate_sb[g].sem, 1)
                    pool.wait_ge(grad_gone[g][k % 2].sem, grad_gone[g][k % 2].at(it * (UNROLL // 2) + k // 2, 0))
                    pool.wait_ge(core_sb[g].sem, core_sb[g].at(s, 1))
                    v.tensor_tensor(stored[g][k % 2][:], core[g][:], rate[g][:].unsqueeze(2).broadcast_to([P, PB, HD]),
                                    ALU.mult).then_inc(stored_sb[g].sem, 1)

            loop(pool, body)

        @block.scalar
        def _(act):
            a = nc.scalar

            def state_out(g):
                a.copy(w_sb[g][:].rearrange("p b a e -> p (b a e)"), ps_w[g][:]).then_inc(state_sb[g].sem, 1)
                a.copy(b_sb[g][:], ps_b[g][:, 0:F]).then_inc(state_sb[g].sem, 1)

            def turned(g, q, s):
                act.wait_ge(kt_ps[g].sem, kt_ps[g].at(s, 1))
                a.copy(k_t[g][q][:], ps_t[:, g, 0:PB]).then_inc(kt_sb[g].sem, 1)

            def spread(g, s):
                act.wait_ge(z_ps[g].sem, z_ps[g].at(s, 1))
                act.wait_ge(rstd_sb[g].sem, rstd_sb[g].at(s, 0))
                for b in range(PB):
                    a.activation(square[:, g, b], ps_z[:, g, b * HD:(b + 1) * HD], ACT.Square,
                                 accum_out=ssq[g][:, b:b + 1]).then_inc(ssq_sb[g].sem, 1)
                act.wait_ge(ssq_sb[g].sem, ssq_sb[g].at(s, PB))
                a.activation(std[g][:], ssq[g][:], ACT.Sqrt, bias=eps[:]).then_inc(std_sb[g].sem, 1)

            act.wait_ge(start_ps, 1)
            act.wait_ge(init, 1)
            state_out(0)
            for g in range(GR):
                turned(g, 0, 0)

            def body(s, it, k, sc, part):
                if k == 0:
                    act.wait_ge(opened.sem, opened.at(it, 0))
                    a.activation(spare[:], eps[:], ACT.Sqrt).then_inc(opened.sem, 1)
                spread(0, s)
                act.wait_ge(state_ps[1].sem, state_ps[1].at(s, 1))
                act.wait_ge(snap_gone[1].sem, snap_gone[1].at(sc + part if k == 0 else sc + 1, 0))
                state_out(1)
                turned(0, (k + 1) % 2, s + 1)
                spread(1, s)
                act.wait_ge(state_ps[0].sem, state_ps[0].at(s, 1))
                act.wait_ge(snap_gone[0].sem, snap_gone[0].at(sc + 1, 0))
                state_out(0)
                turned(1, (k + 1) % 2, s + 1)

            loop(act, body)

        @block.vector
        def _(dve):
            v = nc.vector
            dve.wait_ge(landed, 16 * loads)
            steps.then(dve, v.tensor_tensor(last[:], tok_in[:, 0:1], tok_in[:, 1:2], ALU.add))
            steps.then(dve, v.tensor_scalar(last[:], last[:], 0.0, 1.0 / 8, ALU.max, ALU.mult))
            steps.then(dve, v.tensor_scalar(pair_last[:], pair_in[:], last[:], None, ALU.mult))
            steps.then(dve, v.tensor_scalar(ind_t[:], ind_t[:], last[:], None, ALU.mult))
            steps.then(dve, v.memset(eps[:], HD * 1e-6))
            steps.then(dve, v.memset(step[1][:], 0.0))
            steps.then(dve, v.memset(k_pad[1][1][:], 0.0))
            steps.then(dve, v.memset(stored[1][1][:], 0.0))
            steps.then(dve, v.scalar_tensor_tensor(gain8[:], gain8[:], 8.0, gain8[:], ALU.mult, ALU.mult))
            steps.then(dve, v.tensor_reduce(m0[:], w0_in[:], AX.X, ALU.add))
            steps.then(dve, v.tensor_reduce(mb0[:], b0_in[:], AX.X, ALU.add))
            for b in range(B):
                steps.then(dve, v.scalar_tensor_tensor(w0[:, b], m0[:].unsqueeze(2).broadcast_to([P, HP, HD]), -1.0 / HD,
                                                       w0_in[:], ALU.mult, ALU.add))
                steps.then(dve, v.scalar_tensor_tensor(b0[:, b, :], mb0[:].broadcast_to([NH, HD]), -1.0 / HD,
                                                       b0_in[:], ALU.mult, ALU.add))
            dve.sem_inc(init, 1)

            def body(s, it, k, sc, part):
                for g in range(GR):
                    def wide(x):
                        return x.unsqueeze(2).broadcast_to([P, PB, HD])

                    z = ps_z[:, g, 0:F].rearrange("p (b e) -> p b e", b=PB)
                    dve.wait_ge(ssq_sb[g].sem, ssq_sb[g].at(s, PB))
                    v.tensor_tensor(zg[g][:], z, gain8[:].unsqueeze(1).broadcast_to([P, PB, HD]), ALU.mult)
                    dve.wait_ge(std_sb[g].sem, std_sb[g].at(s, 1))
                    dve.wait_ge(rate_sb[g].sem, rate_sb[g].at(s, 0))
                    v.reciprocal(rstd[g][:], std[g][:]).then_inc(rstd_sb[g].sem, 1)
                    dve.wait_ge(rstd_sb[g].sem, rstd_sb[g].at(s, 1))
                    v.tensor_tensor(xh[g][:], z, wide(rstd[g][:]), ALU.mult).then_inc(xh_sb[g].sem, 1)
                    for b in range(PB):
                        v.scalar_tensor_tensor(t_row[g][:, b], zg[g][:, b], rstd[g][:, b:b + 1], record[g][k][:, b, HD:2 * HD],
                                               ALU.mult, ALU.add).then_inc(t_sb[g].sem, 1)
                    dve.wait_ge(xh_sb[g].sem, xh_sb[g].at(s, 1))
                    for b in range(PB):
                        dve.wait_ge(t_sb[g].sem, t_sb[g].at(s, b + 1))
                        v.scalar_tensor_tensor(tx[g][:, b], t_row[g][:, b], 1.0, xh[g][:, b], ALU.mult, ALU.mult,
                                               accum_out=sum_tx[g][:, b:b + 1]).then_inc(tx_sb[g].sem, 1)
                    for b in range(PB):
                        dve.wait_ge(tx_sb[g].sem, tx_sb[g].at(s, b + 1))
                        v.scalar_tensor_tensor(cx[g][:, b], xh[g][:, b], sum_tx[g][:, b:b + 1], t_row[g][:, b],
                                               ALU.mult, ALU.subtract, accum_out=sum_cx[g][:, b:b + 1]).then_inc(cx_sb[g].sem, 1)
                    dve.wait_ge(stored_sb[g].sem, stored_sb[g].at(s, 0))
                    dve.wait_ge(cx_sb[g].sem, cx_sb[g].at(s, PB))
                    v.scalar_tensor_tensor(core[g][:], wide(sum_cx[g][:]), -1.0 / HD, cx[g][:], ALU.mult,
                                           ALU.add).then_inc(core_sb[g].sem, 1)
                    dve.wait_ge(rate_sb[g].sem, rate_sb[g].at(s, 2))
                    dve.wait_ge(state_ps[g].sem, state_ps[g].at(s, g))
                    dve.wait_ge(core_sb[g].sem, core_sb[g].at(s, 1))
                    v.tensor_tensor(step[g][:], core[g][:].unsqueeze(2).broadcast_to([P, PB, HP, HD]),
                                    rate_pair[g][:].unsqueeze(3).broadcast_to([P, PB, HP, HD]), ALU.mult).then_inc(step_sb[g].sem, 1)

            loop(dve, body)

        @block.tensor
        def _(pe):
            pe.wait_ge(init, 1)
            for g in range(GR):
                pe.matmul(ps_w[g][:], T.ident[:], w0[:, PB * g:PB * g + PB].rearrange("p b a e -> p (b a e)"),
                          start=True, stop=True, skip_group_check=True)
                last_mm = pe.matmul(ps_b[g][:, 0:F], T.ident[0:NH, 0:NH], b0[:, PB * g:PB * g + PB].rearrange("p b e -> p (b e)"),
                                    start=True, stop=True, skip_group_check=True)
            last_mm.then_inc(start_ps, 1)

            def turn(g, q, s):
                pe.wait_ge(pad_sb[g].sem, pad_sb[g].at(s, 1))
                pe.wait_ge(kt_sb[g].sem, kt_sb[g].at(s, 0))
                for b in range(PB):
                    done = pe.transpose(ps_t[:, g, b], k_pad[g][q][:, b].rearrange("p a e -> p (a e)"), T.ident[:])
                done.then_inc(kt_ps[g].sem, 1)

            def project_k(g, q, s):
                pe.wait_ge(kt_sb[g].sem, kt_sb[g].at(s, 1))
                pe.wait_ge(t_sb[g].sem, t_sb[g].at(s, 0))
                pe.wait_ge(xh_sb[g].sem, xh_sb[g].at(s, 0))
                pe.wait_ge(state_sb[g].sem, state_sb[g].at(s, 2))
                for a in range(HP):
                    rows = slice(32 * a, 32 * a + 32)
                    for b in range(PB):
                        pe.matmul(ps_z[rows, g, b * HD:(b + 1) * HD], k_t[g][q][:, b, rows], w_sb[g][:, b, a],
                                  start=b == 0, stop=False, skip_group_check=True)
                pe.matmul(ps_z[:, g, 0:F], ind[:], b_sb[g][:], start=False, stop=True,
                          skip_group_check=True).then_inc(z_ps[g].sem, 1)

            def update(g, q, s):
                pe.wait_ge(step_sb[g].sem, step_sb[g].at(s, 1))
                pe.wait_ge(state_sb[g].sem, state_sb[g].at(s, 2))
                for b in range(PB):
                    n = HP * HD
                    pe.matmul(ps_w[g][:, b * n:(b + 1) * n], k_pad[g][q][:, b].rearrange("p a e -> p (a e)"),
                              step[g][:, b].rearrange("p a e -> p (a e)"), start=False, stop=True, skip_group_check=True)
                pe.wait_ge(stored_sb[g].sem, stored_sb[g].at(s, 1))
                pe.matmul(ps_b[g][:, 0:F], ind_t[:], stored[g][q][:].rearrange("p b e -> p (b e)"), start=False, stop=True,
                          skip_group_check=True).then_inc(state_ps[g].sem, 1)

            for g in range(GR):
                turn(g, 0, 0)

            def body(s, it, k, sc, part):
                q = k % 2
                project_k(0, q, s)
                update(1, 1 - q, s - 1)
                turn(0, 1 - q, s + 1)
                project_k(1, q, s)
                update(0, q, s)
                turn(1, 1 - q, s + 1)

            loop(pe, body)


def read_out(nc, T, d, x_in, rec, q_in, grad, w_snap, b_snap, x_out, chan_stats):
    HP = NH // 2
    SC = TOK // P
    x_view = x_in.rearrange("b (k c) h w -> b c k (h w)", c=P)
    o_view = x_out.rearrange("b (k c) h w -> b c k (h w)", c=P)
    with ExitStack() as ctx:
        def sb(n, shape):
            return ctx.enter_context(nc.sbuf_tensor(f"read_{n}", shape, F32))

        def two(n, shape):
            return [sb(f"{n}{q}", shape) for q in range(2)]

        def ps(n, shape):
            return ctx.enter_context(nc.psum_tensor(f"read_{n}", shape, F32))

        def sig(n, per=1, credit=0):
            return Signal(ctx, nc, f"read_{n}", per, credit)

        k_sb = two("k", [P, NH, HD])
        q_sb = two("q", [P, NH, HD])
        steps_sb = two("steps", [P, NH, HD])
        w_sb = two("w", [P, HP, HD])
        b_sb = two("b", [1, NH, HD])
        x_sb = two("x", [P, CT, P])
        k_t = sb("k_t", [P, HP, P])
        q_t = sb("q_t", [P, HP, P])
        weigh = two("weigh", [P, HP, P])
        zsq = sb("zsq", [P, NH, HD])
        ssq = sb("ssq", [P, NH])
        std = sb("std", [P, NH])
        rstd = sb("rstd", [P, NH])
        zn = two("zn", [P, NH, HD])
        zg = two("zg", [P, NH, HD])
        qb = two("qb", [P, NH, HD])
        o_sb = two("o", [P, NH * HD])
        on = two("on", [P, NH * HD])
        osq = sb("osq", [P, NH * HD])
        osum = two("osum", [P, 2])
        nmean = two("nmean", [P, 1])
        ovar = two("ovar", [P, 1])
        orstd = two("orstd", [P, 1])
        oshift = two("oshift", [P, 1])
        o_t = sb("o_t", [P, CT, P])
        y_sb = two("y", [P, CT, P])
        stats6 = sb("stats6", [P, UNITS, SC, 6])
        mask = sb("mask", [P, P])
        masks_in = sb("masks_in", [P, 2, P])
        tok = sb("tok", [P, 2, P])
        gain8 = sb("gain8", [P, NH * HD])
        eps = sb("eps", [P, 2])
        ones = sb("ones", [1, P])
        ps_kt = ps("ps_kt", [P, HP, P])
        ps_qt = ps("ps_qt", [P, HP, P])
        ps_kq = [ps(f"ps_kq{q}", [P, HP, P]) for q in range(2)]
        ps_z = [ps(f"ps_z{q}", [P, HP, P]) for q in range(2)]
        ps_ot = ps("ps_ot", [P, CT, P])
        ps_y = ps("ps_y", [P, CT, P])

        landed = ctx.enter_context(semaphore(nc, "read_landed"))
        init = ctx.enter_context(semaphore(nc, "read_init"))
        steps = Steps(ctx, nc, "read_steps")
        in_sb = [sig(f"in{q}", 80) for q in range(2)]
        x_in_sb = [sig(f"x_in{q}", 16) for q in range(2)]
        y_gone = [sig(f"y_gone{q}", 16) for q in range(2)]
        turned_ps = sig("turned_ps", 2)
        turned_sb = sig("turned_sb", 2)
        kq_ps = sig("kq_ps", 2)
        weigh_sb = sig("weigh_sb", 2, credit=2)
        z_ps = sig("z_ps", 2, credit=2)
        ssq_in = sig("ssq_in", 2)
        ssq_sb = sig("ssq_sb", 1)
        std_sb = sig("std_sb", 1)
        rstd_sb = sig("rstd_sb", 1)
        zn_sb = sig("zn_sb", 1)
        qb_sb = sig("qb_sb", 1, credit=2)
        zg_sb = sig("zg_sb", 1, credit=2)
        o_done = sig("o_done", 1, credit=2)
        osq_sb = sig("osq_sb", 1)
        small = sig("small", 2)
        ovar_sb = sig("ovar_sb", 1)
        ostd_sb = sig("ostd_sb", 1)
        orstd_sb = sig("orstd_sb", 1)
        oshift_sb = sig("oshift_sb", 1)
        on_sb = sig("on_sb", 1)
        ot_ps = sig("ot_ps", 1)
        ot_sb = sig("ot_sb", 1)
        y_ps = sig("y_ps", 1)
        y_sb_done = sig("y_sb", 1, credit=4)
        stats_sb = sig("stats_sb", CT)
        block = ctx.enter_context(nc.Block())
        loads = 5
        LAG = 2

        def schedule(eng, step):
            def tile(sc, b):
                return (sc + b // B) * B + b % B, b % B, sc + b // B

            step(tile(0, 0), None, None)
            step(tile(0, 1), tile(0, 0), None)
            with eng.Fori(0, SC - 1) as sc:
                for b in range(B):
                    step(tile(sc, b + LAG), tile(sc, b + 1), tile(sc, b))
            for b in range(B):
                step(*(tile(SC - 1, b + n) if b + n < B else None for n in (LAG, 1, 0)))

        @block.sync
        def _(sp):
            sp.dma_start(masks_in[:], d["masks"]).then_inc(landed, 16)
            for n in range(2):
                sp.dma_start(tok[:, n], d["tok_rows"][n].partition_broadcast(P)).then_inc(landed, 16)
            sp.dma_start(gain8[:], d["ttt_rows"][0].partition_broadcast(P)).then_inc(landed, 16)
            sp.dma_start(eps[:], d["eps"]).then_inc(landed, 16)

            def inner(t, b, sc):
                q = b % 2
                sp.dma_start(k_sb[q][:], rec[b, bass.ds(sc * P, P), :, 0:HD]).then_inc(in_sb[q].sem, 16)
                sp.dma_start(q_sb[q][:], q_in[b, bass.ds(sc * P, P)].rearrange("n (h e) -> n h e", h=NH)).then_inc(in_sb[q].sem, 16)
                sp.dma_start(w_sb[q][:], w_snap[bass.ds(sc, 1), b].rearrange("o p a e -> (o p) a e")).then_inc(in_sb[q].sem, 16)
                sp.dma_start(b_sb[q][:], b_snap[bass.ds(sc, 1), b]).then_inc(in_sb[q].sem, 16)
                sp.dma_start(steps_sb[q][:], grad[b, bass.ds(sc * P, P)]).then_inc(in_sb[q].sem, 16)

            def outer(t, b, sc):
                sp.dma_start(x_sb[b % 2][:], x_view[b, :, :, bass.ds(sc * P, P)]).then_inc(x_in_sb[b % 2].sem, 16)

            def step(one, mid, other):
                count = zg_sb.at(one[0], -1) if one else y_sb_done.at(other[0], -1)
                if one:
                    sp.wait_ge(zg_sb.sem, count)
                if other:
                    sp.wait_ge(y_sb_done.sem, count)
                if one:
                    inner(*one)
                if other:
                    outer(*other)

            schedule(sp, step)

        @block.gpsimd
        def _(pool):
            v = nc.gpsimd
            pool.wait_ge(init, 1)

            def inner(t, b, sc):
                q = b % 2
                pool.wait_ge(in_sb[q].sem, in_sb[q].at(sc * 2 + b // 2, 80))
                pool.wait_ge(o_done.sem, o_done.at(t, -1))
                v.tensor_tensor(qb[q][:], q_sb[q][:], T.shift[:].rearrange("p (h e) -> p h e", h=NH), ALU.add).then_inc(qb_sb.sem, 1)
                pool.wait_ge(zn_sb.sem, zn_sb.at(t, 1))
                v.tensor_tensor(zg[q][:], zn[q][:], gain8[:].rearrange("p (h e) -> p h e", h=NH), ALU.mult).then_inc(zg_sb.sem, 1)

            schedule(pool, lambda one, mid, other: inner(*one) if one else None)

        @block.scalar
        def _(act):
            a = nc.scalar
            act.wait_ge(init, 1)

            def inner(t, b, sc):
                for n, (dst, src) in enumerate(((k_t, ps_kt), (q_t, ps_qt))):
                    act.wait_ge(turned_ps.sem, turned_ps.at(t, n + 1))
                    a.copy(dst[:], src[:]).then_inc(turned_sb.sem, 1)

            def norms(t, b, sc):
                act.wait_ge(ssq_sb.sem, ssq_sb.at(t, 0))
                for n in range(2):
                    act.wait_ge(z_ps.sem, z_ps.at(t, n + 1))
                    a.activation(zsq[:].rearrange("p (a n) e -> p a n e", n=2)[:, :, n], ps_z[n][:, :, 0:HD], ACT.Square
                                 ).then_inc(ssq_in.sem, 1)
                act.wait_ge(ssq_sb.sem, ssq_sb.at(t, 1))
                act.wait_ge(rstd_sb.sem, rstd_sb.at(t, 0))
                a.activation(std[:], ssq[:], ACT.Sqrt, bias=eps[:, 0:1]).then_inc(std_sb.sem, 1)

            def outer_norm(t, b, sc):
                q = b % 2
                act.wait_ge(o_done.sem, o_done.at(t, 1))
                act.wait_ge(osq_sb.sem, osq_sb.at(t, 0))
                a.activation(osq[:], o_sb[q][:], ACT.Square, accum_out=osum[q][:, 1:2]).then_inc(osq_sb.sem, 1)
                act.wait_ge(ovar_sb.sem, ovar_sb.at(t, 1))
                a.activation(ovar[q][:], ovar[q][:], ACT.Sqrt, bias=eps[:, 1:2]).then_inc(ostd_sb.sem, 1)
                act.wait_ge(oshift_sb.sem, oshift_sb.at(t, 1))
                a.activation(on[q][:], o_sb[q][:], ACT.Identity, bias=oshift[q][:], scale=orstd[q][:]).then_inc(on_sb.sem, 1)

            def outer(t, b, sc):
                act.wait_ge(ot_ps.sem, ot_ps.at(t, 1))
                a.copy(o_t[:], ps_ot[:]).then_inc(ot_sb.sem, 1)

            def store(t, b, sc):
                q = b % 2
                act.wait_ge(y_sb_done.sem, y_sb_done.at(t, 1))
                act.dma_start(o_view[b, :, :, bass.ds(sc * P, P)], y_sb[q][:]).then_inc(y_gone[q].sem, 16)

            def step(one, mid, other):
                if one:
                    inner(*one)
                if other:
                    outer(*other)
                if mid:
                    outer_norm(*mid)
                if other:
                    store(*other)
                if one:
                    norms(*one)

            schedule(act, step)
            for q in range(2):
                act.wait_ge(y_gone[q].sem, y_gone[q].at(SC * B // 2, 0))

        @block.vector
        def _(dve):
            v = nc.vector
            dve.wait_ge(landed, 16 * loads)
            steps.then(dve, v.tensor_tensor(tok[:, 0], tok[:, 0], tok[:, 1], ALU.add))
            steps.then(dve, v.tensor_scalar(tok[:, 0], tok[:, 0], 0.0, 1.0 / 8, ALU.max, ALU.mult))
            steps.then(dve, v.tensor_tensor(mask[:], masks_in[:, 0], tok[:, 0], ALU.mult))
            steps.then(dve, v.scalar_tensor_tensor(mask[:], masks_in[:, 1], tok[:, 0, CS - 1:CS], mask[:], ALU.mult, ALU.add))
            steps.then(dve, v.tensor_scalar(gain8[:], gain8[:], 8.0, None, ALU.mult))
            steps.then(dve, v.memset(ones[:], 1.0))
            dve.sem_inc(init, 1)

            def inner(t, b, sc):
                wide_mask = mask[:].unsqueeze(1).broadcast_to([P, HP, P])
                for n in range(2):
                    dve.wait_ge(kq_ps.sem, kq_ps.at(t, n + 1))
                    dve.wait_ge(z_ps.sem, z_ps.at(t, n - 1))
                    v.scalar_tensor_tensor(weigh[n][:], ps_kq[n][:], 1.0, wide_mask, ALU.add, ALU.mult).then_inc(weigh_sb.sem, 1)

            def norms(t, b, sc):
                q = b % 2
                dve.wait_ge(ssq_in.sem, ssq_in.at(t, 2))
                dve.wait_ge(std_sb.sem, std_sb.at(t, 0))
                v.tensor_reduce(ssq[:], zsq[:], AX.X, ALU.add).then_inc(ssq_sb.sem, 1)
                dve.wait_ge(std_sb.sem, std_sb.at(t, 1))
                v.reciprocal(rstd[:], std[:]).then_inc(rstd_sb.sem, 1)
                dve.wait_ge(rstd_sb.sem, rstd_sb.at(t, 1))
                dve.wait_ge(zg_sb.sem, zg_sb.at(t, -1))
                for n in range(2):
                    last = v.tensor_tensor(zn[q][:].rearrange("p (a n) e -> p a n e", n=2)[:, :, n], ps_z[n][:, :, 0:HD],
                                           rstd[:].rearrange("p (a n) -> p a n", n=2)[:, :, n:n + 1].broadcast_to([P, HP, HD]), ALU.mult)
                last.then_inc(zn_sb.sem, 1)

            def outer_norm(t, b, sc):
                q = b % 2
                dve.wait_ge(zg_sb.sem, zg_sb.at(t, 1))
                dve.wait_ge(qb_sb.sem, qb_sb.at(t, 1))
                v.scalar_tensor_tensor(o_sb[q][:], zg[q][:].rearrange("p h e -> p (h e)"), 1.0,
                                       qb[q][:].rearrange("p h e -> p (h e)"), ALU.mult, ALU.add,
                                       accum_out=osum[q][:, 0:1]).then_inc(o_done.sem, 1)
                dve.wait_ge(o_done.sem, o_done.at(t, 1))
                v.tensor_scalar(nmean[q][:], osum[q][:, 0:1], -1.0 / C, None, ALU.mult).then_inc(small.sem, 1)
                dve.wait_ge(small.sem, small.at(t, 1))
                dve.wait_ge(osq_sb.sem, osq_sb.at(t, 1))
                v.tensor_tensor(ovar[q][:], nmean[q][:], nmean[q][:], ALU.mult).then_inc(small.sem, 1)
                dve.wait_ge(small.sem, small.at(t, 2))
                v.scalar_tensor_tensor(ovar[q][:], osum[q][:, 1:2], 1.0 / C, ovar[q][:], ALU.mult, ALU.subtract).then_inc(ovar_sb.sem, 1)
                dve.wait_ge(ostd_sb.sem, ostd_sb.at(t, 1))
                v.reciprocal(orstd[q][:], ovar[q][:]).then_inc(orstd_sb.sem, 1)
                dve.wait_ge(orstd_sb.sem, orstd_sb.at(t, 1))
                v.tensor_tensor(oshift[q][:], nmean[q][:], orstd[q][:], ALU.mult).then_inc(oshift_sb.sem, 1)

            def outer(t, b, sc):
                q = b % 2
                dve.wait_ge(y_ps.sem, y_ps.at(t, 1))
                dve.wait_ge(x_in_sb[q].sem, x_in_sb[q].at(sc * 2 + b // 2, 16))
                dve.wait_ge(y_gone[q].sem, y_gone[q].at(sc * 2 + b // 2, 0))
                for n in range(CT):
                    last = v.scalar_tensor_tensor(y_sb[q][:, n], ps_y[:, n], T.wo_bias[:, n:n + 1], x_sb[q][:, n], ALU.add, ALU.add)
                last.then_inc(y_sb_done.sem, 1)
                dve.wait_ge(y_sb_done.sem, y_sb_done.at(t, 1))
                for n in range(CT):
                    where = stats6[:, b * CT + n, bass.ds(sc, 1), :].rearrange("p o e -> p (o e)")
                    v.bn_stats(where, y_sb[q][:, n]).then_inc(stats_sb.sem, 1)

            def step(one, mid, other):
                if one:
                    inner(*one)
                if mid:
                    outer_norm(*mid)
                if other:
                    outer(*other)
                if one:
                    norms(*one)

            schedule(dve, step)
            dve.wait_ge(stats_sb.sem, stats_sb.at(SC * B, 0))
            for u in range(UNITS):
                v.bn_aggr(chan_stats[:, u, :], stats6[:, u].rearrange("p s e -> p (s e)"))

        @block.tensor
        def _(pe):
            pe.wait_ge(init, 1)

            def tile_turns(t, b, sc):
                q = b % 2
                pe.wait_ge(in_sb[q].sem, in_sb[q].at(sc * 2 + b // 2, 80))
                pe.wait_ge(turned_sb.sem, turned_sb.at(t, 0))
                for a in range(HP):
                    last = pe.transpose(ps_kt[:, a], k_sb[q][:, 2 * a:2 * a + 2].rearrange("p h e -> p (h e)"), T.ident[:])
                last.then_inc(turned_ps.sem, 1)
                for a in range(HP):
                    last = pe.transpose(ps_qt[:, a], q_sb[q][:, 2 * a:2 * a + 2].rearrange("p h e -> p (h e)"), T.ident[:])
                last.then_inc(turned_ps.sem, 1)

            def tile_weights(t, b, sc):
                pe.wait_ge(turned_sb.sem, turned_sb.at(t, 2))
                for n in range(2):
                    rows = slice(64 * n, 64 * n + 64)
                    pe.wait_ge(weigh_sb.sem, weigh_sb.at(t, n - 1))
                    for a in range(HP):
                        last = pe.matmul(ps_kq[n][:, a], k_t[rows, a], q_t[rows, a], start=True, stop=True)
                    last.then_inc(kq_ps.sem, 1)

            def tile_outputs(t, b, sc):
                q = b % 2
                pe.wait_ge(zn_sb.sem, zn_sb.at(t, 0))
                for n in range(2):
                    rows = slice(64 * n, 64 * n + 64)
                    out = ps_z[n][:, :, 0:HD]
                    pe.matmul(out, ones[:], b_sb[q][:].rearrange("p (a n) e -> p a n e", n=2)[:, :, n], start=True, stop=False,
                              skip_group_check=True)
                    pe.wait_ge(weigh_sb.sem, weigh_sb.at(t, n + 1))
                    for a in range(HP):
                        pe.matmul(out[:, a], weigh[n][:, a], steps_sb[q][:, 2 * a + n], start=False, stop=False, skip_group_check=True)
                    for a in range(HP):
                        last = pe.matmul(out[:, a], q_t[rows, a], w_sb[q][rows, a], start=False, stop=True, skip_group_check=True)
                    last.then_inc(z_ps.sem, 1)

            def tile_back(t, b, sc):
                q = b % 2
                pe.wait_ge(on_sb.sem, on_sb.at(t, 1))
                pe.wait_ge(ot_sb.sem, ot_sb.at(t, 0))
                for n in range(CT):
                    last = pe.transpose(ps_ot[:, n], on[q][:, n * P:(n + 1) * P], T.ident[:])
                last.then_inc(ot_ps.sem, 1)

            def tile_project(t, b, sc):
                pe.wait_ge(ot_sb.sem, ot_sb.at(t, 1))
                pe.wait_ge(y_sb_done.sem, y_sb_done.at(t, 0))
                for n in range(CT):
                    for ct in range(CT):
                        last = pe.matmul(ps_y[:, n], T.wo[:, ct, n * P:(n + 1) * P], o_t[:, ct], start=ct == 0, stop=ct == CT - 1)
                last.then_inc(y_ps.sem, 1)

            def step(one, mid, other):
                if one:
                    tile_turns(*one)
                if other:
                    tile_back(*other)
                if one:
                    tile_weights(*one)
                if other:
                    tile_project(*other)
                if one:
                    tile_outputs(*one)

            schedule(pe, step)


def norm_factors(nc, name, gmean, grstd, gn, coef):
    with ExitStack() as ctx:
        steps = Steps(ctx, nc, f"{name}_steps")
        block = ctx.enter_context(nc.Block())

        @block.vector
        def _(dve):
            v = nc.vector
            steps.then(dve, v.tensor_copy(gn[:, :, 0], grstd[:]))
            steps.then(dve, v.scalar_tensor_tensor(gn[:, :, 1], gmean[:], -1.0, grstd[:], ALU.mult, ALU.mult))
            if coef is not None:
                steps.then(dve, v.tensor_copy(coef[:, :, 0], grstd[:]))
                steps.then(dve, v.tensor_scalar(coef[:, :, 1], gn[:, :, 1], 64.0, None, ALU.mult))
                steps.then(dve, v.memset(coef[:, :, 2], 1.0))
                steps.then(dve, v.memset(coef[:, :, 3], 0.0))


def gate_channels(nc, d, chan_stats, block_sums, gn, keep, rest, next_stats):
    HID = C // 16
    NBLK = 16
    with ExitStack() as ctx:
        def sb(n, shape):
            return ctx.enter_context(nc.sbuf_tensor(f"gating_{n}", shape, F32))

        w1 = sb("w1", [P, 3, 9])
        w2 = sb("w2", [P, 9])
        fc1 = sb("fc1", [P, CT, HID])
        fc2 = sb("fc2", [HID, C])
        by_scale = sb("by_scale", [P, 3, 4, 4])
        quads = sb("quads", [P, 2, 2])
        rows = sb("rows", [P, 2, 4])
        whole = sb("whole", [P, 1])
        weight = sb("weight", [P, NBLK])
        weight_sum = sb("weight_sum", [P, 1])
        terms = sb("terms", [P, UNITS, NBLK])
        z = sb("z", [P, UNITS])
        hid = sb("hid", [HID, B])
        gate = sb("gate", [P, B, CT])
        ps_hid = ctx.enter_context(nc.psum_tensor("gate_ps_hid", [HID, B], F32))
        ps_gate = ctx.enter_context(nc.psum_tensor("gate_ps_gate", [P, CT, B], F32))
        landed = ctx.enter_context(semaphore(nc, "gate_landed"))
        z_made = ctx.enter_context(semaphore(nc, "gate_z_made"))
        hid_ps = ctx.enter_context(semaphore(nc, "gate_hid_ps"))
        hid_sb = ctx.enter_context(semaphore(nc, "gate_hid_sb"))
        gate_ps = ctx.enter_context(semaphore(nc, "gate_gate_ps"))
        gate_sb = ctx.enter_context(semaphore(nc, "gate_gate_sb"))
        steps = Steps(ctx, nc, "gate_steps")
        block = ctx.enter_context(nc.Block())

        @block.sync
        def _(sp):
            sp.dma_start(w1[:], d["gate_w1"].partition_broadcast(P)).then_inc(landed, 16)
            sp.dma_start(w2[:], d["gate_w2"].partition_broadcast(P)).then_inc(landed, 16)
            sp.dma_start(fc1[:], d["fc1_wT"]).then_inc(landed, 16)
            sp.dma_start(fc2[:], d["fc2_wT"]).then_inc(landed, 16)

        @block.vector
        def _(dve):
            v = nc.vector

            def then(ins):
                steps.then(dve, ins)

            dve.wait_ge(landed, 64)
            then(v.memset(by_scale[:], 0.0))
            for i in range(2):
                for j in range(2):
                    tap = (i + 1) * 3 + j + 1
                    for s in range(3):
                        part = by_scale[:, s, i:i + 3, j:j + 3]
                        then(v.scalar_tensor_tensor(part, w1[:, s].rearrange("p (a b) -> p a b", b=3), w2[:, tap:tap + 1],
                                                    part, ALU.mult, ALU.add))
            then(v.tensor_reduce(whole[:], by_scale[:, 0].rearrange("p a b -> p (a b)"), AX.X, ALU.add))
            for q in range(2):
                then(v.tensor_tensor(rows[:, q], by_scale[:, 1, 2 * q], by_scale[:, 1, 2 * q + 1], ALU.add))
            then(v.tensor_tensor(quads[:], rows[:, :, 0:4:2], rows[:, :, 1:4:2], ALU.add))
            for q in range(2):
                for i in range(2):
                    then(v.scalar_tensor_tensor(weight[:, 8 * q + 4 * i:8 * q + 4 * i + 4].rearrange("p (a b) -> p a b", b=2),
                                                quads[:, q].unsqueeze(2).broadcast_to([P, 2, 2]), 0.25,
                                                by_scale[:, 2, 2 * q + i].rearrange("p (a b) -> p a b", b=2), ALU.mult, ALU.add))
            then(v.scalar_tensor_tensor(weight[:], whole[:].broadcast_to([P, NBLK]), 1.0 / NBLK, weight[:], ALU.mult, ALU.add))
            then(v.tensor_reduce(weight_sum[:], weight[:], AX.X, ALU.add))
            then(v.tensor_tensor(terms[:], block_sums[:], weight[:].unsqueeze(1).broadcast_to([P, UNITS, NBLK]), ALU.mult))
            then(v.tensor_reduce(z[:], terms[:], AX.X, ALU.add))
            then(v.scalar_tensor_tensor(z[:], z[:], 1.0 / 256, gn[:, :, 0], ALU.mult, ALU.mult))
            v.scalar_tensor_tensor(z[:], gn[:, :, 1], weight_sum[:, 0:1], z[:], ALU.mult, ALU.add).then_inc(z_made, 1)
            dve.wait_ge(hid_ps, 1)
            v.tensor_scalar(hid[:], ps_hid[:], 0.0, None, ALU.max).then_inc(hid_sb, 1)
            dve.wait_ge(gate_sb, 1)
            flat = gate[:].rearrange("p b k -> p (b k)")
            then(v.tensor_tensor(keep[:], flat, gn[:, :, 0], ALU.mult))
            then(v.tensor_scalar(keep[:], keep[:], 1.0, None, ALU.add))
            then(v.tensor_tensor(rest[:], flat, gn[:, :, 1], ALU.mult))
            then(v.tensor_tensor(next_stats[:, :, 0], keep[:], chan_stats[:, :, 0], ALU.mult))
            then(v.tensor_tensor(next_stats[:, :, 0], next_stats[:, :, 0], rest[:], ALU.add))
            then(v.tensor_tensor(next_stats[:, :, 1], keep[:], chan_stats[:, :, 1], ALU.mult))
            then(v.tensor_tensor(next_stats[:, :, 1], next_stats[:, :, 1], keep[:], ALU.mult))

        @block.tensor
        def _(pe):
            pe.wait_ge(landed, 64)
            pe.wait_ge(z_made, 1)
            for ct in range(CT):
                last = pe.matmul(ps_hid[:], fc1[:, ct], z[:, ct:UNITS:CT], start=ct == 0, stop=ct == CT - 1)
            last.then_inc(hid_ps, 1)
            pe.wait_ge(hid_sb, 1)
            for ct in range(CT):
                last = pe.matmul(ps_gate[:, ct], fc2[:, ct * P:(ct + 1) * P], hid[:], start=True, stop=True)
            last.then_inc(gate_ps, 1)

        @block.scalar
        def _(act):
            act.wait_ge(gate_ps, 1)
            nc.scalar.activation(gate[:].rearrange("p b k -> p k b"), ps_gate[:], ACT.Sigmoid).then_inc(gate_sb, 1)


def last_coefficients(nc, gmean, grstd, keep, rest, coef):
    with ExitStack() as ctx:
        off = ctx.enter_context(nc.sbuf_tensor("last_off", [P, UNITS], F32))
        steps = Steps(ctx, nc, "last_steps")
        block = ctx.enter_context(nc.Block())

        @block.vector
        def _(dve):
            v = nc.vector
            steps.then(dve, v.tensor_tensor(coef[:, :, 0], grstd[:], keep[:], ALU.mult))
            steps.then(dve, v.tensor_tensor(off[:], rest[:], gmean[:], ALU.subtract))
            steps.then(dve, v.scalar_tensor_tensor(coef[:, :, 1], off[:], 64.0, grstd[:], ALU.mult, ALU.mult))
            steps.then(dve, v.tensor_copy(coef[:, :, 2], keep[:]))
            steps.then(dve, v.tensor_scalar(coef[:, :, 3], rest[:], 64.0, None, ALU.mult))


def load_constants(nc, group_mean, d):
    with ExitStack() as ctx:
        landed = ctx.enter_context(semaphore(nc, "const_landed"))
        block = ctx.enter_context(nc.Block())

        @block.sync
        def _(sp):
            sp.dma_start(group_mean[:], d["group_mean"]).then_inc(landed, 16)
            sp.wait_ge(landed, 16)


class Projections:

    def __init__(self, ctx, nc):
        def sb(n, shape):
            return ctx.enter_context(nc.sbuf_tensor(f"proj_{n}_sb", shape, F32))

        self.w = sb("w", [P, 3, CT, C])
        self.wo = sb("wo", [P, CT, C])
        self.lrw = sb("lrw", [P, CT, NH + 1])
        self.gain = sb("gain", [P, C])
        self.shift = sb("shift", [P, C])
        self.wbias = sb("wbias", [P, 3, C])
        self.lrb = sb("lrb", [P, NH])
        self.wo_bias = sb("wo_bias", [P, CT])
        self.mean_col = sb("mean_col", [P, 1])
        self.ident = sb("ident", [P, P])


def network(nc, d, out):
    def dram(n, shape):
        return nc.dram_tensor(n, shape, F32, kind="Internal").ap()

    rec = dram("records", (B, TOK + 2 * CS, NH, RW))
    q = dram("queries", (B, TOK, C))
    grad = dram("gradients", (B, TOK, NH, HD))
    w_snap = dram("w_snapshots", (TOK // P, B, P, NH // 2, HD))
    b_snap = dram("b_snapshots", (TOK // P, B, NH, HD))
    x1 = dram("x1", (B, C, H, W))
    x2 = dram("x2", (B, C, H, W))
    with ExitStack() as ctx:
        def sb(n, shape):
            return ctx.enter_context(nc.sbuf_tensor(n, shape, F32))

        chan_stats = sb("chan_stats", [P, UNITS, 2])
        gn = sb("gn", [P, UNITS, 2])
        gmean = sb("gmean", [P, UNITS])
        grstd = sb("grstd", [P, UNITS])
        group_mean = sb("group_mean_sb", [P, P])
        coef = sb("coef", [P, UNITS, 4])
        load_constants(nc, group_mean, d)
        with ExitStack() as layer0:
            T = Projections(layer0, nc)
            channel_statistics(nc, "stats0", d["x"], chan_stats)
            group_norm(nc, "norm0", chan_stats, group_mean, 1e-5, gmean, grstd)
            norm_factors(nc, "factors0", gmean, grstd, gn, None)
            prepare_projections(nc, T, d)
            project(nc, T, d["x"], d["rope"], gn, rec, q)
            scan_chunks(nc, T, d, rec, grad, w_snap, b_snap)
            read_out(nc, T, d, d["x"], rec, q, grad, w_snap, b_snap, x1, chan_stats)
        block_sums = sb("block_sums", [P, UNITS, 16])
        keep = sb("keep", [P, UNITS])
        rest = sb("rest", [P, UNITS])
        next_stats = sb("next_stats", [P, UNITS, 2])
        group_norm(nc, "norm1", chan_stats, group_mean, 1e-5, gmean, grstd)
        norm_factors(nc, "factors1", gmean, grstd, gn, coef)
        fourier_layer(nc, "fourier1", x1, x2, d["f1_w"], d["f1_b"], d["dft"], coef, chan_stats, block_sums)
        group_norm(nc, "norm2", chan_stats, group_mean, 1e-5, gmean, grstd)
        norm_factors(nc, "factors2", gmean, grstd, gn, None)
        gate_channels(nc, d, chan_stats, block_sums, gn, keep, rest, next_stats)
        group_norm(nc, "norm3", next_stats, group_mean, 1e-5, gmean, grstd)
        last_coefficients(nc, gmean, grstd, keep, rest, coef)
        fourier_layer(nc, "fourier3", x2, out, d["f3_w"], d["f3_b"], d["dft"], coef, None, None)


def rope_table():
    inv = (1.0 / 10000.0 ** (np.arange(0, HD, 2, dtype=np.float32) / np.float32(HD))).astype(np.float32)
    angle = np.arange(TOK, dtype=np.float32)[:, None] * inv[None]
    return np.concatenate([np.cos(angle), -np.sin(angle), np.sin(angle)], 1).astype(np.float32)


def shape_constants():
    j = np.arange(P)
    chunk = j // CS
    same = (chunk[:, None] == chunk[None]) & (j[:, None] <= j[None])
    earlier = chunk[:, None] < chunk[None]
    ind = np.kron(np.eye(NH), np.ones((1, CS)))
    constants = {
        "dft": dft_matrices(),
        "rope": rope_table(),
        "group_mean": np.kron(np.eye(P // 16), np.full((16, 16), 1 / 16)),
        "masks": np.stack([same, earlier], 1),
        "place": np.tile(np.repeat(np.eye(2), CS, 0), (NH // 2, 1)),
        "pairs": np.repeat(np.eye(NH // 2), 2 * CS, 0),
        "ind": ind,
        "ind_t": ind.T,
        "tok_inv": np.tile(1.0 / np.arange(1, CS + 1, dtype=np.float32), NH),
        "eps": np.tile(np.array([[HD * 1e-6, 1e-6]]), (P, 1)),
    }
    return {n: a.astype(np.float32) for n, a in constants.items()}


def layout(i):
    def rows_of(w):
        return w.T.reshape(CT, P, w.shape[0]).transpose(1, 0, 2)

    def columns(v):
        return v.reshape(CT, P).T

    def fourier(n):
        w1, w2, b1, b2 = (i[f"{n}_conv_{k}"] for k in ("w1", "w2", "b1", "b2"))
        return (np.stack([w1[0], w1[1], w2[0], w2[1]], axis=2), np.stack([b1[0], b1[1], b2[0], b2[1]], axis=2))

    L0 = {k[8:]: i[k] for k in i if k.startswith("L0_conv_")}
    d = shape_constants()
    d["x"] = i["x"]
    d["wT"] = np.stack([rows_of(L0[n]) for n in ("q_w", "k_w", "v_w", "o_w")])
    d["lr_wT"] = rows_of(L0["lr_w"].reshape(NH, C))
    d["vecs"] = np.stack([columns(L0[n]) for n in ("ln_w", "ln_b", "post_w", "post_b")], 1)
    d["ttt_rows"] = np.stack([L0["ttt_ln_w"].reshape(-1), L0["ttt_ln_b"].reshape(-1)])
    d["lr_b_row"] = L0["lr_b"].reshape(-1)
    d["tok_rows"] = np.stack([d.pop("tok_inv"), np.tile(L0["tok_idx_delta"], NH)])
    d["gain_rows"] = np.repeat(L0["ttt_ln_w"], CS, 0)
    d["w0"] = L0["W1"].reshape(NH // 2, 2, HD, HD).transpose(1, 2, 0, 3).reshape(P, NH // 2, HD)
    d["b0"] = L0["b1"].reshape(NH, HD)
    d["f1_w"], d["f1_b"] = fourier("L1")
    d["f3_w"], d["f3_b"] = fourier("L3")
    d["gate_w1"] = i["L2_conv_w1"].reshape(3, 9)
    d["gate_w2"] = i["L2_conv_w2"].reshape(9)
    d["fc1_wT"] = rows_of(i["L2_conv_fc1_w"])
    d["fc2_wT"] = i["L2_conv_fc2_w"].T
    return {n: np.ascontiguousarray(a) for n, a in d.items()}


def kernel(**inputs):
    import concourse.bacc as bacc
    from concourse.bass_utils import run_bass_kernel_spmd

    arrays = layout({n: np.asarray(a) for n, a in inputs.items()})
    nc = bacc.Bacc("TRN2", target_bir_lowering=False, num_devices=1)
    d = {n: nc.dram_tensor(n, a.shape, F32, kind="ExternalInput").ap() for n, a in arrays.items()}
    out = nc.dram_tensor("out", (B, C, H, W), F32, kind="ExternalOutput").ap()
    network(nc, d, out)
    r = run_bass_kernel_spmd(nc, [arrays], core_ids=[0])
    return r.results[0]["out"]
```
